# Optimizing a Trainium2 kernel written in Bass

```python
import numpy as np
import jax
import jax.numpy as jnp

def _softmax(x, axis=-1):
    return jax.nn.softmax(x, axis=axis)

def _gelu(x):
    return jax.nn.gelu(x, approximate=True)

def _silu(x):
    return jax.nn.silu(x)

def _sigmoid(x):
    return jax.nn.sigmoid(x)

def _layernorm(x, axis=-1, eps=1e-05):
    m = jnp.mean(x, axis=axis, keepdims=True)
    v = jnp.var(x, axis=axis, keepdims=True)
    return (x - m) / jnp.sqrt(v + eps)

def _scatter_add(tgt, idx, src, axis=0):
    return tgt.at[idx].add(src)

def _segment_sum(src, seg, n):
    return jax.ops.segment_sum(src, seg, n)
kernel_name = 'mk_gnn_ffn_d4_gnn_r16_3df3e4'

def setup_inputs(seed: int=0):
    np.random.seed(seed)
    _w = jnp.asarray

    def _rec_inputs():
        import jax
        import jax.numpy as jnp
        _gk = jax.random.key(seed)
        x = -0.0003713 + 1 * jax.random.normal(jax.random.fold_in(_gk, 1), (3125, 256), jnp.float32)
        _s = jax.random.randint(jax.random.fold_in(_gk, 2), (25000,), 0, 3125, jnp.int32)
        _d = jax.random.randint(jax.random.fold_in(_gk, 3), (25000,), 0, 3125, jnp.int32)
        _loop = jnp.arange(3125, dtype=jnp.int32)
        src = jnp.concatenate([_s, _d, _loop])
        dst = jnp.concatenate([_d, _s, _loop])
        _o = jnp.argsort(dst, stable=True)
        src = src[_o]
        dst = dst[_o]
        edge_attr_20 = jax.random.uniform(jax.random.fold_in(_gk, 11), (53125, 20), jnp.float32, 0.0, 1)
        edge_attr_256 = 9.41057e-06 + 1 * jax.random.normal(jax.random.fold_in(_gk, 12), (53125, 256), jnp.float32)
        return (x, src, dst, edge_attr_20, edge_attr_256)
    x, src, dst, edge_attr_20, edge_attr_256 = _rec_inputs()

    def _L0_gnn_setup():
        import jax, jax.numpy as jnp
        import numpy as np
        N, IN_CH, HEADS, OUT_CH, E = (3125, 256, 4, 64, 50000)
        key = jax.random.key(seed)
        k1, k2, k3, k4, k5 = jax.random.split(key, 5)
        x = jax.random.normal(k1, (N, IN_CH), dtype=jnp.float32)
        edge_index = jax.random.randint(k2, (2, E), 0, N, dtype=jnp.int64)
        bw = float(np.sqrt(6.0 / (IN_CH + HEADS * OUT_CH)))
        ba = float(np.sqrt(6.0 / (HEADS + OUT_CH)))
        weight = jax.random.uniform(k3, (IN_CH, HEADS * OUT_CH), jnp.float32, -bw, bw)
        attn_l = jax.random.uniform(k4, (HEADS, OUT_CH), jnp.float32, -ba, ba)
        attn_r = jax.random.uniform(k5, (HEADS, OUT_CH), jnp.float32, -ba, ba)
        return {'x': x, 'edge_index': edge_index, 'weight': weight, 'attn_l': attn_l, 'attn_r': attn_r}
    _L0_gnn_all = _L0_gnn_setup()
    _L0_gnn_in = {k: v for k, v in _L0_gnn_all.items() if k in ('weight', 'attn_l', 'attn_r')}
    del _L0_gnn_all

    def _L0_ffn_setup():
        import jax, jax.numpy as jnp
        import numpy as np
        B, S, D = (8, 256, 256)
        H = 4 * D
        CAPACITY = 0.5
        key = jax.random.key(seed)
        ks = jax.random.split(key, 6)
        x = jax.random.normal(ks[0], (B, S, D), dtype=jnp.float32)
        attention_mask = jnp.zeros((B, 1, 1, S), dtype=jnp.float32)
        wr = jax.random.normal(ks[1], (D, 1), dtype=jnp.float32) * 0.02
        br = jnp.zeros((1,), dtype=jnp.float32)
        w1 = jax.random.normal(ks[2], (D, H), dtype=jnp.float32) * 0.02
        b1 = jnp.zeros((H,), dtype=jnp.float32)
        w2 = jax.random.normal(ks[3], (H, D), dtype=jnp.float32) * 0.02
        b2 = jnp.zeros((D,), dtype=jnp.float32)
        return {'x': x, 'attention_mask': attention_mask, 'wr': wr, 'br': br, 'w1': w1, 'b1': b1, 'w2': w2, 'b2': b2}
    _L0_ffn_all = _L0_ffn_setup()
    _L0_ffn_in = {k: v for k, v in _L0_ffn_all.items() if k in ('attention_mask', 'wr', 'br', 'w1', 'b1', 'w2', 'b2')}
    del _L0_ffn_all

    def _L1_gnn_setup():
        import jax, jax.numpy as jnp
        import numpy as np
        N, E, NIN, H, C = (3125, 50000, 256, 8, 32)
        HC = H * C
        key = jax.random.key(seed)
        ks = jax.random.split(key, 12)
        s = 0.05
        x = jax.random.normal(ks[0], (N, NIN), dtype=jnp.float32)
        edge_index = jax.random.randint(ks[1], (2, E), 0, N, dtype=jnp.int64)
        edge_attr = jax.random.normal(ks[2], (E, NIN), dtype=jnp.float32)
        Wq = jax.random.normal(ks[3], (NIN, HC), dtype=jnp.float32) * s
        bq = jax.random.normal(ks[4], (HC,), dtype=jnp.float32) * s
        Wk = jax.random.normal(ks[5], (NIN, HC), dtype=jnp.float32) * s
        bk = jax.random.normal(ks[6], (HC,), dtype=jnp.float32) * s
        Wv = jax.random.normal(ks[7], (NIN, HC), dtype=jnp.float32) * s
        bv = jax.random.normal(ks[8], (HC,), dtype=jnp.float32) * s
        We = jax.random.normal(ks[9], (NIN, HC), dtype=jnp.float32) * s
        Ws = jax.random.normal(ks[10], (NIN, HC), dtype=jnp.float32) * s
        bs = jax.random.normal(ks[11], (HC,), dtype=jnp.float32) * s
        return {'x': x, 'edge_index': edge_index, 'edge_attr': edge_attr, 'Wq': Wq, 'bq': bq, 'Wk': Wk, 'bk': bk, 'Wv': Wv, 'bv': bv, 'We': We, 'Ws': Ws, 'bs': bs}
    _L1_gnn_all = _L1_gnn_setup()
    _L1_gnn_in = {k: v for k, v in _L1_gnn_all.items() if k in ('Wq', 'bq', 'Wk', 'bk', 'Wv', 'bv', 'We', 'Ws', 'bs')}
    del _L1_gnn_all

    def _L1_ffn_setup():
        import jax, jax.numpy as jnp
        import numpy as np
        B, K, D = (512, 16, 256)
        E = 32
        H = int(D * 0.25)
        key = jax.random.key(seed)
        ks = jax.random.split(key, 7)
        d_rs = D ** (-0.5)
        h_rs = H ** (-0.5)
        x = jax.random.normal(ks[0], (B, K, D), dtype=jnp.float32)
        router_w = jax.random.uniform(ks[1], (E, D), jnp.float32, -d_rs, d_rs)
        router_b = jax.random.uniform(ks[2], (E,), jnp.float32, -d_rs, d_rs)
        W1 = jax.random.uniform(ks[3], (E, D, H), jnp.float32, -h_rs, h_rs)
        b1 = jax.random.uniform(ks[4], (E, H), jnp.float32, -h_rs, h_rs)
        W2 = jax.random.uniform(ks[5], (E, H, D), jnp.float32, -d_rs, d_rs)
        b2 = jax.random.uniform(ks[6], (E, D), jnp.float32, -d_rs, d_rs)
        return {'x': x, 'router_w': router_w, 'router_b': router_b, 'W1': W1, 'b1': b1, 'W2': W2, 'b2': b2}
    _L1_ffn_all = _L1_ffn_setup()
    _L1_ffn_in = {k: v for k, v in _L1_ffn_all.items() if k in ('router_w', 'router_b', 'W1', 'b1', 'W2', 'b2')}
    del _L1_ffn_all

    def _L2_gnn_setup():
        import jax, jax.numpy as jnp
        import numpy as np
        N, E, HDIM, NG = (625, 20000, 256, 20)
        BN_EPS = 1e-05
        key = jax.random.key(seed)
        ks = jax.random.split(key, 12)
        inp = {'x': jax.random.normal(ks[0], (N, HDIM), dtype=jnp.float32), 'rbf': jax.random.uniform(ks[1], (E, NG), dtype=jnp.float32), 'ei': jax.random.randint(ks[2], (2, E), 0, N, dtype=jnp.int64), 'Wf1': jax.random.normal(ks[3], (NG, HDIM), dtype=jnp.float32) / np.sqrt(NG), 'bf1': jnp.zeros((HDIM,), dtype=jnp.float32), 'Wf2': jax.random.normal(ks[4], (HDIM, HDIM), dtype=jnp.float32) / np.sqrt(HDIM), 'bf2': jnp.zeros((HDIM,), dtype=jnp.float32), 'Wu1': jax.random.normal(ks[5], (HDIM, HDIM), dtype=jnp.float32) / np.sqrt(HDIM), 'bu1': jnp.zeros((HDIM,), dtype=jnp.float32), 'Wu2': jax.random.normal(ks[6], (HDIM, HDIM), dtype=jnp.float32) / np.sqrt(HDIM), 'bu2': jnp.zeros((HDIM,), dtype=jnp.float32), 'gamma': jnp.ones((HDIM,), dtype=jnp.float32), 'beta': jnp.zeros((HDIM,), dtype=jnp.float32)}
        return inp
    _L2_gnn_all = _L2_gnn_setup()
    _L2_gnn_in = {k: v for k, v in _L2_gnn_all.items() if k in ('Wf1', 'bf1', 'Wf2', 'bf2', 'Wu1', 'bu1', 'Wu2', 'bu2', 'gamma', 'beta')}
    del _L2_gnn_all

    def _L2_ffn_setup():
        import jax, jax.numpy as jnp
        import numpy as np
        BN_EPS = 0.001

        def _bn(h, g, b, m, v):
            return g * (h - m) * jax.lax.rsqrt(v + BN_EPS) + b
        key = jax.random.key(seed)
        ks = jax.random.split(key, 8)
        B, F, Df = (256, 64, 256)
        E, H, D = (8, 256, 256)
        s1 = 1.0 / np.sqrt(Df)
        s2 = 1.0 / np.sqrt(H)
        return {'x': jax.random.normal(ks[0], (B, F, Df), jnp.float32), 'Wr': jax.random.normal(ks[1], (Df, E), jnp.float32) * s1, 'br': jnp.zeros((E,), jnp.float32), 'W1': jax.random.normal(ks[2], (E, Df, H), jnp.float32) * s1, 'b1': jnp.zeros((E, H), jnp.float32), 'g1': jnp.ones((E, H), jnp.float32), 'be1': jnp.zeros((E, H), jnp.float32), 'm1': jnp.zeros((E, H), jnp.float32), 'v1': jnp.ones((E, H), jnp.float32), 'W2': jax.random.normal(ks[3], (E, H, H), jnp.float32) * s2, 'b2': jnp.zeros((E, H), jnp.float32), 'g2': jnp.ones((E, H), jnp.float32), 'be2': jnp.zeros((E, H), jnp.float32), 'm2': jnp.zeros((E, H), jnp.float32), 'v2': jnp.ones((E, H), jnp.float32), 'Wo': jax.random.normal(ks[4], (E, H, D), jnp.float32) * s2, 'bo': jnp.zeros((E, D), jnp.float32)}
    _L2_ffn_all = _L2_ffn_setup()
    _L2_ffn_in = {k: v for k, v in _L2_ffn_all.items() if k in ('Wr', 'br', 'W1', 'b1', 'g1', 'be1', 'm1', 'v1', 'W2', 'b2', 'g2', 'be2', 'm2', 'v2', 'Wo', 'bo')}
    del _L2_ffn_all

    def _L3_gnn_setup():
        import jax, jax.numpy as jnp
        import numpy as np
        N_NODES = 6250
        N_EDGES = 100000
        D_IN = 256
        HEADS = 8
        D_HEAD = 32
        NEG_SLOPE = 0.2
        BN_EPS = 1e-05
        key = jax.random.key(seed)
        ks = jax.random.split(key, 8)
        x = jax.random.normal(ks[0], (N_NODES, D_IN), dtype=jnp.float32)
        edge_index = jax.random.randint(ks[1], (2, N_EDGES), 0, N_NODES, dtype=jnp.int32)
        W = jax.random.normal(ks[2], (D_IN, HEADS * D_HEAD), dtype=jnp.float32) / np.sqrt(D_IN)
        att_src = jax.random.normal(ks[3], (HEADS, D_HEAD), dtype=jnp.float32) / np.sqrt(D_HEAD)
        att_dst = jax.random.normal(ks[4], (HEADS, D_HEAD), dtype=jnp.float32) / np.sqrt(D_HEAD)
        bias = jax.random.normal(ks[5], (HEADS * D_HEAD,), dtype=jnp.float32) * 0.01
        gamma = jnp.ones((HEADS * D_HEAD,), dtype=jnp.float32)
        beta = jnp.zeros((HEADS * D_HEAD,), dtype=jnp.float32)
        return {'x': x, 'edge_index': edge_index, 'W': W, 'att_src': att_src, 'att_dst': att_dst, 'bias': bias, 'gamma': gamma, 'beta': beta}
    _L3_gnn_all = _L3_gnn_setup()
    _L3_gnn_in = {k: v for k, v in _L3_gnn_all.items() if k in ('W', 'att_src', 'att_dst', 'bias', 'gamma', 'beta')}
    del _L3_gnn_all

    def _L3_ffn_setup():
        import jax, jax.numpy as jnp
        import numpy as np
        B, A = (256, 8)
        IN, OUT = (256, 256)
        SH1, SH2 = (256, 128)
        EH1, EH2 = (128, 64)
        E, TOPK = (4, 2)

        def _shared_mlp(x, W1, b1, W2, b2, W3, b3):
            h = jax.nn.relu(x @ W1 + b1)
            h = jax.nn.relu(h @ W2 + b2)
            return h @ W3 + b3

        def _experts_mlp(x, eW1, eb1, eW2, eb2, eW3, eb3):
            h = jax.nn.relu(jnp.einsum('baf,efh->ebah', x, eW1) + eb1[:, None, None, :])
            h = jax.nn.relu(jnp.einsum('ebah,ehg->ebag', h, eW2) + eb2[:, None, None, :])
            o = jnp.einsum('ebag,ego->ebao', h, eW3) + eb3[:, None, None, :]
            return jnp.moveaxis(o, 0, -1)
        key = jax.random.key(seed)
        ks = jax.random.split(key, 16)
        s = 0.05
        return {'x': jax.random.normal(ks[0], (B, A, IN), jnp.float32), 'sW1': jax.random.normal(ks[1], (IN, SH1), jnp.float32) * s, 'sb1': jnp.zeros((SH1,), jnp.float32), 'sW2': jax.random.normal(ks[2], (SH1, SH2), jnp.float32) * s, 'sb2': jnp.zeros((SH2,), jnp.float32), 'sW3': jax.random.normal(ks[3], (SH2, OUT), jnp.float32) * s, 'sb3': jnp.zeros((OUT,), jnp.float32), 'eW1': jax.random.normal(ks[4], (E, IN, EH1), jnp.float32) * s, 'eb1': jnp.zeros((E, EH1), jnp.float32), 'eW2': jax.random.normal(ks[5], (E, EH1, EH2), jnp.float32) * s, 'eb2': jnp.zeros((E, EH2), jnp.float32), 'eW3': jax.random.normal(ks[6], (E, EH2, OUT), jnp.float32) * s, 'eb3': jnp.zeros((E, OUT), jnp.float32), 'gW': jax.random.normal(ks[7], (IN, E), jnp.float32) * s, 'gb': jnp.zeros((E,), jnp.float32)}
    _L3_ffn_all = _L3_ffn_setup()
    _L3_ffn_in = {k: v for k, v in _L3_ffn_all.items() if k in ('sW1', 'sb1', 'sW2', 'sb2', 'sW3', 'sb3', 'eW1', 'eb1', 'eW2', 'eb2', 'eW3', 'eb3', 'gW', 'gb')}
    del _L3_ffn_all
    return {'x': x, 'src': src, 'dst': dst, 'edge_attr_20': edge_attr_20, 'edge_attr_256': edge_attr_256, 'L0_gnn_weight': _L0_gnn_in['weight'], 'L0_gnn_attn_l': _L0_gnn_in['attn_l'], 'L0_gnn_attn_r': _L0_gnn_in['attn_r'], 'L0_ffn_attention_mask': _L0_ffn_in['attention_mask'], 'L0_ffn_wr': _L0_ffn_in['wr'], 'L0_ffn_br': _L0_ffn_in['br'], 'L0_ffn_w1': _L0_ffn_in['w1'], 'L0_ffn_b1': _L0_ffn_in['b1'], 'L0_ffn_w2': _L0_ffn_in['w2'], 'L0_ffn_b2': _L0_ffn_in['b2'], 'L1_gnn_Wq': _L1_gnn_in['Wq'], 'L1_gnn_bq': _L1_gnn_in['bq'], 'L1_gnn_Wk': _L1_gnn_in['Wk'], 'L1_gnn_bk': _L1_gnn_in['bk'], 'L1_gnn_Wv': _L1_gnn_in['Wv'], 'L1_gnn_bv': _L1_gnn_in['bv'], 'L1_gnn_We': _L1_gnn_in['We'], 'L1_gnn_Ws': _L1_gnn_in['Ws'], 'L1_gnn_bs': _L1_gnn_in['bs'], 'L1_ffn_router_w': _L1_ffn_in['router_w'], 'L1_ffn_router_b': _L1_ffn_in['router_b'], 'L1_ffn_W1': _L1_ffn_in['W1'], 'L1_ffn_b1': _L1_ffn_in['b1'], 'L1_ffn_W2': _L1_ffn_in['W2'], 'L1_ffn_b2': _L1_ffn_in['b2'], 'L2_gnn_Wf1': _L2_gnn_in['Wf1'], 'L2_gnn_bf1': _L2_gnn_in['bf1'], 'L2_gnn_Wf2': _L2_gnn_in['Wf2'], 'L2_gnn_bf2': _L2_gnn_in['bf2'], 'L2_gnn_Wu1': _L2_gnn_in['Wu1'], 'L2_gnn_bu1': _L2_gnn_in['bu1'], 'L2_gnn_Wu2': _L2_gnn_in['Wu2'], 'L2_gnn_bu2': _L2_gnn_in['bu2'], 'L2_gnn_gamma': _L2_gnn_in['gamma'], 'L2_gnn_beta': _L2_gnn_in['beta'], 'L2_ffn_Wr': _L2_ffn_in['Wr'], 'L2_ffn_br': _L2_ffn_in['br'], 'L2_ffn_W1': _L2_ffn_in['W1'], 'L2_ffn_b1': _L2_ffn_in['b1'], 'L2_ffn_g1': _L2_ffn_in['g1'], 'L2_ffn_be1': _L2_ffn_in['be1'], 'L2_ffn_m1': _L2_ffn_in['m1'], 'L2_ffn_v1': _L2_ffn_in['v1'], 'L2_ffn_W2': _L2_ffn_in['W2'], 'L2_ffn_b2': _L2_ffn_in['b2'], 'L2_ffn_g2': _L2_ffn_in['g2'], 'L2_ffn_be2': _L2_ffn_in['be2'], 'L2_ffn_m2': _L2_ffn_in['m2'], 'L2_ffn_v2': _L2_ffn_in['v2'], 'L2_ffn_Wo': _L2_ffn_in['Wo'], 'L2_ffn_bo': _L2_ffn_in['bo'], 'L3_gnn_W': _L3_gnn_in['W'], 'L3_gnn_att_src': _L3_gnn_in['att_src'], 'L3_gnn_att_dst': _L3_gnn_in['att_dst'], 'L3_gnn_bias': _L3_gnn_in['bias'], 'L3_gnn_gamma': _L3_gnn_in['gamma'], 'L3_gnn_beta': _L3_gnn_in['beta'], 'L3_ffn_sW1': _L3_ffn_in['sW1'], 'L3_ffn_sb1': _L3_ffn_in['sb1'], 'L3_ffn_sW2': _L3_ffn_in['sW2'], 'L3_ffn_sb2': _L3_ffn_in['sb2'], 'L3_ffn_sW3': _L3_ffn_in['sW3'], 'L3_ffn_sb3': _L3_ffn_in['sb3'], 'L3_ffn_eW1': _L3_ffn_in['eW1'], 'L3_ffn_eb1': _L3_ffn_in['eb1'], 'L3_ffn_eW2': _L3_ffn_in['eW2'], 'L3_ffn_eb2': _L3_ffn_in['eb2'], 'L3_ffn_eW3': _L3_ffn_in['eW3'], 'L3_ffn_eb3': _L3_ffn_in['eb3'], 'L3_ffn_gW': _L3_ffn_in['gW'], 'L3_ffn_gb': _L3_ffn_in['gb']}

def reference(x, src, dst, edge_attr_20, edge_attr_256, L0_gnn_weight, L0_gnn_attn_l, L0_gnn_attn_r, L0_ffn_attention_mask, L0_ffn_wr, L0_ffn_br, L0_ffn_w1, L0_ffn_b1, L0_ffn_w2, L0_ffn_b2, L1_gnn_Wq, L1_gnn_bq, L1_gnn_Wk, L1_gnn_bk, L1_gnn_Wv, L1_gnn_bv, L1_gnn_We, L1_gnn_Ws, L1_gnn_bs, L1_ffn_router_w, L1_ffn_router_b, L1_ffn_W1, L1_ffn_b1, L1_ffn_W2, L1_ffn_b2, L2_gnn_Wf1, L2_gnn_bf1, L2_gnn_Wf2, L2_gnn_bf2, L2_gnn_Wu1, L2_gnn_bu1, L2_gnn_Wu2, L2_gnn_bu2, L2_gnn_gamma, L2_gnn_beta, L2_ffn_Wr, L2_ffn_br, L2_ffn_W1, L2_ffn_b1, L2_ffn_g1, L2_ffn_be1, L2_ffn_m1, L2_ffn_v1, L2_ffn_W2, L2_ffn_b2, L2_ffn_g2, L2_ffn_be2, L2_ffn_m2, L2_ffn_v2, L2_ffn_Wo, L2_ffn_bo, L3_gnn_W, L3_gnn_att_src, L3_gnn_att_dst, L3_gnn_bias, L3_gnn_gamma, L3_gnn_beta, L3_ffn_sW1, L3_ffn_sb1, L3_ffn_sW2, L3_ffn_sb2, L3_ffn_sW3, L3_ffn_sb3, L3_ffn_eW1, L3_ffn_eb1, L3_ffn_eW2, L3_ffn_eb2, L3_ffn_eW3, L3_ffn_eb3, L3_ffn_gW, L3_ffn_gb):
    import jax
    import jax.numpy as jnp

    def _L0_gnn_ref(x, edge_index, weight, attn_l, attn_r):
        import jax, jax.numpy as jnp
        import numpy as np
        N, IN_CH, HEADS, OUT_CH, E = (3125, 256, 4, 64, 50000)
        heads, out_ch = attn_l.shape
        n = x.shape[0]
        xt = jnp.matmul(x, weight).reshape(-1, heads, out_ch)
        row, col = (edge_index[0], edge_index[1])
        alpha_l = jnp.einsum('ehd,hd->eh', xt[row], attn_l)
        alpha_r = jnp.einsum('ehd,hd->eh', xt[col], attn_r)
        alpha = jax.nn.softmax(jax.nn.leaky_relu(alpha_l + alpha_r, 0.01), axis=1)
        tmp = jnp.einsum('nh,nhd->nd', alpha[:n], xt[col[:n]])
        out = jnp.broadcast_to(tmp[:, None, :], (n, heads, out_ch))
        return out.reshape(n, heads * out_ch)

    def _L0_ffn_ref(x, attention_mask, wr, br, w1, b1, w2, b2):
        import jax, jax.numpy as jnp
        import numpy as np
        B, S, D = (8, 256, 256)
        H = 4 * D
        CAPACITY = 0.5
        b, s, d = x.shape
        weights = (jnp.einsum('bsd,do->bso', x, wr) + br)[..., 0]
        k = max(1, int(CAPACITY * s))
        kk = k - 1 if k > 1 else 1
        _, idx = jax.lax.top_k(weights, k)
        sel_idx = idx[:, :kk]
        sel = jnp.take_along_axis(x, sel_idx[:, :, None], axis=1)
        h = jax.nn.gelu(jnp.einsum('bkd,dh->bkh', sel, w1) + b1)
        y = jnp.einsum('bkh,hd->bkd', h, w2) + b2
        w_sel = jnp.take_along_axis(weights, sel_idx, axis=1)
        y = y * w_sel[..., None]
        batch_idx = jnp.arange(b)[:, None]
        processed = jnp.zeros_like(x).at[batch_idx, sel_idx].set(y)
        return processed + x

    def _L1_gnn_ref(x, edge_index, edge_attr, Wq, bq, Wk, bk, Wv, bv, We, Ws, bs):
        import jax, jax.numpy as jnp
        import numpy as np
        N, E, NIN, H, C = (3125, 50000, 256, 8, 32)
        HC = H * C
        src, dst = (edge_index[0], edge_index[1])
        n = x.shape[0]
        q = (x @ Wq + bq).reshape(n, H, C)
        k = (x @ Wk + bk).reshape(n, H, C)
        v = (x @ Wv + bv).reshape(n, H, C)
        e = (edge_attr @ We).reshape(-1, H, C)
        k_j = k[src] + e
        v_j = v[src] + e
        q_i = q[dst]
        alpha = jnp.sum(q_i * k_j, axis=-1) / jnp.sqrt(jnp.float32(C))
        amax = jax.ops.segment_max(alpha, dst, num_segments=n)
        ex = jnp.exp(alpha - amax[dst])
        denom = jax.ops.segment_sum(ex, dst, num_segments=n)
        alpha = ex / denom[dst]
        out = jax.ops.segment_sum(v_j * alpha[:, :, None], dst, num_segments=n)
        out = out.reshape(n, HC)
        out = out + x @ Ws + bs
        return out

    def _L1_ffn_ref(x, router_w, router_b, W1, b1, W2, b2):
        import jax, jax.numpy as jnp
        import numpy as np
        B, K, D = (512, 16, 256)
        E = 32
        H = int(D * 0.25)
        xf = x.reshape(-1, D)
        logits = xf @ router_w.T + router_b
        idx = jnp.argmax(logits, axis=-1)
        w1t = jnp.take(W1, idx, axis=0)
        h = jnp.einsum('nd,ndh->nh', xf, w1t) + jnp.take(b1, idx, axis=0)
        h = jax.nn.relu(h)
        w2t = jnp.take(W2, idx, axis=0)
        out = jnp.einsum('nh,nhd->nd', h, w2t) + jnp.take(b2, idx, axis=0)
        out = jax.nn.relu(out)
        return out.reshape(x.shape)

    def _L2_gnn_ref(x, rbf, Wf1, bf1, Wf2, bf2, Wu1, bu1, Wu2, bu2, gamma, beta, ei):
        import jax, jax.numpy as jnp
        import numpy as np
        N, E, HDIM, NG = (625, 20000, 256, 20)
        BN_EPS = 1e-05
        row, col = (ei[0], ei[1])
        filt = jax.nn.silu(rbf @ Wf1 + bf1) @ Wf2 + bf2
        msg = x[col] * filt
        agg = jax.ops.segment_sum(msg, row, num_segments=x.shape[0])
        h = jax.nn.silu(agg @ Wu1 + bu1) @ Wu2 + bu2
        mean = jnp.mean(h, axis=0)
        var = jnp.mean(jnp.square(h - mean), axis=0)
        bn = gamma * (h - mean) * jax.lax.rsqrt(var + BN_EPS) + beta
        return x + bn

    def _L2_ffn_ref(x, Wr, br, W1, b1, g1, be1, m1, v1, W2, b2, g2, be2, m2, v2, Wo, bo):
        import jax, jax.numpy as jnp
        import numpy as np
        BN_EPS = 0.001

        def _bn(h, g, b, m, v):
            return g * (h - m) * jax.lax.rsqrt(v + BN_EPS) + b
        feat = jnp.mean(x, axis=0)
        w = jax.nn.softmax(feat @ Wr + br, axis=-1)
        h = jnp.einsum('bfd,edh->bfeh', x, W1) + b1
        h = jax.nn.relu(_bn(h, g1, be1, m1, v1))
        h = jnp.einsum('bfeh,ehk->bfek', h, W2) + b2
        h = jax.nn.relu(_bn(h, g2, be2, m2, v2))
        y = jnp.einsum('bfeh,ehd->bfed', h, Wo) + bo
        return jnp.einsum('bfed,fe->bfd', y, w)

    def _L3_gnn_ref(x, edge_index, W, att_src, att_dst, bias, gamma, beta):
        import jax, jax.numpy as jnp
        import numpy as np
        N_NODES = 6250
        N_EDGES = 100000
        D_IN = 256
        HEADS = 8
        D_HEAD = 32
        NEG_SLOPE = 0.2
        BN_EPS = 1e-05
        N = x.shape[0]
        H, D = att_src.shape
        xh = (x @ W).reshape(N, H, D)
        a_src = jnp.einsum('nhd,hd->nh', xh, att_src)
        a_dst = jnp.einsum('nhd,hd->nh', xh, att_dst)
        loops = jnp.arange(N, dtype=edge_index.dtype)
        src = jnp.concatenate([edge_index[0], loops])
        dst = jnp.concatenate([edge_index[1], loops])
        e = jax.nn.leaky_relu(a_src[src] + a_dst[dst], NEG_SLOPE)
        m = jax.ops.segment_max(e, dst, num_segments=N)
        e = jnp.exp(e - m[dst])
        denom = jax.ops.segment_sum(e, dst, num_segments=N)
        alpha = e / denom[dst]
        msg = xh[src] * alpha[:, :, None]
        out = jax.ops.segment_sum(msg, dst, num_segments=N).reshape(N, H * D) + bias
        mean = jnp.mean(out, axis=0)
        var = jnp.var(out, axis=0)
        out = (out - mean) * jax.lax.rsqrt(var + BN_EPS) * gamma + beta
        return out + x

    def _L3_ffn_ref(x, sW1, sb1, sW2, sb2, sW3, sb3, eW1, eb1, eW2, eb2, eW3, eb3, gW, gb):
        import jax, jax.numpy as jnp
        import numpy as np
        B, A = (256, 8)
        IN, OUT = (256, 256)
        SH1, SH2 = (256, 128)
        EH1, EH2 = (128, 64)
        E, TOPK = (4, 2)

        def _shared_mlp(x, W1, b1, W2, b2, W3, b3):
            h = jax.nn.relu(x @ W1 + b1)
            h = jax.nn.relu(h @ W2 + b2)
            return h @ W3 + b3

        def _experts_mlp(x, eW1, eb1, eW2, eb2, eW3, eb3):
            h = jax.nn.relu(jnp.einsum('baf,efh->ebah', x, eW1) + eb1[:, None, None, :])
            h = jax.nn.relu(jnp.einsum('ebah,ehg->ebag', h, eW2) + eb2[:, None, None, :])
            o = jnp.einsum('ebag,ego->ebao', h, eW3) + eb3[:, None, None, :]
            return jnp.moveaxis(o, 0, -1)
        all_out = _experts_mlp(x, eW1, eb1, eW2, eb2, eW3, eb3)
        shared = _shared_mlp(x, sW1, sb1, sW2, sb2, sW3, sb3)
        gates = jax.nn.softmax(x @ gW + gb, axis=-1)
        topv, topi = jax.lax.top_k(gates, TOPK)
        topw = jax.nn.softmax(topv, axis=-1)
        sel = jnp.take_along_axis(all_out, topi[:, :, None, :], axis=-1)
        gated = jnp.sum(sel * topw[:, :, None, :], axis=-1)
        return shared + gated
    edge_index = jnp.stack([src, dst])
    x = x + _L0_gnn_ref(_layernorm(x, axis=-1), edge_index, L0_gnn_weight, L0_gnn_attn_l, L0_gnn_attn_r)
    x = x + _L0_ffn_ref(_layernorm(x, axis=-1)[None], L0_ffn_attention_mask, L0_ffn_wr, L0_ffn_br, L0_ffn_w1, L0_ffn_b1, L0_ffn_w2, L0_ffn_b2)[0]
    x = x + _L1_gnn_ref(_layernorm(x, axis=-1), edge_index, edge_attr_256, L1_gnn_Wq, L1_gnn_bq, L1_gnn_Wk, L1_gnn_bk, L1_gnn_Wv, L1_gnn_bv, L1_gnn_We, L1_gnn_Ws, L1_gnn_bs)
    x = x + _L1_ffn_ref(_layernorm(x, axis=-1)[None], L1_ffn_router_w, L1_ffn_router_b, L1_ffn_W1, L1_ffn_b1, L1_ffn_W2, L1_ffn_b2)[0]
    x = x + _L2_gnn_ref(_layernorm(x, axis=-1), edge_attr_20, L2_gnn_Wf1, L2_gnn_bf1, L2_gnn_Wf2, L2_gnn_bf2, L2_gnn_Wu1, L2_gnn_bu1, L2_gnn_Wu2, L2_gnn_bu2, L2_gnn_gamma, L2_gnn_beta, edge_index)
    x = x + _L2_ffn_ref(_layernorm(x, axis=-1)[None], L2_ffn_Wr, L2_ffn_br, L2_ffn_W1, L2_ffn_b1, L2_ffn_g1, L2_ffn_be1, L2_ffn_m1, L2_ffn_v1, L2_ffn_W2, L2_ffn_b2, L2_ffn_g2, L2_ffn_be2, L2_ffn_m2, L2_ffn_v2, L2_ffn_Wo, L2_ffn_bo)[0]
    x = x + _L3_gnn_ref(_layernorm(x, axis=-1), edge_index, L3_gnn_W, L3_gnn_att_src, L3_gnn_att_dst, L3_gnn_bias, L3_gnn_gamma, L3_gnn_beta)
    x = x + _L3_ffn_ref(_layernorm(x, axis=-1)[None], L3_ffn_sW1, L3_ffn_sb1, L3_ffn_sW2, L3_ffn_sb2, L3_ffn_sW3, L3_ffn_sb3, L3_ffn_eW1, L3_ffn_eb1, L3_ffn_eW2, L3_ffn_eb2, L3_ffn_eW3, L3_ffn_eb3, L3_ffn_gW, L3_ffn_gb)[0]
    return x

_drawn_inputs = setup_inputs


def setup_inputs(seed=0):
    import zlib

    import numpy as np

    out = dict(_drawn_inputs(seed))
    spreads = {'L0_ffn_b1': (0.0, 0.8),
     'L0_ffn_b2': (0.0, 0.609),
     'L2_gnn_bf1': (0.0, 0.1),
     'L2_gnn_bf2': (0.0, 0.1),
     'L2_gnn_bu1': (0.0, 0.481),
     'L2_gnn_bu2': (0.0, 2.0),
     'L2_gnn_gamma': (1.0, 0.2),
     'L2_gnn_beta': (0.0, 0.271),
     'L2_ffn_br': (0.0, 0.8),
     'L2_ffn_b1': (0.0, 0.8),
     'L2_ffn_g1': (1.0, 0.6),
     'L2_ffn_be1': (0.0, 0.8),
     'L2_ffn_m1': (0.0, 0.8),
     'L2_ffn_v1': (1.0, 0.6),
     'L2_ffn_b2': (0.0, 0.777),
     'L2_ffn_g2': (1.0, 0.6),
     'L2_ffn_be2': (0.0, 0.8),
     'L2_ffn_m2': (0.0, 0.756),
     'L2_ffn_v2': (1.0, 0.6),
     'L2_ffn_bo': (0.0, 0.562),
     'L3_gnn_gamma': (1.0, 0.2),
     'L3_gnn_beta': (0.0, 0.372),
     'L3_ffn_sb1': (0.0, 2.0),
     'L3_ffn_sb2': (0.0, 2.0),
     'L3_ffn_sb3': (0.0, 0.388),
     'L3_ffn_eb1': (0.0, 0.8),
     'L3_ffn_eb2': (0.0, 0.8),
     'L3_ffn_eb3': (0.0, 0.528),
     'L3_ffn_gb': (0.0, 0.8)}
    factors = {'L0_ffn_wr': 3.631,
     'L0_ffn_w1': 4.253,
     'L0_ffn_w2': 3.761,
     'L1_gnn_bq': 5.325,
     'L1_gnn_bk': 64.0,
     'L1_ffn_router_b': 2.857,
     'L1_ffn_b1': 8.0,
     'L1_ffn_b2': 5.19,
     'L3_gnn_bias': 64.0,
     'L3_ffn_eW1': 5.893,
     'L3_ffn_eW2': 5.144,
     'L3_ffn_eW3': 4.127,
     'L3_ffn_gW': 3.87,
     'L3_ffn_sW1': 4.044,
     'L3_ffn_sW2': 2.688}
    for name, (base, spread) in spreads.items():
        noise = np.random.default_rng([zlib.crc32(name.encode()), seed]).standard_normal(out[name].shape)
        drawn = base * np.exp(spread * noise) if base else spread * noise
        out[name] = jnp.asarray(drawn.astype(out[name].dtype))
    for name, factor in factors.items():
        out[name] = (out[name] * factor).astype(out[name].dtype)
    return out
```

```python
from contextlib import ExitStack, contextmanager

import numpy as np

import concourse.bass as bass
from concourse import mybir

F32 = mybir.dt.float32
BF16 = mybir.dt.bfloat16
I32 = mybir.dt.int32
ACT = mybir.ActivationFunctionType
ALU = mybir.AluOpType
AX = mybir.AxisListType.X

P = 128
N = 3125
D = 256
KD = D // P
TILES = -(-N // P)
GROUP = 5
GROUPS = TILES // GROUP
NPAD = TILES * P
GTOK = GROUP * P
HALF = GTOK // 2
E = 53125
CT = 16
CHUNK = CT * P
CHUNKS = -(-E // CHUNK)
ETILES = CHUNKS * CT
EPAD = ETILES * P
QT = ETILES // 4
HEADS = 8
HD = D // HEADS
SEG = D + HEADS
ROW = SEG + HEADS + 1
BIG = 1e30
KEEP = (N + 1) // 2 - 2
assert GROUPS * GROUP == TILES and KEEP == int(0.5 * N) - 1 and QT <= P

CONST = {}
_at = 0
for _name, _w in (("ident", P), ("le", P), ("lt", P), ("before", P), ("ones", P), ("iota", P), ("iota25", TILES),
                  ("iota_p", 1), ("iota32", 32), ("valid", TILES), ("node", TILES)):
    CONST[_name] = (_at, _w)
    _at += _w
NCONST = _at


def constants():
    p = np.arange(P)[:, None]
    f = np.arange(P)[None, :]
    node = p + P * np.arange(TILES)[None, :]
    parts = [p == f, p <= f, p < f, f < p, np.ones((P, P)), f + 0 * p, np.arange(TILES)[None, :] + 0 * p,
             p, np.arange(32)[None, :] + 0 * p, node < N, node]
    return np.concatenate([np.asarray(x, np.float32) for x in parts], axis=1)


class Chain:

    def __init__(self, eng, sem):
        self.eng, self.sem, self.n, self.step = eng, sem, 0, None

    def add(self, ins):
        ins.then_inc(self.sem, 1)
        self.n += 1

    def settle(self):
        self.eng.wait_ge(self.sem, self.n if self.step is None else self.step + self.n)

    def link(self, ins):
        self.add(ins)
        self.settle()

    @contextmanager
    def loop(self, count, per):
        before = self.n
        with self.eng.Fori(0, count) as i:
            self.step, self.n = i * per + before, 0
            yield i
            assert self.n == per, (self.n, per)
        self.step, self.n = None, before + count * per


class Moved:

    def __init__(self, sem):
        self.sem, self.before, self.after = sem, 0, 0

    def begin(self, raised):
        self.before, self.after = self.after, self.after + raised
        return self

    def count(self, ins):
        ins.then_inc(self.sem, 16)

    def wait(self, eng, value):
        eng.wait_ge(self.sem, value + self.before)


class Core:

    def __init__(self, nc, ctx):
        self.nc = nc
        self.x = ctx.enter_context(nc.sbuf_tensor("x_sb", [P, TILES, D], F32))
        self.xn = ctx.enter_context(nc.sbuf_tensor("xn_sb", [P, TILES, D], F32))
        self.const = ctx.enter_context(nc.sbuf_tensor("const_sb", [P, NCONST], F32))
        self.ps = ctx.enter_context(nc.psum_tensor("ps", [P, 8, 512], F32))
        self.moved = [Moved(ctx.enter_context(nc.semaphore(f"indirect_rows_moved{k}"))) for k in range(8)]

    def c(self, name):
        a, w = CONST[name]
        return self.const[:, a:a + w]


class Stage:

    def __init__(self, core, name):
        self.core, self.nc, self.name = core, core.nc, name
        self.ctx = ExitStack()
        self.sems = []

    def __enter__(self):
        return self

    def __exit__(self, failed, *_):
        if failed is None:
            for s in self.sems:
                self.nc.gpsimd.sem_clear(s)
            self.nc.all_engine_barrier()
        self.ctx.close()

    def sb(self, name, shape, dt=F32):
        return self.ctx.enter_context(self.nc.sbuf_tensor(f"{self.name}_{name}", shape, dt))

    def sem(self, name):
        self.sems.append(self.ctx.enter_context(self.nc.semaphore(f"{self.name}_{name}")))
        return self.sems[-1]

    def moved(self, k, dmas):
        return self.core.moved[k].begin(16 * dmas)

    def block(self):
        return self.nc.Block()


def rows(w):
    return w.rearrange("(k p) m -> p k m", p=P)


def bcast(v):
    return v.partition_broadcast(P)


def load_stage(core, x, consts):
    with Stage(core, "load") as st:
        nc = core.nc
        loaded, zeroed = st.sem("loaded"), st.sem("zeroed")
        with st.block() as block:
            @block.vector
            def _(dve):
                nc.vector.memset(core.x[:, TILES - 1, :], 0.0).then_inc(zeroed, 1)

            @block.sync
            def _(sp):
                sp.dma_start(core.const[:], consts).then_inc(loaded, 16)
                sp.dma_start(core.x[:, 0:TILES - 1, :],
                             x[0:(TILES - 1) * P, :].rearrange("(a p) d -> p a d", p=P)).then_inc(loaded, 16)
                sp.wait_ge(zeroed, 1)
                sp.dma_start(core.x[0:N - (TILES - 1) * P, TILES - 1, :], x[(TILES - 1) * P:N, :]).then_inc(loaded, 16)
                sp.wait_ge(loaded, 48)


def norm_stage(core, name, xt):
    with Stage(core, name) as st:
        nc, x, xn, ps = core.nc, core.x, core.xn, core.ps
        stats = st.sb("stats", [P, TILES, 6])
        mv = st.sb("mv", [P, TILES, 2])
        std = st.sb("std", [P, TILES])
        rstd = st.sb("rstd", [P, TILES])
        chain, var_ready, std_ready, normed = st.sem("chain"), st.sem("var"), st.sem("std"), st.sem("normed")
        transposed, bank_free = st.sem("transposed"), st.sem("bank_free")
        with st.block() as block:
            @block.vector
            def _(dve):
                ch = Chain(dve, chain)
                with ch.loop(TILES, 1) as a:
                    ch.add(nc.vector.bn_stats(stats[:, bass.ds(a, 1), :].rearrange("p a s -> p (a s)"),
                                              x[:, bass.ds(a, 1), :].rearrange("p a d -> p (a d)")))
                ch.settle()
                for a in range(TILES):
                    ch.add(nc.vector.bn_aggr(mv[:, a, :], stats[:, a, :]))
                ch.settle()
                nc.vector.tensor_scalar_add(rstd[:], mv[:, :, 1], 1e-5).then_inc(var_ready, 1)
                dve.wait_ge(std_ready, 1)
                ch.link(nc.vector.reciprocal(rstd[:], std[:]))
                with dve.Fori(0, TILES) as a:
                    nc.vector.tensor_scalar(xn[:, bass.ds(a, 1), :], x[:, bass.ds(a, 1), :],
                                            mv[:, bass.ds(a, 1), 0], rstd[:, bass.ds(a, 1)],
                                            ALU.subtract, ALU.mult).then_inc(normed, 1)

            @block.tensor
            def _(pe):
                for a in range(TILES):
                    pe.wait_ge(normed, a + 1)
                    pe.wait_ge(bank_free, a + 1)
                    for k in range(KD):
                        last = nc.tensor.transpose(ps[:, a % GROUP, k * P:(k + 1) * P], xn[:, a, k * P:(k + 1) * P], core.c("ident"))
                    last.then_inc(transposed, 1)

            @block.scalar
            def _(act):
                act.sem_inc(bank_free, GROUP)
                act.wait_ge(var_ready, 1)
                nc.scalar.activation(std[:], rstd[:], ACT.Sqrt).then_inc(std_ready, 1)
                with act.Fori(0, GROUPS) as g:
                    for j in range(GROUP):
                        act.wait_ge(transposed, g * GROUP + j + 1)
                        nc.scalar.copy(xt[:, :, bass.ds((g * GROUP + j) * P, P)],
                                       ps[:, j, 0:D].rearrange("p (k t) -> p k t", k=KD)).then_inc(bank_free, 1)


def l0_gnn_stage(core, xt, src, dst, weight, attn_l, attn_r, xt_table, al_table):
    H0, C0 = 4, D // 4
    with Stage(core, "g0") as st:
        nc, ps = core.nc, core.ps
        w = st.sb("w", [P, KD, D])
        av = st.sb("av", [P, 2, D])
        idx = st.sb("idx", [P, 2, TILES], I32)
        own = st.sb("own", [P, TILES, D])
        al = st.sb("al", [P, TILES, 2 * H0])
        prod = st.sb("prod", [P, 2, D])
        far = st.sb("far", [P, TILES, D])
        fa = st.sb("fa", [P, 2, TILES, 2 * H0])
        lg = st.sb("lg", [P, TILES, H0])
        lk = st.sb("lk", [P, TILES, H0])
        mx = st.sb("mx", [P, TILES])
        mix = st.sb("mix", [P, GROUP, C0])
        loaded, chain, projected, bank_free, copied = (st.sem(s) for s in ("loaded", "chain", "projected", "bank_free", "copied"))
        rows_ready, stored, centred, expd = (st.sem(s) for s in ("rows_ready", "stored", "centred", "expd"))
        gathered = st.moved(0, 3 * TILES)
        with st.block() as block:
            @block.sync
            def _(sp):
                sp.dma_start(w[:], rows(weight)).then_inc(loaded, 16)
                sp.dma_start(av[:, 0, :], bcast(attn_l)).then_inc(loaded, 16)
                sp.dma_start(av[:, 1, :], bcast(attn_r)).then_inc(loaded, 16)
                sp.dma_start(idx[:, 0, :], src[0:NPAD].rearrange("(a p) -> p a", p=P), allow_slow_non_contiguous=True).then_inc(loaded, 16)
                sp.dma_start(idx[:, 1, :], dst[0:NPAD].rearrange("(a p) -> p a", p=P), allow_slow_non_contiguous=True).then_inc(loaded, 16)
                sp.wait_ge(rows_ready, 1)
                sp.dma_start(xt_table.rearrange("(a p) d -> p a d", p=P), own[:]).then_inc(stored, 16)
                sp.dma_start(al_table.rearrange("(a p) d -> p a d", p=P), al[:]).then_inc(stored, 16)

            @block.tensor
            def _(pe):
                pe.wait_ge(loaded, 80)
                for a in range(TILES):
                    pe.wait_ge(bank_free, a + 1)
                    for k in range(KD):
                        last = nc.tensor.matmul(ps[:, a % GROUP, 0:D], xt[:, k, a * P:(a + 1) * P], w[:, k, :],
                                                start=(k == 0), stop=(k == KD - 1))
                    last.then_inc(projected, 1)

            @block.scalar
            def _(act):
                act.sem_inc(bank_free, GROUP)
                with act.Fori(0, GROUPS) as g:
                    for j in range(GROUP):
                        act.wait_ge(projected, g * GROUP + j + 1)
                        nc.scalar.copy(own[:, bass.ds(g * GROUP + j, 1), :], ps[:, j, 0:D]).then_inc(copied, 1)
                act.wait_ge(centred, 1)
                nc.scalar.activation(lg[:], lk[:], ACT.Exp).then_inc(expd, 1)

            @block.vector
            def _(dve):
                ch = Chain(dve, chain)
                dve.wait_ge(loaded, 80)
                with ch.loop(GROUPS, 4 * GROUP) as g:
                    for j in range(GROUP):
                        dve.wait_ge(copied, g * GROUP + j + 1)
                        for s in range(2):
                            ch.add(nc.vector.tensor_tensor(prod[:, s, :], ps[:, j, 0:D], av[:, s, :], ALU.mult))
                        ch.settle()
                        for s in range(2):
                            ch.add(nc.vector.tensor_reduce(al[:, bass.ds(g * GROUP + j, 1), s * H0:(s + 1) * H0],
                                                           prod[:, s, :].rearrange("p (h c) -> p h c", h=H0), AX, ALU.add))
                        ch.settle()
                        dve.sem_inc(bank_free, 1)
                dve.sem_inc(rows_ready, 1)
                gathered.wait(dve, 3 * TILES * 16)
                ch.link(nc.vector.tensor_tensor(lg[:], fa[:, 0, :, 0:H0], fa[:, 1, :, H0:2 * H0], ALU.add))
                ch.link(nc.vector.scalar_tensor_tensor(lk[:], lg[:], 0.01, lg[:], ALU.mult, ALU.max))
                ch.link(nc.vector.tensor_reduce(mx[:], lk[:], AX, ALU.max))
                nc.vector.tensor_tensor(lk[:], lk[:], mx[:].unsqueeze(2).broadcast_to([P, TILES, H0]), ALU.subtract).then_inc(centred, 1)
                dve.wait_ge(expd, 1)
                ch.link(nc.vector.tensor_reduce(mx[:], lg[:], AX, ALU.add))
                ch.link(nc.vector.reciprocal(mx[:], mx[:]))
                ch.link(nc.vector.tensor_tensor(lk[:], lg[:], mx[:].unsqueeze(2).broadcast_to([P, TILES, H0]), ALU.mult))
                with ch.loop(GROUPS, GROUP * (H0 + 1)) as g:
                    for h in range(H0):
                        for j in range(GROUP):
                            v = far[:, bass.ds(g * GROUP + j, 1), h * C0:(h + 1) * C0].rearrange("p a d -> p (a d)")
                            s = lk[:, bass.ds(g * GROUP + j, 1), h]
                            if h == 0:
                                ch.add(nc.vector.tensor_scalar(mix[:, j, :], v, s, None, ALU.mult))
                            else:
                                ch.add(nc.vector.scalar_tensor_tensor(mix[:, j, :], v, s, mix[:, j, :], ALU.mult, ALU.add))
                        ch.settle()
                    for j in range(GROUP):
                        xa = core.x[:, bass.ds(g * GROUP + j, 1), :].rearrange("p a (h c) -> p (a h) c", h=H0)
                        ch.add(nc.vector.tensor_tensor(xa, xa, mix[:, j, :].unsqueeze(1).broadcast_to([P, H0, C0]), ALU.add))
                    ch.settle()

            @block.gpsimd
            def _(pool):
                pool.wait_ge(loaded, 80)
                pool.wait_ge(stored, 32)
                for a in range(TILES):
                    for to, table, e in ((far[:, a, :], xt_table, 1), (fa[:, 0, a, :], al_table, 0), (fa[:, 1, a, :], al_table, 1)):
                        gathered.count(nc.gpsimd.indirect_dma_start(out=to, out_offset=None, in_=table,
                                                     in_offset=bass.IndirectOffsetOnAxis(ap=idx[:, e, a:a + 1], axis=0),
                                                     bounds_check=NPAD - 1, oob_is_err=False))


def l0_ffn_stage(core, xt, wr, br, w1, b1, w2, b2):
    H = w1.shape[1]
    MH = H // P
    HID, OUT = (0, 1, 2, 3), (4, 5, 6, 4, 5)
    with Stage(core, "f0") as st:
        nc, ps, x = core.nc, core.ps, core.x
        wr_sb, br_sb = st.sb("wr", [P, KD]), st.sb("br", [P, 1])
        w1_sb, b1_sb, w2_sb, b2_sb = st.sb("w1", [P, KD, H]), st.sb("b1", [P, MH]), st.sb("w2", [P, MH, D]), st.sb("b2", [1, D])
        wgt, key = st.sb("wgt", [P, TILES]), st.sb("key", [P, TILES])
        key_row = st.sb("key_row", [P, NPAD])
        hit = st.sb("hit", [P, NPAD], BF16)
        hits = st.sb("hits", [P, TILES, 4])
        rank = st.sb("rank", [P, TILES])
        hid = st.sb("hid", [P, MH, GTOK])
        y = st.sb("y", [P, TILES, D])
        loaded, chain, routed, keyed, spread, spread_free = (st.sem(s) for s in ("loaded", "chain", "routed", "keyed", "spread", "spread_free"))
        hid_ready, hid_free, act_done, out_ready, out_free, y_ready = (st.sem(s) for s in ("hid_ready", "hid_free", "act_done", "out_ready", "out_free", "y_ready"))
        with st.block() as block:
            @block.sync
            def _(sp):
                sp.dma_start(wr_sb[:], wr.rearrange("(k p) -> p k", p=P), allow_slow_non_contiguous=True).then_inc(loaded, 16)
                sp.dma_start(br_sb[:], bcast(br)).then_inc(loaded, 16)
                sp.dma_start(w1_sb[:], rows(w1)).then_inc(loaded, 16)
                sp.dma_start(b1_sb[:], b1.rearrange("(k p) -> p k", p=P), allow_slow_non_contiguous=True).then_inc(loaded, 16)
                sp.dma_start(w2_sb[:], rows(w2)).then_inc(loaded, 16)
                sp.dma_start(b2_sb[:], b2.rearrange("(o d) -> o d", o=1)).then_inc(loaded, 16)

            @block.tensor
            def _(pe):
                pe.wait_ge(loaded, 96)
                for a in range(TILES):
                    for k in range(KD):
                        last = nc.tensor.matmul(ps[:, 7, a:a + 1], xt[:, k, a * P:(a + 1) * P], wr_sb[:, k:k + 1],
                                                start=(k == 0), stop=(k == KD - 1))
                last.then_inc(routed, 1)
                pe.wait_ge(keyed, 1)
                for a in range(TILES):
                    if a >= 4:
                        pe.wait_ge(spread_free, a - 3)
                    nc.tensor.transpose(ps[:, a % 4, 0:P], key[:, a:a + 1].broadcast_to([P, P]), core.c("ident")).then_inc(spread, 1)
                pe.wait_ge(spread_free, TILES)
                with pe.Fori(0, GROUPS) as g:
                    for m in range(MH):
                        for half in range(2):
                            n = m * 2 + half
                            pe.wait_ge(hid_free, g * 2 * MH + n + 1)
                            for k in range(KD):
                                last = nc.tensor.matmul(ps[:, HID[n % 4], 0:HALF], w1_sb[:, k, m * P:(m + 1) * P],
                                                        xt[:, k, bass.ds(g * GTOK + half * HALF, HALF)],
                                                        start=(k == 0), stop=(k == KD - 1))
                            last.then_inc(hid_ready, 1)
                    pe.wait_ge(act_done, (g + 1) * 2 * MH)
                    for j in range(GROUP):
                        pe.wait_ge(out_free, g * GROUP + j + 1)
                        nc.tensor.matmul(ps[:, OUT[j], 0:D], core.c("ones")[0:1, :], b2_sb[:], start=True, stop=False)
                        for m in range(MH):
                            last = nc.tensor.matmul(ps[:, OUT[j], 0:D], hid[:, m, j * P:(j + 1) * P], w2_sb[:, m, :],
                                                    start=False, stop=(m == MH - 1))
                        last.then_inc(out_ready, 1)

            @block.scalar
            def _(act):
                act.sem_inc(hid_free, 4)
                act.sem_inc(out_free, 2)
                for a in range(TILES):
                    act.wait_ge(spread, a + 1)
                    nc.scalar.copy(key_row[:, a * P:(a + 1) * P], ps[:, a % 4, 0:P]).then_inc(spread_free, 1)
                act.wait_ge(loaded, 96)
                with act.Fori(0, GROUPS) as g:
                    act.wait_ge(out_ready, g * GROUP)
                    for m in range(MH):
                        for half in range(2):
                            n = m * 2 + half
                            act.wait_ge(hid_ready, g * 2 * MH + n + 1)
                            nc.scalar.activation(hid[:, m, half * HALF:(half + 1) * HALF], ps[:, HID[n % 4], 0:HALF],
                                                 ACT.Gelu_apprx_tanh, bias=b1_sb[:, m:m + 1]).then_inc(act_done, 1)
                            act.wait_ge(act_done, g * 2 * MH + n + 1)
                            act.sem_inc(hid_free, 1)
                    for j in range(GROUP):
                        act.wait_ge(out_ready, g * GROUP + j + 1)
                        nc.scalar.copy(y[:, bass.ds(g * GROUP + j, 1), :], ps[:, OUT[j], 0:D]).then_inc(y_ready, 1)
                        act.wait_ge(y_ready, g * GROUP + j + 1)
                        act.sem_inc(out_free, 1)

            @block.vector
            def _(dve):
                ch = Chain(dve, chain)
                dve.wait_ge(loaded, 96)
                dve.wait_ge(routed, 1)
                ch.link(nc.vector.tensor_scalar(wgt[:], ps[:, 7, 0:TILES], br_sb[:], None, ALU.add))
                ch.link(nc.vector.tensor_tensor(key[:], wgt[:], core.c("valid"), ALU.mult))
                ch.link(nc.vector.tensor_scalar(rank[:], core.c("valid"), 1.0, BIG, ALU.subtract, ALU.mult))
                nc.vector.tensor_tensor(key[:], key[:], rank[:], ALU.add).then_inc(keyed, 1)
                dve.wait_ge(keyed, 1)
                ch.link(nc.vector.memset(hits[:], 0.0))
                dve.wait_ge(spread_free, TILES)
                for a in range(TILES):
                    own = key[:, a:a + 1]
                    if a > 0:
                        ch.add(nc.vector.tensor_scalar(hit[:, 0:a * P], key_row[:, 0:a * P], own, 0.0, ALU.is_ge, ALU.add,
                                                       accum_out=hits[:, a, 0:1]))
                    if a < TILES - 1:
                        ch.add(nc.vector.tensor_scalar(hit[:, (a + 1) * P:], key_row[:, (a + 1) * P:], own, 0.0, ALU.is_gt, ALU.add,
                                                       accum_out=hits[:, a, 1:2]))
                    ch.add(nc.vector.tensor_scalar(hit[:, a * P:(a + 1) * P], key_row[:, a * P:(a + 1) * P], own, 0.0,
                                                   ALU.is_gt, ALU.add, accum_out=hits[:, a, 2:3]))
                    ch.settle()
                    ch.link(nc.vector.scalar_tensor_tensor(hit[:, a * P:(a + 1) * P], key_row[:, a * P:(a + 1) * P], own,
                                                           core.c("before"), ALU.is_equal, ALU.mult, accum_out=hits[:, a, 3:4]))
                ch.link(nc.vector.tensor_reduce(rank[:], hits[:], AX, ALU.add))
                ch.link(nc.vector.scalar_tensor_tensor(wgt[:], rank[:], float(KEEP), wgt[:], ALU.is_lt, ALU.mult))
                with ch.loop(TILES, 2) as a:
                    dve.wait_ge(y_ready, a + 1)
                    xa = x[:, bass.ds(a, 1), :].rearrange("p a d -> p (a d)")
                    ya = y[:, bass.ds(a, 1), :].rearrange("p a d -> p (a d)")
                    ch.link(nc.vector.scalar_tensor_tensor(ya, ya, wgt[:, bass.ds(a, 1)],
                                                           core.xn[:, bass.ds(a, 1), :].rearrange("p a d -> p (a d)"), ALU.mult, ALU.add))
                    ch.link(nc.vector.tensor_tensor(xa, xa, ya, ALU.add))


def l1_ffn_stage(core, xt, router_wt, router_b, w1, b1t, w2, b2, sel):
    NE = router_wt.shape[1]
    H = w1.shape[1]
    MH = H // P
    HID, OUT = (0, 1, 2, 3), (4, 5, 6, 4, 5)
    with Stage(core, "f1") as st:
        nc, ps, x = core.nc, core.ps, core.x
        rw, rb = st.sb("rw", [P, KD, NE]), st.sb("rb", [P, NE])
        w1_sb, b1_sb, w2_sb, b2_sb, sel_sb = (st.sb("w1", [P, KD, H]), st.sb("b1", [P, MH]), st.sb("w2", [P, MH, D]),
                                              st.sb("b2", [NE, D]), st.sb("sel", [NE, H]))
        lg, top, one_hot = st.sb("lg", [P, TILES, NE]), st.sb("top", [P, TILES]), st.sb("one_hot", [P, TILES, NE])
        choice = st.sb("choice", [NE, NPAD])
        sink = st.sb("sink", [NE, NPAD])
        choice_g = st.sb("choice_g", [NE, GTOK])
        hid = st.sb("hid", [P, MH, GTOK])
        loaded, chain, routed, chosen, turned, turned_free = (st.sem(s) for s in ("loaded", "chain", "routed", "chosen", "turned", "turned_free"))
        sunk, hid_ready, hid_free, out_ready, out_free, choice_ready = (st.sem(s) for s in ("sunk", "hid_ready", "hid_free", "out_ready", "out_free", "choice_ready"))
        FIRST = 13
        with st.block() as block:
            @block.sync
            def _(sp):
                sp.dma_start(rw[:], rows(router_wt)).then_inc(loaded, 16)
                sp.dma_start(rb[:], bcast(router_b)).then_inc(loaded, 16)
                sp.dma_start(w1_sb[:], rows(w1)).then_inc(loaded, 16)
                sp.dma_start(b1_sb[:], b1t).then_inc(loaded, 16)
                sp.dma_start(w2_sb[:], rows(w2)).then_inc(loaded, 16)
                sp.dma_start(b2_sb[:], b2).then_inc(loaded, 16)
                sp.dma_start(sel_sb[:], sel).then_inc(loaded, 16)

            @block.tensor
            def _(pe):
                pe.wait_ge(loaded, 112)
                for a in range(TILES):
                    at = ps[:, 6, a * NE:(a + 1) * NE] if a < FIRST else ps[:, 7, (a - FIRST) * NE:(a - FIRST + 1) * NE]
                    for k in range(KD):
                        last = nc.tensor.matmul(at, xt[:, k, a * P:(a + 1) * P], rw[:, k, :], start=(k == 0), stop=(k == KD - 1))
                last.then_inc(routed, 1)
                pe.wait_ge(chosen, 1)
                for a in range(TILES):
                    if a >= 4:
                        pe.wait_ge(turned_free, a - 3)
                    nc.tensor.transpose(ps[0:NE, a % 4, 0:P], one_hot[:, a, :], core.c("ident")).then_inc(turned, 1)
                pe.wait_ge(turned_free, TILES)
                pe.wait_ge(sunk, 1)
                with pe.Fori(0, GROUPS) as g:
                    for m in range(MH):
                        for half in range(2):
                            n = m * 2 + half
                            pe.wait_ge(hid_free, g * 2 * MH + n + 1)
                            cols = bass.ds(g * GTOK + half * HALF, HALF)
                            for k in range(KD):
                                nc.tensor.matmul(ps[:, HID[n % 4], 0:HALF], w1_sb[:, k, m * P:(m + 1) * P], xt[:, k, cols],
                                                 start=(k == 0), stop=False)
                            nc.tensor.matmul(ps[:, HID[n % 4], 0:HALF], sel_sb[:, m * P:(m + 1) * P], sink[:, cols],
                                             start=False, stop=True).then_inc(hid_ready, 1)
                    pe.wait_ge(hid_free, (g + 1) * 2 * MH + 4)
                    pe.wait_ge(choice_ready, g + 1)
                    for j in range(GROUP):
                        pe.wait_ge(out_free, g * GROUP + j + 1)
                        nc.tensor.matmul(ps[:, OUT[j], 0:D], choice_g[:, j * P:(j + 1) * P], b2_sb[:], start=True, stop=False)
                        for m in range(MH):
                            last = nc.tensor.matmul(ps[:, OUT[j], 0:D], hid[:, m, j * P:(j + 1) * P], w2_sb[:, m, :],
                                                    start=False, stop=(m == MH - 1))
                        last.then_inc(out_ready, 1)

            @block.scalar
            def _(act):
                act.sem_inc(hid_free, 4)
                act.sem_inc(out_free, 2)
                act.wait_ge(loaded, 112)
                for a in range(TILES):
                    act.wait_ge(turned, a + 1)
                    nc.scalar.copy(choice[:, a * P:(a + 1) * P], ps[0:NE, a % 4, 0:P]).then_inc(turned_free, 1)
                act.wait_ge(turned_free, TILES)
                with act.Fori(0, GROUPS) as g:
                    act.wait_ge(out_ready, g * GROUP)
                    nc.scalar.copy(choice_g[:], choice[:, bass.ds(g * GTOK, GTOK)]).then_inc(choice_ready, 1)
                    for m in range(MH):
                        for half in range(2):
                            n = m * 2 + half
                            act.wait_ge(hid_ready, g * 2 * MH + n + 1)
                            nc.scalar.activation(hid[:, m, half * HALF:(half + 1) * HALF], ps[:, HID[n % 4], 0:HALF],
                                                 ACT.Relu, bias=b1_sb[:, m:m + 1]).then_inc(hid_free, 1)

            @block.vector
            def _(dve):
                ch = Chain(dve, chain)
                dve.wait_ge(loaded, 112)
                dve.wait_ge(routed, 1)
                for a0, a1, bank in ((0, FIRST, 6), (FIRST, TILES, 7)):
                    ch.add(nc.vector.tensor_tensor(lg[:, a0:a1, :], ps[:, bank, 0:(a1 - a0) * NE].rearrange("p (a e) -> p a e", e=NE),
                                                   rb[:].unsqueeze(1).broadcast_to([P, a1 - a0, NE]), ALU.add))
                ch.settle()
                ch.link(nc.vector.tensor_reduce(top[:], lg[:], AX, ALU.max))
                ch.link(nc.vector.tensor_tensor(one_hot[:], lg[:], top[:].unsqueeze(2).broadcast_to([P, TILES, NE]), ALU.is_equal))
                ch.link(nc.vector.scalar_tensor_tensor(lg[:], one_hot[:], -2.0 * NE, core.c("iota32").unsqueeze(1).broadcast_to([P, TILES, NE]),
                                                       ALU.mult, ALU.add))
                ch.link(nc.vector.tensor_reduce(top[:], lg[:], AX, ALU.min))
                nc.vector.tensor_tensor(one_hot[:], lg[:], top[:].unsqueeze(2).broadcast_to([P, TILES, NE]), ALU.is_equal).then_inc(chosen, 1)
                dve.wait_ge(turned_free, TILES)
                nc.vector.tensor_scalar(sink[:], choice[:], 1.0, BIG, ALU.subtract, ALU.mult).then_inc(sunk, 1)
                with dve.Fori(0, GROUPS) as g:
                    for j in range(GROUP):
                        dve.wait_ge(out_ready, g * GROUP + j + 1)
                        xa = x[:, bass.ds(g * GROUP + j, 1), :].rearrange("p a d -> p (a d)")
                        nc.vector.scalar_tensor_tensor(xa, ps[:, OUT[j], 0:D], 0.0, xa, ALU.max, ALU.add).then_inc(out_free, 1)


def gate_bias(core, pe, ps, cw, cwt, turned, turned_free, bias, n, bias_ready, bias_free):
    nc = core.nc
    for a in range(TILES):
        if a >= 4:
            pe.wait_ge(turned_free, a - 3)
        nc.tensor.transpose(ps[0:n, a % 4, 0:P], cw[:, a, :], core.c("ident")).then_inc(turned, 1)
    pe.wait_ge(turned_free, TILES)
    for a in range(TILES):
        if a >= 4:
            pe.wait_ge(bias_free, a - 3)
        nc.tensor.matmul(ps[:, a % 4, 0:D], cwt[:, a * P:(a + 1) * P], bias, start=True, stop=True).then_inc(bias_ready, 1)
    pe.wait_ge(bias_free, TILES)


def l2_ffn_stage(core, xt, wr, br, w1, bn1, w2, bn2, wo, bo):
    NE = wr.shape[1]
    EM = NE * KD
    with Stage(core, "f2") as st:
        nc, ps, x = core.nc, core.ps, core.x
        wr_sb, br_sb, bo_sb = st.sb("wr", [P, KD, NE]), st.sb("br", [P, NE]), st.sb("bo", [NE, D])
        w_sb = st.sb("w", [P, 3, NE * KD, D])
        bn = st.sb("bn", [P, 2, 5, EM])
        lg, top, cw = st.sb("lg", [P, TILES, NE]), st.sb("top", [P, TILES]), st.sb("cw", [P, TILES, NE])
        cwt = st.sb("cwt", [NE, NPAD])
        hid = st.sb("hid", [P, 2, 2, KD, GTOK])
        loaded, chain, routed, expd, gated, turned, turned_free = (st.sem(s) for s in ("loaded", "chain", "routed", "expd", "gated", "turned", "turned_free"))
        bias_ready, bias_free, var_ready, std_ready, bn_ready = (st.sem(s) for s in ("bias_ready", "bias_free", "var_ready", "std_ready", "bn_ready"))
        hid_ready, hid_free, out_ready, out_free, expert_out = (st.sem(s) for s in ("hid_ready", "hid_free", "out_ready", "out_free", "expert_out"))
        with st.block() as block:
            @block.sync
            def _(sp):
                sp.dma_start(wr_sb[:], rows(wr)).then_inc(loaded, 16)
                sp.dma_start(br_sb[:], bcast(br)).then_inc(loaded, 16)
                sp.dma_start(bo_sb[:], bo).then_inc(loaded, 16)
                sp.dma_start(bn[:, 0], bn1).then_inc(loaded, 16)
                sp.dma_start(bn[:, 1], bn2).then_inc(loaded, 16)
                for i, w in enumerate((w1, w2, wo)):
                    sp.dma_start(w_sb[:, i], rows(w)).then_inc(loaded, 16)

            @block.tensor
            def _(pe):
                pe.wait_ge(loaded, 128)
                for a in range(TILES):
                    for k in range(KD):
                        last = nc.tensor.matmul(ps[:, 7, a * NE:(a + 1) * NE], xt[:, k, a * P:(a + 1) * P], wr_sb[:, k, :],
                                                start=(k == 0), stop=(k == KD - 1))
                last.then_inc(routed, 1)
                pe.wait_ge(gated, 1)
                gate_bias(core, pe, ps, cw, cwt, turned, turned_free, bo_sb[:], NE, bias_ready, bias_free)

                def hidden(g, e, layer):
                    for m in range(KD):
                        for half in range(2):
                            n = (e * 2 + layer) * 4 + m * 2 + half
                            pe.wait_ge(hid_free, g * NE * 8 + n + 1)
                            for k in range(KD):
                                cols = bass.ds(g * GTOK + half * HALF, HALF) if layer == 0 else slice(half * HALF, (half + 1) * HALF)
                                src = xt[:, k, cols] if layer == 0 else hid[:, e % 2, 0, k, cols]
                                last = nc.tensor.matmul(ps[:, n % 4, 0:HALF], w_sb[:, layer, e * KD + k, m * P:(m + 1) * P], src,
                                                        start=(k == 0), stop=(k == KD - 1))
                            last.then_inc(hid_ready, 1)

                def output(g, e):
                    pe.wait_ge(hid_free, g * NE * 8 + (e * 2 + 2) * 4 + 4)
                    for j in range(GROUP):
                        n = e * GROUP + j
                        pe.wait_ge(out_free, g * NE * GROUP + n + 1)
                        for k in range(KD):
                            last = nc.tensor.matmul(ps[:, 4 + n % 4, 0:D], hid[:, e % 2, 1, k, j * P:(j + 1) * P],
                                                    w_sb[:, 2, e * KD + k, :], start=(k == 0), stop=(k == KD - 1))
                        last.then_inc(out_ready, 1)

                with pe.Fori(0, GROUPS) as g:
                    for e in range(NE):
                        hidden(g, e, 0)
                        if e > 0:
                            output(g, e - 1)
                        pe.wait_ge(hid_free, g * NE * 8 + (e * 2 + 1) * 4 + 4)
                        hidden(g, e, 1)
                    output(g, NE - 1)

            @block.scalar
            def _(act):
                act.sem_inc(hid_free, 4)
                act.sem_inc(out_free, 4)
                act.wait_ge(var_ready, 1)
                nc.scalar.activation(bn[:, :, 4, :], bn[:, :, 4, :], ACT.Sqrt).then_inc(std_ready, 1)
                act.wait_ge(routed, 2)
                nc.scalar.activation(cw[:], lg[:], ACT.Exp).then_inc(expd, 1)
                for a in range(TILES):
                    act.wait_ge(turned, a + 1)
                    nc.scalar.copy(cwt[:, a * P:(a + 1) * P], ps[0:NE, a % 4, 0:P]).then_inc(turned_free, 1)
                act.wait_ge(bn_ready, 1)
                with act.Fori(0, GROUPS) as g:
                    for e in range(NE):
                        for layer in range(2):
                            if layer == 0 and e >= 2:
                                act.wait_ge(out_ready, g * NE * GROUP + (e - 1) * GROUP)
                            if layer == 0 and e < 2:
                                act.wait_ge(out_ready, g * NE * GROUP)
                            for m in range(KD):
                                for half in range(2):
                                    n = (e * 2 + layer) * 4 + m * 2 + half
                                    act.wait_ge(hid_ready, g * NE * 8 + n + 1)
                                    nc.scalar.activation(hid[:, e % 2, layer, m, half * HALF:(half + 1) * HALF], ps[:, n % 4, 0:HALF],
                                                         ACT.Relu, bias=bn[:, layer, 2, e * KD + m:e * KD + m + 1],
                                                         scale=bn[:, layer, 1, e * KD + m:e * KD + m + 1]).then_inc(hid_free, 1)

            @block.vector
            def _(dve):
                ch = Chain(dve, chain)
                dve.wait_ge(loaded, 128)
                ch.link(nc.vector.tensor_scalar_add(bn[:, :, 4, :], bn[:, :, 4, :], 1e-3))
                dve.sem_inc(var_ready, 1)
                dve.wait_ge(std_ready, 1)
                ch.link(nc.vector.reciprocal(bn[:, :, 4, :], bn[:, :, 4, :]))
                ch.link(nc.vector.tensor_tensor(bn[:, :, 1, :], bn[:, :, 1, :], bn[:, :, 4, :], ALU.mult))
                ch.link(nc.vector.tensor_tensor(bn[:, :, 0, :], bn[:, :, 0, :], bn[:, :, 3, :], ALU.subtract))
                ch.link(nc.vector.tensor_tensor(bn[:, :, 0, :], bn[:, :, 0, :], bn[:, :, 1, :], ALU.mult))
                ch.link(nc.vector.tensor_tensor(bn[:, :, 2, :], bn[:, :, 2, :], bn[:, :, 0, :], ALU.add))
                dve.sem_inc(bn_ready, 1)
                dve.wait_ge(routed, 1)
                ch.link(nc.vector.tensor_tensor(lg[:], ps[:, 7, 0:TILES * NE].rearrange("p (a e) -> p a e", e=NE),
                                                br_sb[:].unsqueeze(1).broadcast_to([P, TILES, NE]), ALU.add))
                ch.link(nc.vector.tensor_reduce(top[:], lg[:], AX, ALU.max))
                ch.link(nc.vector.tensor_tensor(lg[:], lg[:], top[:].unsqueeze(2).broadcast_to([P, TILES, NE]), ALU.subtract))
                dve.sem_inc(routed, 1)
                dve.wait_ge(expd, 1)
                ch.link(nc.vector.tensor_reduce(top[:], cw[:], AX, ALU.add))
                ch.link(nc.vector.reciprocal(top[:], top[:]))
                ch.link(nc.vector.tensor_tensor(cw[:], cw[:], top[:].unsqueeze(2).broadcast_to([P, TILES, NE]), ALU.mult))
                dve.sem_inc(gated, 1)
                for a in range(TILES):
                    dve.wait_ge(bias_ready, a + 1)
                    nc.vector.tensor_tensor(x[:, a, :], ps[:, a % 4, 0:D], x[:, a, :], ALU.add).then_inc(bias_free, 1)
                dve.wait_ge(bias_free, TILES)
                with dve.Fori(0, GROUPS) as g:
                    for e in range(NE):
                        if e > 0:
                            dve.wait_ge(out_free, g * NE * GROUP + e * GROUP + 4)
                        for j in range(GROUP):
                            n = e * GROUP + j
                            dve.wait_ge(out_ready, g * NE * GROUP + n + 1)
                            xa = x[:, bass.ds(g * GROUP + j, 1), :].rearrange("p a d -> p (a d)")
                            nc.vector.scalar_tensor_tensor(xa, ps[:, 4 + n % 4, 0:D], cw[:, bass.ds(g * GROUP + j, 1), e], xa,
                                                           ALU.mult, ALU.add).then_inc(out_free, 1)


def l3_ffn_stage(core, xt, sw1, sb1, sw2, sb2, sw3, ew1, eb1, ew2, eb2, ew3, b3, gw, gb):
    NE, EH1, EH2 = 4, 128, 64
    NC = NE + 1
    with Stage(core, "f3") as st:
        nc, ps, x = core.nc, core.ps, core.x
        gw_sb, gb_sb, b3_sb = st.sb("gw", [P, KD, NE]), st.sb("gb", [P, NE]), st.sb("b3", [NC, D])
        sw1_sb, sw2_sb, sw3_sb = st.sb("sw1", [P, KD, D]), st.sb("sw2", [P, KD, P]), st.sb("sw3", [P, D])
        ew1_sb, ew2_sb, ew3_sb = st.sb("ew1", [P, NE, KD, EH1]), st.sb("ew2", [P, NE, EH2]), st.sb("ew3", [EH2, NE, D])
        sb1_sb, sb2_sb, eb1_sb, eb2_sb = st.sb("sb1", [P, KD]), st.sb("sb2", [P, 1]), st.sb("eb1", [P, NE]), st.sb("eb2", [EH2, NE])
        lg, top, gate, first, rest = (st.sb("lg", [P, TILES, NE]), st.sb("top", [P, 2, TILES]), st.sb("gate", [P, TILES, NE]),
                                      st.sb("first", [P, TILES, NE]), st.sb("rest", [P, TILES, NE]))
        cw, cwt = st.sb("cw", [P, TILES, NC]), st.sb("cwt", [NC, NPAD])
        h1 = st.sb("h1", [P, 3, 2, GTOK])
        h2 = st.sb("h2", [P, 3, GTOK])
        names = ("loaded", "chain", "routed", "expd", "gated", "turned", "turned_free", "bias_ready", "bias_free",
                 "hid_ready", "hid_free", "out_ready", "out_free")
        loaded, chain, routed, expd, gated, turned, turned_free, bias_ready, bias_free, hid_ready, hid_free, out_ready, out_free = map(st.sem, names)
        blocks = {(-1, 0): [0, 1], (-1, 1): [0]}
        for e in range(NE):
            blocks[(e, 0)] = blocks[(e, 1)] = [0]
        order = [(-1, 0), (0, 0), (-1, 1), (1, 0), (0, 1), (2, 0), (1, 1), (3, 0), (2, 1), (3, 1)]
        first_use, uses = {}, 0
        for key in order:
            first_use[key] = uses
            uses += 2 * len(blocks[key])
        outs = [-1, 0, 1, 2, 3]
        slot = {-1: 2, 0: 0, 1: 1, 2: 0, 3: 1}
        assert uses == 22
        HIDB = [i % 4 for i in range(20)] + [0, 1]
        OUTS = GROUP * NC
        OUTB = [4 + i % 3 for i in range(OUTS - 1)] + [5]
        with st.block() as block:
            @block.sync
            def _(sp):
                for to, of in ((gw_sb, rows(gw)), (gb_sb, bcast(gb)), (b3_sb, b3), (sw1_sb, rows(sw1)), (sw2_sb, rows(sw2)), (sw3_sb, sw3),
                               (ew2_sb, ew2.rearrange("e p m -> p e m")), (ew3_sb, ew3.rearrange("e p m -> p e m")),
                               (sb1_sb, sb1), (sb2_sb, sb2), (eb1_sb, eb1), (eb2_sb, eb2)):
                    sp.dma_start(to[:], of).then_inc(loaded, 16)
                for e in range(NE):
                    sp.dma_start(ew1_sb[:, e], rows(ew1[e])).then_inc(loaded, 16)

            @block.tensor
            def _(pe):
                pe.wait_ge(loaded, 256)
                for a in range(TILES):
                    for k in range(KD):
                        last = nc.tensor.matmul(ps[:, 7, a * NE:(a + 1) * NE], xt[:, k, a * P:(a + 1) * P], gw_sb[:, k, :],
                                                start=(k == 0), stop=(k == KD - 1))
                last.then_inc(routed, 1)
                pe.wait_ge(gated, 1)
                gate_bias(core, pe, ps, cw, cwt, turned, turned_free, b3_sb[:], NC, bias_ready, bias_free)

                def hidden(g, part, layer):
                    s = slot[part]
                    if layer == 1:
                        pe.wait_ge(hid_free, g * uses + first_use[(part, 0)] + 2 * len(blocks[(part, 0)]) + 2)
                    for m in blocks[(part, layer)]:
                        for half in range(2):
                            n = first_use[(part, layer)] + m * 2 + half
                            pe.wait_ge(hid_free, g * uses + n + 1)
                            cols = slice(half * HALF, (half + 1) * HALF)
                            if layer == 0:
                                w = [(sw1_sb[:, k, m * P:(m + 1) * P] if part < 0 else ew1_sb[:, part, k, :]) for k in range(KD)]
                                v = [xt[:, k, bass.ds(g * GTOK + half * HALF, HALF)] for k in range(KD)]
                            elif part < 0:
                                w = [sw2_sb[:, k, :] for k in range(KD)]
                                v = [h1[:, s, k, cols] for k in range(KD)]
                            else:
                                w, v = [ew2_sb[:, part, :]], [h1[:, s, 0, cols]]
                            rows_out = EH2 if (part >= 0 and layer == 1) else P
                            for k in range(len(w)):
                                last = nc.tensor.matmul(ps[0:rows_out, HIDB[n], 0:HALF], w[k], v[k], start=(k == 0), stop=(k == len(w) - 1))
                            last.then_inc(hid_ready, 1)

                def output(g, i):
                    part = outs[i]
                    s = slot[part]
                    pe.wait_ge(hid_free, g * uses + first_use[(part, 1)] + 2 + 2)
                    for j in range(GROUP):
                        n = i * GROUP + j
                        pe.wait_ge(out_free, g * OUTS + n + 1)
                        if part < 0:
                            w, v = h2[:, s, j * P:(j + 1) * P], sw3_sb[:]
                        else:
                            w, v = h2[0:EH2, s, j * P:(j + 1) * P], ew3_sb[:, part, :]
                        nc.tensor.matmul(ps[:, OUTB[n], 0:D], w, v, start=True, stop=True).then_inc(out_ready, 1)

                with pe.Fori(0, GROUPS) as g:
                    hidden(g, -1, 0)
                    hidden(g, 0, 0)
                    hidden(g, -1, 1)
                    hidden(g, 1, 0)
                    output(g, 0)
                    hidden(g, 0, 1)
                    hidden(g, 2, 0)
                    output(g, 1)
                    hidden(g, 1, 1)
                    hidden(g, 3, 0)
                    output(g, 2)
                    hidden(g, 2, 1)
                    output(g, 3)
                    hidden(g, 3, 1)
                    output(g, 4)

            @block.scalar
            def _(act):
                act.sem_inc(hid_free, 2)
                act.sem_inc(out_free, 2)
                act.wait_ge(routed, 2)
                nc.scalar.activation(gate[:], lg[:], ACT.Exp).then_inc(expd, 1)
                act.wait_ge(expd, 2)
                nc.scalar.activation(rest[:], lg[:], ACT.Exp).then_inc(expd, 1)
                for a in range(TILES):
                    act.wait_ge(turned, a + 1)
                    nc.scalar.copy(cwt[:, a * P:(a + 1) * P], ps[0:NC, a % 4, 0:P]).then_inc(turned_free, 1)
                act.wait_ge(loaded, 256)
                with act.Fori(0, GROUPS) as g:
                    act.wait_ge(out_ready, g * OUTS)
                    for part, layer in order:
                        s = slot[part]
                        if part >= 2 and layer == 0:
                            act.wait_ge(out_ready, g * OUTS + GROUP * (outs.index(part - 2) + 1))
                        for m in blocks[(part, layer)]:
                            for half in range(2):
                                n = first_use[(part, layer)] + m * 2 + half
                                cols = slice(half * HALF, (half + 1) * HALF)
                                act.wait_ge(hid_ready, g * uses + n + 1)
                                if layer == 0:
                                    to, b = h1[:, s, m, cols], (sb1_sb[:, m:m + 1] if part < 0 else eb1_sb[:, part:part + 1])
                                elif part < 0:
                                    to, b = h2[:, s, cols], sb2_sb[:]
                                else:
                                    to, b = h2[0:EH2, s, cols], eb2_sb[:, part:part + 1]
                                nc.scalar.activation(to, ps[0:to.shape[0], HIDB[n], 0:HALF], ACT.Relu, bias=b).then_inc(hid_free, 1)

            @block.vector
            def _(dve):
                ch = Chain(dve, chain)
                b = lambda v: v.unsqueeze(2).broadcast_to([P, TILES, NE])
                iota = core.c("iota32")[:, 0:NE].unsqueeze(1).broadcast_to([P, TILES, NE])
                dve.wait_ge(loaded, 256)
                dve.wait_ge(routed, 1)
                ch.link(nc.vector.tensor_tensor(lg[:], ps[:, 7, 0:TILES * NE].rearrange("p (a e) -> p a e", e=NE),
                                                gb_sb[:].unsqueeze(1).broadcast_to([P, TILES, NE]), ALU.add))
                ch.link(nc.vector.tensor_reduce(top[:, 0], lg[:], AX, ALU.max))
                ch.link(nc.vector.tensor_tensor(lg[:], lg[:], b(top[:, 0]), ALU.subtract))
                dve.sem_inc(routed, 1)
                dve.wait_ge(expd, 1)
                ch.link(nc.vector.tensor_reduce(top[:, 0], gate[:], AX, ALU.add))
                ch.link(nc.vector.reciprocal(top[:, 0], top[:, 0]))
                ch.link(nc.vector.tensor_tensor(gate[:], gate[:], b(top[:, 0]), ALU.mult))

                def pick(values, best, to):
                    ch.link(nc.vector.tensor_reduce(best, values, AX, ALU.max))
                    ch.link(nc.vector.tensor_tensor(to, values, b(best), ALU.is_equal))
                    ch.link(nc.vector.scalar_tensor_tensor(lg[:], to, -2.0 * NE, iota, ALU.mult, ALU.add))
                    ch.link(nc.vector.tensor_reduce(top[:, 1], lg[:], AX, ALU.min))
                    ch.link(nc.vector.tensor_tensor(to, lg[:], b(top[:, 1]), ALU.is_equal))

                pick(gate[:], top[:, 0], first[:])
                ch.link(nc.vector.scalar_tensor_tensor(rest[:], first[:], -4.0, gate[:], ALU.mult, ALU.add))
                ch.link(nc.vector.tensor_reduce(top[:, 1], rest[:], AX, ALU.max))
                pick(rest[:], top[:, 1], cw[:, :, 0:NE])
                ch.link(nc.vector.tensor_tensor(first[:], first[:], cw[:, :, 0:NE], ALU.add))
                ch.link(nc.vector.tensor_tensor(lg[:], gate[:], b(top[:, 0]), ALU.subtract))
                dve.sem_inc(expd, 1)
                dve.wait_ge(expd, 3)
                ch.link(nc.vector.tensor_tensor(rest[:], rest[:], first[:], ALU.mult))
                ch.link(nc.vector.tensor_reduce(top[:, 1], rest[:], AX, ALU.add))
                ch.link(nc.vector.reciprocal(top[:, 1], top[:, 1]))
                ch.link(nc.vector.memset(cw[:], 1.0))
                ch.link(nc.vector.tensor_tensor(cw[:, :, 0:NE], rest[:], b(top[:, 1]), ALU.mult))
                dve.sem_inc(gated, 1)
                for a in range(TILES):
                    dve.wait_ge(bias_ready, a + 1)
                    nc.vector.tensor_tensor(x[:, a, :], ps[:, a % 4, 0:D], x[:, a, :], ALU.add).then_inc(bias_free, 1)
                dve.wait_ge(bias_free, TILES)
                with dve.Fori(0, GROUPS) as g:
                    for i, part in enumerate(outs):
                        c = NE if part < 0 else part
                        if i > 0:
                            dve.wait_ge(out_free, g * OUTS + i * GROUP + 2)
                        for j in range(GROUP):
                            n = i * GROUP + j
                            dve.wait_ge(out_ready, g * OUTS + n + 1)
                            xa = x[:, bass.ds(g * GROUP + j, 1), :].rearrange("p a d -> p (a d)")
                            nc.vector.scalar_tensor_tensor(xa, ps[:, OUTB[n], 0:D], cw[:, bass.ds(g * GROUP + j, 1), c], xa,
                                                           ALU.mult, ALU.add).then_inc(out_free, 1)


def count_stage(core, keys, split, base, count):
    with Stage(core, "count") as st:
        nc, ps = core.nc, core.ps
        raw = st.sb("raw", [P, 2, 3, ETILES], I32)
        lo_hot = st.sb("lo_hot", [P, 2, CT, P], BF16)
        hi_hot = st.sb("hi_hot", [P, 2, CT, TILES], BF16)
        zero = st.sb("zero", [P, P], BF16)
        total = st.sb("total", [P, 2, TILES])
        run = st.sb("run", [P, 2, TILES])
        loaded, chain, hot, used, opened, counted, summed = (st.sem(s) for s in ("loaded", "chain", "hot", "used", "opened", "counted", "summed"))
        iota = core.c("iota").unsqueeze(1).broadcast_to([P, CT, P])
        iota25 = core.c("iota25").unsqueeze(1).broadcast_to([P, CT, TILES])
        with st.block() as block:
            @block.sync
            def _(sp):
                for s in range(2):
                    sp.dma_start(raw[:, s, 0, :].rearrange("p (c t) -> p c t", t=CT),
                                 keys[s].rearrange("(c p t) -> p c t", p=P, t=CT)).then_inc(loaded, 16)

            @block.vector
            def _(dve):
                ch = Chain(dve, chain)
                ch.add(nc.vector.memset(zero[:], 0.0))
                dve.wait_ge(loaded, 32)
                ch.add(nc.vector.tensor_scalar(raw[:, :, 1, :], raw[:, :, 0, :], P - 1, None, ALU.bitwise_and))
                ch.add(nc.vector.tensor_scalar(raw[:, :, 2, :], raw[:, :, 0, :], 7, None, ALU.logical_shift_right))
                ch.settle()
                ch.link(nc.vector.tensor_copy(split[:], raw[:]))
                dve.sem_inc(opened, 1)
                for s in range(2):
                    with ch.loop(CHUNKS // 2, 4) as i:
                        for q in range(2):
                            dve.wait_ge(used, i * 2 + q + s * CHUNKS + 1)
                            at = bass.ds((i * 2 + q) * CT, CT)
                            ch.add(nc.vector.tensor_tensor(lo_hot[:, q], iota, split[:, s, 1, at].unsqueeze(2).broadcast_to([P, CT, P]), ALU.is_equal))
                            ch.add(nc.vector.tensor_tensor(hi_hot[:, q], iota25, split[:, s, 2, at].unsqueeze(2).broadcast_to([P, CT, TILES]), ALU.is_equal))
                            ch.settle()
                            dve.sem_inc(hot, 1)
                dve.wait_ge(counted, 2)
                ch.link(nc.vector.tensor_copy(count[:], ps[:, 0:2, 0:TILES]))
                dve.sem_inc(opened, 1)
                dve.wait_ge(summed, 1)
                ch.link(nc.vector.tensor_copy(total[:], ps[:, 4:6, 0:TILES]))
                for s in range(2):
                    ch.add(nc.vector.tensor_tensor_scan(run[:, s], total[:, s], total[:, s], 0.0, ALU.add, ALU.max))
                ch.settle()
                ch.link(nc.vector.tensor_tensor(run[:], run[:], total[:], ALU.subtract))
                ch.link(nc.vector.tensor_tensor(base[:], ps[:, 2:4, 0:TILES], run[:], ALU.add))

            @block.tensor
            def _(pe):
                pe.sem_inc(used, 2)
                pe.wait_ge(opened, 1)
                for s in range(2):
                    nc.tensor.matmul(ps[:, s, 0:TILES], zero[:], zero[:, 0:TILES], start=True, stop=False)
                    with pe.Fori(0, CHUNKS // 2) as i:
                        for q in range(2):
                            pe.wait_ge(hot, i * 2 + q + s * CHUNKS + 1)
                            for t in range(CT):
                                last = nc.tensor.matmul(ps[:, s, 0:TILES], lo_hot[:, q, t, :], hi_hot[:, q, t, :], start=False, stop=False)
                            last.then_inc(used, 1)
                    nc.tensor.matmul(ps[:, s, 0:TILES], zero[:], zero[:, 0:TILES], start=False, stop=True).then_inc(counted, 1)
                pe.wait_ge(opened, 2)
                for s in range(2):
                    nc.tensor.matmul(ps[:, 2 + s, 0:TILES], core.c("lt"), count[:, s], start=True, stop=True)
                    last = nc.tensor.matmul(ps[:, 4 + s, 0:TILES], core.c("ones"), count[:, s], start=True, stop=True)
                last.then_inc(summed, 1)


def sort_stage(core, name, s, split, base, payload, width, table, project=None):
    W = width + 2
    with Stage(core, name) as st:
        nc, ps = core.nc, core.ps
        own = st.sb("own", [P, 2, 3, CT])
        lo_hot = st.sb("lo_hot", [P, 2, CT, P])
        hi_hot = st.sb("hi_hot", [P, 2, CT, TILES])
        lo_hot_t = st.sb("lo_hot_t", [P, 2, P])
        running = st.sb("running", [P, 2, TILES])
        scrap = st.sb("scrap", [P, P])
        picked = st.sb("picked", [P, CT, TILES])
        rank = st.sb("rank", [P, CT])
        before = st.sb("before", [P, CT])
        place = st.sb("place", [P, 2, CT], I32)
        row = st.sb("row", [P, 2, CT, W])
        if project is not None:
            w_sb = st.sb("w", [P, KD, D])
            attr = st.sb("attr", [P, 2, CT, D])
            attr_t = st.sb("attr_t", [P, 2, KD, P])
            w_loaded, attr_free, attr_turned, attr_copied, projected, moved = (st.sem(x) for x in ("w_loaded", "attr_free", "attr_turned", "attr_copied", "projected", "moved"))
        loaded = [st.sem("loaded0"), st.sem("loaded1")]
        scattered = [st.moved(q, CHUNKS // 2 * CT) for q in range(2)]
        chain, hot, keys_turned, ranked, hot_turned, hot_copied, snapped, looked, counted, placed, pool_passed = (
            st.sem(x) for x in ("chain", "hot", "keys_turned", "ranked", "hot_turned", "hot_copied", "snapped", "looked", "counted", "placed", "pool_passed"))
        RUN, LOOK, KEYS, HOT, ATTR, PROJ = 0, 1, 2, 3, (4, 5), (6, 7)
        iota25 = core.c("iota25").unsqueeze(1).broadcast_to([P, CT, TILES])
        with st.block() as block:
            @block.sync
            def _(sp):
                if project is not None:
                    sp.dma_start(w_sb[:], rows(project)).then_inc(w_loaded, 16)
                with sp.Fori(0, CHUNKS // 2) as i:
                    for q in range(2):
                        c = i * 2 + q
                        if project is None:
                            scattered[q].wait(sp, i * CT * 16)
                            to = row[:, q, :, 0:width]
                        else:
                            sp.wait_ge(attr_free, c + 1)
                            to = attr[:, q]
                        sp.dma_start(to, payload[bass.ds(c * CHUNK, CHUNK), :].rearrange("(p t) d -> p t d", t=CT)).then_inc(loaded[q], 16)
                for q in range(2):
                    scattered[q].wait(sp, (CHUNKS // 2) * CT * 16)

            @block.gpsimd
            def _(pool):
                with pool.Fori(0, CHUNKS // 2) as i:
                    for q in range(2):
                        c = i * 2 + q
                        pool.wait_ge(placed, c + 1)
                        if project is None:
                            pool.wait_ge(loaded[q], (i + 1) * 16)
                        pool.sem_inc(pool_passed, 1)
                        for t in range(CT):
                            scattered[q].count(nc.gpsimd.indirect_dma_start(out=table, out_offset=bass.IndirectOffsetOnAxis(ap=place[:, q, t:t + 1], axis=0),
                                                         in_=row[:, q, t, :], in_offset=None,
                                                         bounds_check=EPAD - 1, oob_is_err=False))

            @block.tensor
            def _(pe):
                nc.tensor.matmul(ps[:, RUN, 0:TILES], core.c("ident"), base[:, s], start=True, stop=True, skip_group_check=True).then_inc(counted, 1)
                if project is not None:
                    pe.wait_ge(w_loaded, 16)
                with pe.Fori(0, CHUNKS // 2) as i:
                    for q in range(2):
                        c = i * 2 + q
                        pe.wait_ge(hot, c + 1)
                        if project is not None:
                            pe.wait_ge(loaded[q], (i + 1) * 16)
                        for b in range(4):
                            pe.wait_ge(ranked, c * 4 + b)
                            for t in range(4):
                                last = nc.tensor.transpose(ps[:, KEYS, t * P:(t + 1) * P], own[:, q, 0, b * 4 + t:b * 4 + t + 1].broadcast_to([P, P]), core.c("ident"))
                            last.then_inc(keys_turned, 1)
                            for t in range(4 * b, 4 * b + 4):
                                n = c * CT + t
                                pe.wait_ge(hot_copied, n)
                                nc.tensor.transpose(ps[:, HOT, 0:P], lo_hot[:, q, t, :], core.c("ident")).then_inc(hot_turned, 1)
                                if project is not None:
                                    pe.wait_ge(attr_copied, n + 1)
                                    for k in range(KD):
                                        last = nc.tensor.transpose(ps[:, ATTR[t % 2], k * P:(k + 1) * P], attr[:, q, t, k * P:(k + 1) * P], core.c("ident"))
                                    last.then_inc(attr_turned, 1)
                                pe.wait_ge(snapped, n + 1)
                                pe.wait_ge(hot_copied, n + 1)
                                if t == 0:
                                    pe.wait_ge(placed, c)
                                nc.tensor.matmul(ps[:, LOOK, t * TILES:(t + 1) * TILES], lo_hot_t[:, t % 2, :], running[:, t % 2, :],
                                                 start=True, stop=True).then_inc(looked, 1)
                                nc.tensor.matmul(ps[:, RUN, 0:TILES], lo_hot[:, q, t, :], hi_hot[:, q, t, :],
                                                 start=False, stop=True, skip_group_check=True).then_inc(counted, 1)
                                if project is not None:
                                    pe.wait_ge(attr_copied, n + 2 + 1)
                                    pe.wait_ge(moved, n + 1)
                                    for k in range(KD):
                                        last = nc.tensor.matmul(ps[:, PROJ[t % 2], 0:D], attr_t[:, t % 2, k, :], w_sb[:, k, :],
                                                                start=(k == 0), stop=(k == KD - 1))
                                    last.then_inc(projected, 1)

            @block.scalar
            def _(act):
                if project is not None:
                    act.sem_inc(attr_copied, 2)
                    act.sem_inc(attr_free, 2)
                with act.Fori(0, CHUNKS // 2) as i:
                    for q in range(2):
                        for t in range(CT):
                            n = (i * 2 + q) * CT + t
                            act.wait_ge(hot_turned, n + 1)
                            if t >= 1:
                                act.wait_ge(looked, n - 1)
                            else:
                                act.wait_ge(looked, (i * 2 + q) * CT)
                            nc.scalar.copy(lo_hot_t[:, t % 2, :], ps[:, HOT, 0:P]).then_inc(hot_copied, 1)
                            act.wait_ge(counted, n + 1)
                            nc.scalar.copy(running[:, t % 2, :], ps[:, RUN, 0:TILES]).then_inc(snapped, 1)
                            if project is not None:
                                act.wait_ge(attr_turned, n + 1)
                                if t >= 1:
                                    act.wait_ge(projected, n - 1)
                                else:
                                    act.wait_ge(projected, (i * 2 + q) * CT)
                                nc.scalar.copy(attr_t[:, t % 2], ps[:, ATTR[t % 2], 0:D].rearrange("p (k e) -> p k e", k=KD)).then_inc(attr_copied, 1)
                                if t == CT - 1:
                                    act.sem_inc(attr_free, 1)

            @block.vector
            def _(dve):
                ch = Chain(dve, chain)
                if project is not None:
                    dve.sem_inc(moved, 2)
                with ch.loop(CHUNKS // 2, 2 * (1 + CT + 1 + CT + 2 + 4)) as i:
                    for q in range(2):
                        c = i * 2 + q
                        dve.wait_ge(counted, c * CT)
                        ch.link(nc.vector.tensor_scalar(own[:, q], split[:, s, :, bass.ds(c * CT, CT)], 1.0, None, ALU.mult))
                        for t in range(CT):
                            ch.add(nc.vector.tensor_scalar(lo_hot[:, q, t, :], core.c("iota"), own[:, q, 1, t:t + 1], None, ALU.is_equal))
                        ch.add(nc.vector.tensor_tensor(hi_hot[:, q], iota25, own[:, q, 2].unsqueeze(2).broadcast_to([P, CT, TILES]), ALU.is_equal))
                        ch.settle()
                        dve.sem_inc(hot, 1)
                        scattered[q].wait(dve, i * CT * 16)
                        ch.add(nc.vector.tensor_scalar(row[:, q, :, width], split[:, s, 0, bass.ds(c * CT, CT)], 1.0, None, ALU.mult))
                        ch.add(nc.vector.tensor_scalar(row[:, q, :, width + 1], split[:, 1 - s, 0, bass.ds(c * CT, CT)], 1.0, None, ALU.mult))
                        for b in range(4):
                            dve.wait_ge(keys_turned, c * 4 + b + 1)
                            for t in range(4 * b, 4 * b + 4):
                                ch.link(nc.vector.scalar_tensor_tensor(scrap[:], ps[:, KEYS, (t % 4) * P:(t % 4 + 1) * P], own[:, q, 0, t:t + 1],
                                                                       core.c("before"), ALU.is_equal, ALU.mult, accum_out=rank[:, t:t + 1]))
                            dve.sem_inc(ranked, 1)
                            if project is not None:
                                for t in range(4 * b, 4 * b + 4):
                                    dve.wait_ge(projected, c * CT + t + 1)
                                    nc.vector.tensor_copy(row[:, q, t, 0:D], ps[:, PROJ[t % 2], 0:D]).then_inc(moved, 1)
                        dve.wait_ge(looked, (c + 1) * CT)
                        if project is not None:
                            dve.wait_ge(moved, (c + 1) * CT + 2)
                        ch.link(nc.vector.tensor_tensor(picked[:], ps[:, LOOK, 0:CT * TILES].rearrange("p (t a) -> p t a", a=TILES), hi_hot[:, q], ALU.mult))
                        ch.link(nc.vector.tensor_reduce(before[:], picked[:], AX, ALU.add))
                        ch.link(nc.vector.tensor_tensor(before[:], before[:], rank[:], ALU.add))
                        ch.link(nc.vector.tensor_copy(place[:, q], before[:]))
                        dve.sem_inc(placed, 1)


def project_stage(core, xt, weights, biases, q_table, kv_table):
    with Stage(core, "p1") as st:
        nc, ps, x = core.nc, core.ps, core.x
        w_sb, b_sb = st.sb("w", [P, 4, KD, D]), st.sb("b", [P, 4, D])
        out = st.sb("out", [P, 3, TILES, D])
        skip = st.sb("skip", [P, D])
        loaded, chain, projected, bank_free, stored = (st.sem(s) for s in ("loaded", "chain", "projected", "bank_free", "stored"))
        with st.block() as block:
            @block.sync
            def _(sp):
                for i in range(4):
                    sp.dma_start(w_sb[:, i], rows(weights[i])).then_inc(loaded, 16)
                    sp.dma_start(b_sb[:, i], bcast(biases[i])).then_inc(loaded, 16)
                sp.wait_ge(bank_free, 4 * TILES + 4)
                sp.dma_start(q_table.rearrange("(a p) d -> p a d", p=P), out[:, 0]).then_inc(stored, 16)
                for i in range(2):
                    sp.dma_start(kv_table[:, i * D:(i + 1) * D].rearrange("(a p) d -> p a d", p=P), out[:, 1 + i]).then_inc(stored, 16)
                sp.wait_ge(stored, 48)

            @block.tensor
            def _(pe):
                pe.sem_inc(bank_free, 4)
                pe.wait_ge(loaded, 128)
                for a in range(TILES):
                    for i in range(4):
                        pe.wait_ge(bank_free, a * 4 + i + 1)
                        for k in range(KD):
                            last = nc.tensor.matmul(ps[:, i, 0:D], xt[:, k, a * P:(a + 1) * P], w_sb[:, i, k, :], start=(k == 0), stop=(k == KD - 1))
                        last.then_inc(projected, 1)

            @block.vector
            def _(dve):
                ch = Chain(dve, chain)
                dve.wait_ge(loaded, 128)
                with ch.loop(TILES, 2) as a:
                    for i in range(3):
                        dve.wait_ge(projected, a * 4 + i + 1)
                        nc.vector.tensor_tensor(out[:, i, bass.ds(a, 1), :].rearrange("p a d -> p (a d)"), ps[:, i, 0:D], b_sb[:, i], ALU.add).then_inc(bank_free, 1)
                    dve.wait_ge(projected, a * 4 + 4)
                    ch.link(nc.vector.tensor_tensor(skip[:], ps[:, 3, 0:D], b_sb[:, 3], ALU.add))
                    dve.sem_inc(bank_free, 1)
                    xa = x[:, bass.ds(a, 1), :].rearrange("p a d -> p (a d)")
                    ch.link(nc.vector.tensor_tensor(xa, xa, skip[:], ALU.add))


def attend_stage(core, name, ends, src_table, dst_table, edge_rows, partial, scale):
    RING = 8 if edge_rows is not None else 2 * CT
    SW, DW = src_table.shape[1], dst_table.shape[1]
    with Stage(core, name) as st:
        nc, ps = core.nc, core.ps
        if edge_rows is not None:
            edge = st.sb("edge", [P, 2, CT, D + 2])
            prod = st.sb("prod", [P, 2, D])
            edge_loaded = [st.sem("edge_loaded0"), st.sem("edge_loaded1")]
            scored = st.sem("scored")
        far = st.sb("far", [P, RING, SW])
        near = st.sb("near", [P, RING, DW])
        index = st.sb("index", [P, 2, 2, CT], I32)
        node = st.sb("node", [P, 2, CT])
        alpha = st.sb("alpha", [P, CT, HEADS])
        raw = st.sb("raw", [P, CT, HEADS])
        node_t = st.sb("node_t", [P, P])
        fresh = st.sb("fresh", [P, P + 1])
        up, down = st.sb("up", [P, P]), st.sb("down", [P, P])
        weight = st.sb("weight", [P, CT, HEADS])
        same = st.sb("same", [P, 2, P])
        msg = st.sb("msg", [P, 2, SEG])
        out = st.sb("out", [P, 2, CT, ROW])
        gathered = [st.moved(k, CHUNKS * 2 * CT // 8 if edge_rows is not None else CHUNKS * CT) for k in range(RING if edge_rows is not None else 2)]
        stored = [st.sem("stored0"), st.sem("stored1")]
        chain, indexed, ring_free, chunk_free, alpha_ready, turned, node_copied, top_ready, top_turned = (
            st.sem(x) for x in ("chain", "indexed", "ring_free", "chunk_free", "alpha_ready", "turned", "node_copied", "top_ready", "top_turned"))
        centred, weighed, keys_turned, msg_ready, summed, copied, pool_passed = (st.sem(x) for x in ("centred", "weighed", "keys_turned", "msg_ready", "summed", "copied", "pool_passed"))
        SCORES, NODES, TOPS, KEYS, SUMS = 0, 1, 2, (3, 4), (5, 6)
        PER = 16 * 2 * (CT // 8)
        with st.block() as block:
            @block.sync
            def _(sp):
                with sp.Fori(0, CHUNKS // 2) as i:
                    for q in range(2):
                        c = i * 2 + q
                        if edge_rows is not None:
                            sp.wait_ge(chunk_free, c + 1)
                            sp.dma_start(edge[:, q], edge_rows[bass.ds(c * CHUNK, CHUNK), :].rearrange("(t p) d -> p t d", p=P)).then_inc(edge_loaded[q], 16)

            @block.gpsimd
            def _(pool):
                with pool.Fori(0, CHUNKS // 2) as i:
                    for q in range(2):
                        c = i * 2 + q
                        for t in range(CT):
                            slot = t % 8 if edge_rows is not None else q * CT + t
                            if edge_rows is not None:
                                pool.wait_ge(indexed, c + 1)
                                pool.wait_ge(ring_free, c * CT + t + 1)
                            elif t == 0:
                                pool.wait_ge(indexed, c + 1)
                                pool.wait_ge(chunk_free, c + 1)
                            pool.sem_inc(pool_passed, 1)
                            for to, table, e in ((near[:, slot, :], dst_table, 0), (far[:, slot, :], src_table, 1)):
                                gathered[slot if edge_rows is not None else q].count(nc.gpsimd.indirect_dma_start(out=to, out_offset=None, in_=table,
                                                             in_offset=bass.IndirectOffsetOnAxis(ap=index[:, q, e, t:t + 1], axis=0),
                                                             bounds_check=NPAD - 1, oob_is_err=False))

            @block.tensor
            def _(pe):
                ident = core.c("ident")
                with pe.Fori(0, CHUNKS // 2) as i:
                    for q in range(2):
                        c = i * 2 + q
                        pe.wait_ge(alpha_ready, c + 1)
                        nc.tensor.transpose(ps[:, SCORES, 0:P], alpha[:].rearrange("p t h -> p (t h)"), ident)
                        nc.tensor.transpose(ps[:, NODES, 0:P], raw[:].rearrange("p t h -> p (t h)"), ident).then_inc(turned, 1)
                        pe.wait_ge(top_ready, c + 1)
                        nc.tensor.transpose(ps[:, TOPS, 0:P], down[:], ident).then_inc(top_turned, 1)
                        for t in range(CT):
                            n = c * CT + t
                            if t % 4 == 0:
                                pe.wait_ge(msg_ready, n - 4 if t > 0 else n)
                                for u in range(4):
                                    last = nc.tensor.transpose(ps[:, KEYS[(t // 4) % 2], u * P:(u + 1) * P], node[:, q, t + u:t + u + 1].broadcast_to([P, P]), ident)
                                last.then_inc(keys_turned, 1)
                            pe.wait_ge(msg_ready, n + 1)
                            pe.wait_ge(copied, n + 1)
                            nc.tensor.matmul(ps[:, SUMS[t % 2], 0:SEG], same[:, t % 2, :], msg[:, t % 2, :], start=True, stop=True).then_inc(summed, 1)

            @block.scalar
            def _(act):
                act.sem_inc(copied, 2)
                with act.Fori(0, CHUNKS // 2) as i:
                    for q in range(2):
                        c = i * 2 + q
                        act.wait_ge(turned, c + 1)
                        nc.scalar.copy(node_t[:], ps[:, NODES, 0:P]).then_inc(node_copied, 1)
                        act.wait_ge(stored[q], i * 16)
                        act.wait_ge(centred, c + 1)
                        nc.scalar.activation(weight[:], raw[:], ACT.Exp, scale=scale).then_inc(weighed, 1)
                        for t in range(CT):
                            n = c * CT + t
                            act.wait_ge(summed, n + 1)
                            nc.scalar.copy(out[:, q, t, 0:SEG], ps[:, SUMS[t % 2], 0:SEG]).then_inc(copied, 1)
                        act.wait_ge(copied, (c + 1) * CT + 2)
                        act.dma_start(partial[bass.ds(c * CHUNK, CHUNK), :].rearrange("(t p) d -> p t d", p=P), out[:, q]).then_inc(stored[q], 16)
                for q in range(2):
                    act.wait_ge(stored[q], (CHUNKS // 2) * 16)

            @block.vector
            def _(dve):
                ch = Chain(dve, chain)
                dve.sem_inc(chunk_free, 2)
                if edge_rows is not None:
                    dve.sem_inc(ring_free, RING)
                ch.link(nc.vector.memset(fresh[:], 0.0))
                heads = lambda v: v.rearrange("p (h c) -> p h c", h=HEADS)
                per = 2 * ((4 if edge_rows is not None else 3) + (4 * CT if edge_rows is not None else 2) + 1 + 5 + 2 + 2 * CT)
                with ch.loop(CHUNKS // 2, per) as i:
                    for q in range(2):
                        c = i * 2 + q
                        if edge_rows is not None:
                            dve.wait_ge(edge_loaded[q], (i + 1) * 16)
                            for e in range(2):
                                ch.add(nc.vector.tensor_scalar(ends[:, e, bass.ds(c * CT, CT)], edge[:, q, :, D + e], 1.0, None, ALU.mult))
                            ch.add(nc.vector.tensor_copy(index[:, q], edge[:, q, :, D:D + 2].rearrange("p t e -> p e t")))
                            ch.add(nc.vector.tensor_copy(node[:, q], edge[:, q, :, D]))
                        else:
                            for e in range(2):
                                ch.add(nc.vector.tensor_scalar(index[:, q, e], ends[:, e, bass.ds(c * CT, CT)], 1.0, None, ALU.mult))
                            ch.add(nc.vector.tensor_scalar(node[:, q], ends[:, 0, bass.ds(c * CT, CT)], 1.0, None, ALU.mult))
                        ch.settle()
                        dve.sem_inc(indexed, 1)
                        if edge_rows is not None:
                            for t in range(CT):
                                s = t % 8
                                gathered[s].wait(dve, c * PER + (t // 8 + 1) * 32)
                                ch.add(nc.vector.tensor_tensor(prod[:, t % 2, :], far[:, s, 0:D], edge[:, q, t, 0:D], ALU.add))
                                ch.settle()
                                ch.add(nc.vector.tensor_tensor(prod[:, t % 2, :], prod[:, t % 2, :], near[:, s, :], ALU.mult))
                                ch.add(nc.vector.tensor_tensor(edge[:, q, t, 0:D], far[:, s, D:2 * D], edge[:, q, t, 0:D], ALU.add))
                                ch.settle()
                                dve.sem_inc(ring_free, 1)
                                ch.add(nc.vector.tensor_reduce(alpha[:, t, :], heads(prod[:, t % 2, :]), AX, ALU.add))
                            ch.settle()
                        else:
                            gathered[q].wait(dve, (i + 1) * 2 * CT * 16)
                            ch.link(nc.vector.tensor_tensor(raw[:], far[:, q * CT:(q + 1) * CT, D:SW], near[:, q * CT:(q + 1) * CT, :], ALU.add))
                            ch.link(nc.vector.scalar_tensor_tensor(alpha[:], raw[:], 0.2, raw[:], ALU.mult, ALU.max))
                        ch.link(nc.vector.tensor_scalar(raw[:], node[:, q].unsqueeze(2).broadcast_to([P, CT, HEADS]), 1.0, None, ALU.mult))
                        dve.sem_inc(alpha_ready, 1)
                        dve.wait_ge(node_copied, c + 1)
                        ch.link(nc.vector.tensor_tensor(fresh[:, 1:P], node_t[:, 1:P], node_t[:, 0:P - 1], ALU.not_equal))
                        ch.link(nc.vector.tensor_scalar(fresh[:, 1:P], fresh[:, 1:P], -BIG, None, ALU.mult))
                        ch.link(nc.vector.tensor_tensor_scan(up[:], fresh[:, 0:P], ps[:, SCORES, 0:P], -BIG, ALU.add, ALU.max))
                        ch.link(nc.vector.tensor_tensor_scan(down[:, ::-1], fresh[:, 1:P + 1][:, ::-1], up[:, ::-1], -BIG, ALU.add, ALU.max))
                        dve.sem_inc(top_ready, 1)
                        dve.wait_ge(top_turned, c + 1)
                        dve.wait_ge(stored[q], i * 16)
                        tops = ps[:, TOPS, 0:P].rearrange("p (t h) -> p t h", h=HEADS)
                        ch.link(nc.vector.tensor_tensor(raw[:], alpha[:], tops, ALU.subtract))
                        dve.sem_inc(centred, 1)
                        ch.add(nc.vector.tensor_copy(out[:, q, :, SEG:SEG + HEADS], tops))
                        ch.add(nc.vector.tensor_copy(out[:, q, :, ROW - 1], node[:, q]))
                        dve.wait_ge(weighed, c + 1)
                        for t in range(CT):
                            n = c * CT + t
                            if t % 4 == 0:
                                dve.wait_ge(keys_turned, c * 4 + t // 4 + 1)
                            if t >= 2:
                                dve.wait_ge(summed, n - 1)
                            else:
                                dve.wait_ge(summed, c * CT)
                            value = edge[:, q, t, 0:D] if edge_rows is not None else far[:, q * CT + t, 0:D]
                            ch.add(nc.vector.tensor_tensor(heads(msg[:, t % 2, 0:D]), heads(value), weight[:, t, :].unsqueeze(2).broadcast_to([P, HEADS, HD]), ALU.mult))
                            ch.add(nc.vector.tensor_copy(msg[:, t % 2, D:SEG], weight[:, t, :]))
                            nc.vector.scalar_tensor_tensor(same[:, t % 2, :], ps[:, KEYS[(t // 4) % 2], (t % 4) * P:(t % 4 + 1) * P], node[:, q, t:t + 1],
                                                           core.c("le"), ALU.is_equal, ALU.mult).then_inc(msg_ready, 1)
                        ch.settle()
                        dve.wait_ge(msg_ready, (c + 1) * CT)
                        dve.sem_inc(chunk_free, 1)


def filter_stage(core, name, edge_rows, table, wf1, bf1, wf2, bf2, partial):
    NG = wf1.shape[0]
    with Stage(core, name) as st:
        nc, ps = core.nc, core.ps
        w1_sb, b1_sb, w2_sb, b2_sb = st.sb("w1", [NG, D]), st.sb("b1", [P, KD]), st.sb("w2", [P, KD, D]), st.sb("b2", [P, D])
        edge = st.sb("edge", [P, 2, CT, NG + 2])
        far = st.sb("far", [P, 2, CT, D])
        index = st.sb("index", [P, 2, CT], I32)
        rbf_t = st.sb("rbf_t", [NG, 2, 4 * P])
        hid = st.sb("hid", [P, 2, KD, 4 * P])
        filt = st.sb("filt", [P, 2, D])
        same = st.sb("same", [P, 2, P])
        msg = st.sb("msg", [P, 2, D])
        out = st.sb("out", [P, 2, CT, D + 1])
        loaded = st.sem("loaded")
        edge_loaded = [st.sem("edge_loaded0"), st.sem("edge_loaded1")]
        gathered = [st.moved(q, CHUNKS // 2 * CT) for q in range(2)]
        stored = [st.sem("stored0"), st.sem("stored1")]
        names = ("chain", "indexed", "rbf_turned", "rbf_copied", "hid_ready", "hid_done", "keys_turned", "filtered", "msg_ready", "summed", "copied", "chunk_free", "pool_passed")
        chain, indexed, rbf_turned, rbf_copied, hid_ready, hid_done, keys_turned, filtered, msg_ready, summed, copied, chunk_free, pool_passed = map(st.sem, names)
        RBF, HIDB, KEYS, FILT, SUMS = 0, (1, 2), 3, (4, 5), (6, 7)
        with st.block() as block:
            @block.sync
            def _(sp):
                for to, of in ((w1_sb, wf1), (b1_sb, bf1), (w2_sb, rows(wf2)), (b2_sb, bcast(bf2))):
                    sp.dma_start(to[:], of).then_inc(loaded, 16)
                with sp.Fori(0, CHUNKS // 2) as i:
                    for q in range(2):
                        c = i * 2 + q
                        sp.wait_ge(chunk_free, c + 1)
                        sp.dma_start(edge[:, q], edge_rows[bass.ds(c * CHUNK, CHUNK), :].rearrange("(t p) d -> p t d", p=P)).then_inc(edge_loaded[q], 16)

            @block.gpsimd
            def _(pool):
                with pool.Fori(0, CHUNKS // 2) as i:
                    for q in range(2):
                        c = i * 2 + q
                        pool.wait_ge(indexed, c + 1)
                        pool.wait_ge(chunk_free, c + 1)
                        pool.sem_inc(pool_passed, 1)
                        for t in range(CT):
                            gathered[q].count(nc.gpsimd.indirect_dma_start(out=far[:, q, t, :], out_offset=None, in_=table,
                                                         in_offset=bass.IndirectOffsetOnAxis(ap=index[:, q, t:t + 1], axis=0),
                                                         bounds_check=NPAD - 1, oob_is_err=False))

            @block.tensor
            def _(pe):
                ident = core.c("ident")
                pe.wait_ge(loaded, 64)
                with pe.Fori(0, CHUNKS // 2) as i:
                    for q in range(2):
                        c = i * 2 + q
                        pe.wait_ge(edge_loaded[q], (i + 1) * 16)
                        for b in range(4):
                            m4 = c * 4 + b
                            pe.wait_ge(rbf_copied, m4)
                            for u in range(4):
                                last = nc.tensor.transpose(ps[0:NG, RBF, u * P:(u + 1) * P], edge[:, q, b * 4 + u, 0:NG], ident)
                            last.then_inc(rbf_turned, 1)
                            pe.wait_ge(rbf_copied, m4 + 1)
                            for m in range(KD):
                                pe.wait_ge(hid_done, m4 * 2)
                                nc.tensor.matmul(ps[:, HIDB[m], :], w1_sb[:, m * P:(m + 1) * P], rbf_t[:, b % 2, :], start=True, stop=True).then_inc(hid_ready, 1)
                            pe.wait_ge(msg_ready, m4 * 4)
                            for u in range(4):
                                last = nc.tensor.transpose(ps[:, KEYS, u * P:(u + 1) * P], edge[:, q, b * 4 + u, NG:NG + 1].broadcast_to([P, P]), ident)
                            last.then_inc(keys_turned, 1)
                            pe.wait_ge(hid_done, m4 * 2 + 2)

                            def total(t):
                                n = c * CT + t
                                pe.wait_ge(msg_ready, n + 1)
                                pe.wait_ge(copied, n + 1)
                                nc.tensor.matmul(ps[:, SUMS[t % 2], 0:D], same[:, t % 2, :], msg[:, t % 2, :], start=True, stop=True).then_inc(summed, 1)

                            for u in range(4):
                                t = b * 4 + u
                                n = c * CT + t
                                if u >= 2:
                                    pe.wait_ge(msg_ready, n - 1)
                                for k in range(KD):
                                    last = nc.tensor.matmul(ps[:, FILT[u % 2], 0:D], hid[:, b % 2, k, u * P:(u + 1) * P], w2_sb[:, k, :], start=(k == 0), stop=(k == KD - 1))
                                last.then_inc(filtered, 1)
                                if u >= 1:
                                    total(t - 1)
                            total(b * 4 + 3)

            @block.scalar
            def _(act):
                act.sem_inc(copied, 2)
                act.wait_ge(loaded, 64)
                with act.Fori(0, CHUNKS // 2) as i:
                    for q in range(2):
                        c = i * 2 + q
                        for b in range(4):
                            m4 = c * 4 + b
                            act.wait_ge(rbf_turned, m4 + 1)
                            nc.scalar.copy(rbf_t[:, b % 2, :], ps[0:NG, RBF, :]).then_inc(rbf_copied, 1)
                            for m in range(KD):
                                act.wait_ge(hid_ready, m4 * 2 + m + 1)
                                nc.scalar.activation(hid[:, b % 2, m, :], ps[:, HIDB[m], :], ACT.Silu, bias=b1_sb[:, m:m + 1]).then_inc(hid_done, 1)
                            if b == 0:
                                act.wait_ge(stored[q], i * 16)
                            for u in range(4):
                                t = b * 4 + u
                                act.wait_ge(summed, c * CT + t + 1)
                                nc.scalar.copy(out[:, q, t, 0:D], ps[:, SUMS[t % 2], 0:D]).then_inc(copied, 1)
                        act.wait_ge(copied, (c + 1) * CT + 2)
                        act.dma_start(partial[bass.ds(c * CHUNK, CHUNK), :].rearrange("(t p) d -> p t d", p=P), out[:, q]).then_inc(stored[q], 16)
                for q in range(2):
                    act.wait_ge(stored[q], (CHUNKS // 2) * 16)

            @block.vector
            def _(dve):
                ch = Chain(dve, chain)
                dve.wait_ge(loaded, 64)
                dve.sem_inc(chunk_free, 2)
                with ch.loop(CHUNKS // 2, 2 * (2 + 3 * CT)) as i:
                    for q in range(2):
                        c = i * 2 + q
                        dve.wait_ge(edge_loaded[q], (i + 1) * 16)
                        dve.wait_ge(stored[q], i * 16)
                        ch.add(nc.vector.tensor_copy(index[:, q], edge[:, q, :, NG + 1]))
                        ch.add(nc.vector.tensor_copy(out[:, q, :, D], edge[:, q, :, NG]))
                        ch.settle()
                        dve.sem_inc(indexed, 1)
                        gathered[q].wait(dve, (i + 1) * CT * 16)
                        for t in range(CT):
                            n = c * CT + t
                            dve.wait_ge(filtered, n + 1)
                            ch.add(nc.vector.tensor_tensor(filt[:, t % 2, :], ps[:, FILT[t % 2], 0:D], b2_sb[:], ALU.add))
                            if t % 4 == 0:
                                dve.wait_ge(keys_turned, c * 4 + t // 4 + 1)
                            if t >= 2:
                                dve.wait_ge(summed, n - 1)
                            else:
                                dve.wait_ge(summed, c * CT)
                            ch.add(nc.vector.scalar_tensor_tensor(same[:, t % 2, :], ps[:, KEYS, (t % 4) * P:(t % 4 + 1) * P], edge[:, q, t, NG:NG + 1],
                                                                  core.c("le"), ALU.is_equal, ALU.mult))
                            ch.settle()
                            ch.link(nc.vector.tensor_tensor(msg[:, t % 2, :], filt[:, t % 2, :], far[:, q, t, :], ALU.mult))
                            dve.sem_inc(msg_ready, 1)
                        dve.sem_inc(chunk_free, 1)


def carry_stage(core, name, partial, carry, sums, tops, scale):
    W = sums + tops
    with Stage(core, name) as st:
        nc, ps = core.nc, core.ps
        part = st.sb("part", [QT, 4, W + 1])
        last_node = st.sb("last_node", [QT, 4])
        node_row = st.sb("node_row", [P, ETILES])
        reach = st.sb("reach", [QT, 4, 4, QT])
        out = st.sb("out", [QT, 4, W])
        loaded, chain, nodes_ready, turned, row_copied, reach_ready, summed, done, stored = (
            st.sem(x) for x in ("loaded", "chain", "nodes_ready", "turned", "row_copied", "reach_ready", "summed", "done", "stored"))
        if tops:
            fresh = st.sb("fresh", [HEADS, ETILES + 1])
            up, down = st.sb("up", [HEADS, ETILES]), st.sb("down", [HEADS, ETILES])
            factor = st.sb("factor", [QT, 4, HEADS])
            top_ready, top_turned, centred, expd = (st.sem(x) for x in ("top_ready", "top_turned", "centred", "expd"))
        ident = core.c("ident")
        with st.block() as block:
            @block.sync
            def _(sp):
                sp.dma_start(part[:], partial.rearrange("(q p r) w -> p q r w", q=4, r=P)[:, :, P - 1, :]).then_inc(loaded, 16)
                sp.wait_ge(done, 1)
                sp.dma_start(carry.rearrange("(q p) w -> p q w", q=4), out[:]).then_inc(stored, 16)
                sp.wait_ge(stored, 16)

            @block.tensor
            def _(pe):
                pe.wait_ge(nodes_ready, 1)
                for q in range(4):
                    last = nc.tensor.transpose(ps[:, 0, q * QT:(q + 1) * QT], last_node[:, q:q + 1].broadcast_to([QT, P]), ident[0:QT, 0:QT])
                if tops:
                    for q in range(4):
                        last = nc.tensor.transpose(ps[0:HEADS, 1, q * QT:(q + 1) * QT], part[:, q, sums:W], ident[0:QT, 0:QT])
                last.then_inc(turned, 1)
                if tops:
                    pe.wait_ge(top_ready, 1)
                    for q in range(4):
                        last = nc.tensor.transpose(ps[0:QT, 2, q * HEADS:(q + 1) * HEADS], down[:, q * QT:(q + 1) * QT], ident[0:HEADS, 0:HEADS])
                    last.then_inc(top_turned, 1)
                pe.wait_ge(reach_ready, 1)
                for qo in range(4):
                    for qi in range(qo + 1):
                        last = nc.tensor.matmul(ps[0:QT, 3 + qo, 0:sums], reach[:, qi, qo, :], part[:, qi, 0:sums], start=(qi == 0), stop=(qi == qo))
                last.then_inc(summed, 1)

            @block.scalar
            def _(act):
                if tops:
                    act.wait_ge(centred, 1)
                    nc.scalar.activation(factor[:], factor[:], ACT.Exp, scale=scale).then_inc(expd, 1)

            @block.vector
            def _(dve):
                ch = Chain(dve, chain)
                dve.wait_ge(loaded, 16)
                ch.link(nc.vector.tensor_copy(last_node[:], part[:, :, W]))
                dve.sem_inc(nodes_ready, 1)
                dve.wait_ge(turned, 1)
                ch.link(nc.vector.tensor_copy(node_row[:], ps[:, 0, 0:ETILES]))
                if tops:
                    ch.link(nc.vector.memset(fresh[:], 0.0))
                    ch.link(nc.vector.tensor_tensor(fresh[:, 1:ETILES], node_row[0:HEADS, 1:], node_row[0:HEADS, 0:ETILES - 1], ALU.not_equal))
                    ch.link(nc.vector.tensor_scalar(fresh[:, 1:ETILES], fresh[:, 1:ETILES], -BIG, None, ALU.mult))
                    ch.link(nc.vector.tensor_tensor_scan(up[:], fresh[:, 0:ETILES], ps[0:HEADS, 1, 0:ETILES], -BIG, ALU.add, ALU.max))
                    ch.link(nc.vector.tensor_tensor_scan(down[:, ::-1], fresh[:, 1:][:, ::-1], up[:, ::-1], -BIG, ALU.add, ALU.max))
                    dve.sem_inc(top_ready, 1)
                    dve.wait_ge(top_turned, 1)
                    both = ps[0:QT, 2, 0:4 * HEADS].rearrange("p (q h) -> p q h", q=4)
                    ch.link(nc.vector.tensor_tensor(factor[:], part[:, :, sums:W], both, ALU.subtract))
                    dve.sem_inc(centred, 1)
                    ch.link(nc.vector.tensor_copy(out[:, :, sums:W], both))
                    dve.wait_ge(expd, 1)
                    for q in range(4):
                        v = part[:, q, 0:D].rearrange("p (h c) -> p h c", h=HEADS)
                        ch.add(nc.vector.tensor_tensor(v, v, factor[:, q].unsqueeze(2).broadcast_to([QT, HEADS, HD]), ALU.mult))
                    ch.link(nc.vector.tensor_tensor(part[:, :, D:sums], part[:, :, D:sums], factor[:], ALU.mult))
                for qo in range(4):
                    for qi in range(qo + 1):
                        to, row, own = reach[:, qi, qo, :], node_row[0:QT, qo * QT:(qo + 1) * QT], last_node[:, qi:qi + 1]
                        if qi == qo:
                            ch.add(nc.vector.scalar_tensor_tensor(to, row, own, core.c("le")[0:QT, 0:QT], ALU.is_equal, ALU.mult))
                        else:
                            ch.add(nc.vector.tensor_scalar(to, row, own, None, ALU.is_equal))
                ch.settle()
                dve.sem_inc(reach_ready, 1)
                dve.wait_ge(summed, 1)
                ch.link(nc.vector.tensor_copy(out[:, :, 0:sums], ps[0:QT, 3:7, 0:sums]))
                dve.sem_inc(done, 1)


def node_stage(core, name, s, base, count, partial, carry, sums, tops, scale, agg=None, bias=None, self_rows=None):
    W = sums + tops
    with Stage(core, name) as st:
        nc, x = core.nc, core.x
        end, spans, tile = st.sb("end", [P, TILES]), st.sb("spans", [P, TILES]), st.sb("tile", [P, TILES])
        end_i, tile_i, carry_i = st.sb("end_i", [P, TILES], I32), st.sb("tile_i", [P, TILES], I32), st.sb("carry_i", [P, TILES], I32)
        own = st.sb("own", [P, TILES, W + 1])
        far = st.sb("far", [P, TILES, W])
        f = st.sb("f", [P, 6, TILES, HEADS])
        if self_rows is not None:
            own_value, own_score = st.sb("own_value", [P, TILES, SEG]), st.sb("own_score", [P, TILES, HEADS])
        PARTS = 3 if self_rows is not None else 2
        loaded, chain, indexed, centred, expd = (st.sem(x) for x in ("loaded", "chain", "indexed", "centred", "expd"))
        gathered = st.moved(0, 2 * TILES)
        if bias is not None:
            bias_sb = st.sb("bias", [P, D])
        with st.block() as block:
            @block.sync
            def _(sp):
                if bias is not None:
                    sp.dma_start(bias_sb[:], bcast(bias)).then_inc(loaded, 16)
                if self_rows is not None:
                    for to, of in zip((own_value, own_score), self_rows):
                        sp.dma_start(to[:], of.rearrange("(a p) d -> p a d", p=P)).then_inc(loaded, 16)

            @block.gpsimd
            def _(pool):
                pool.wait_ge(indexed, 1)
                for a in range(TILES):
                    for to, table, index in ((own, partial, end_i), (far, carry, carry_i)):
                        gathered.count(nc.gpsimd.indirect_dma_start(out=to[:, a, :], out_offset=None, in_=table,
                                                     in_offset=bass.IndirectOffsetOnAxis(ap=index[:, a:a + 1], axis=0),
                                                     bounds_check=table.shape[0] - 1, oob_is_err=False))

            @block.scalar
            def _(act):
                if tops:
                    act.wait_ge(centred, 1)
                    nc.scalar.activation(f[:, 1:1 + PARTS], f[:, 1:1 + PARTS], ACT.Exp, scale=scale).then_inc(expd, 1)

            @block.vector
            def _(dve):
                ch = Chain(dve, chain)
                b, n = base[:, s], count[:, s]
                bh = lambda v: v.unsqueeze(2).broadcast_to([P, TILES, HEADS])
                ch.link(nc.vector.scalar_tensor_tensor(end[:], b, -1.0, n, ALU.add, ALU.add))
                ch.link(nc.vector.tensor_scalar(end[:], end[:], 0.0, None, ALU.max))
                ch.link(nc.vector.tensor_copy(end_i[:], end[:]))
                ch.link(nc.vector.tensor_scalar(tile_i[:], end_i[:], 7, None, ALU.logical_shift_right))
                ch.link(nc.vector.tensor_copy(tile[:], tile_i[:]))
                ch.link(nc.vector.scalar_tensor_tensor(spans[:], tile[:], float(P), b, ALU.mult, ALU.is_gt))
                ch.link(nc.vector.tensor_scalar(tile[:], tile[:], 1.0, 0.0, ALU.subtract, ALU.max))
                ch.link(nc.vector.tensor_copy(carry_i[:], tile[:]))
                dve.sem_inc(indexed, 1)
                ch.link(nc.vector.tensor_scalar(end[:], n, 0.0, None, ALU.is_gt))
                gathered.wait(dve, 2 * TILES * 16)
                if bias is not None:
                    dve.wait_ge(loaded, 48 if self_rows is not None else 16)
                if tops:
                    mine, its = own[:, :, sums:W], far[:, :, sums:W]
                    ch.link(nc.vector.tensor_tensor(f[:, 0], its, bh(spans[:]), ALU.mult))
                    ch.link(nc.vector.tensor_scalar(tile[:], spans[:], 1.0, BIG, ALU.subtract, ALU.mult))
                    ch.link(nc.vector.tensor_tensor(f[:, 0], f[:, 0], bh(tile[:]), ALU.add))
                    if self_rows is not None:
                        ch.link(nc.vector.tensor_tensor(mine, mine, bh(end[:]), ALU.mult))
                        ch.link(nc.vector.tensor_scalar(tile[:], end[:], 1.0, BIG, ALU.subtract, ALU.mult))
                        ch.link(nc.vector.tensor_tensor(mine, mine, bh(tile[:]), ALU.add))
                        ch.link(nc.vector.tensor_tensor(f[:, 5], own_value[:, :, D:SEG], own_score[:], ALU.add))
                        ch.link(nc.vector.scalar_tensor_tensor(f[:, 3], f[:, 5], 0.2, f[:, 5], ALU.mult, ALU.max))
                    ch.link(nc.vector.tensor_tensor(f[:, 4], f[:, 0], mine, ALU.max))
                    if self_rows is not None:
                        ch.link(nc.vector.tensor_tensor(f[:, 4], f[:, 4], f[:, 3], ALU.max))
                        ch.link(nc.vector.tensor_tensor(f[:, 3], f[:, 3], f[:, 4], ALU.subtract))
                    ch.link(nc.vector.tensor_tensor(f[:, 1], mine, f[:, 4], ALU.subtract))
                    ch.link(nc.vector.tensor_tensor(f[:, 2], f[:, 0], f[:, 4], ALU.subtract))
                    dve.sem_inc(centred, 1)
                    dve.wait_ge(expd, 1)
                    ch.link(nc.vector.tensor_tensor(f[:, 4], own[:, :, D:sums], f[:, 1], ALU.mult))
                    ch.link(nc.vector.tensor_tensor(f[:, 5], far[:, :, D:sums], f[:, 2], ALU.mult))
                    ch.link(nc.vector.tensor_tensor(f[:, 4], f[:, 4], f[:, 5], ALU.add))
                    if self_rows is not None:
                        ch.link(nc.vector.tensor_tensor(f[:, 4], f[:, 4], f[:, 3], ALU.add))
                    ch.link(nc.vector.reciprocal(f[:, 4], f[:, 4]))
                    if self_rows is None:
                        ch.link(nc.vector.tensor_tensor(f[:, 4], f[:, 4], bh(end[:]), ALU.mult))
                    for k in range(1, 1 + PARTS):
                        ch.link(nc.vector.tensor_tensor(f[:, k], f[:, k], f[:, 4], ALU.mult))
                    parts = [(1, own), (2, far)] + ([(3, own_value)] if self_rows is not None else [])
                    with ch.loop(GROUPS, 2 * PARTS * GROUP) as g:
                        for k, rows_ in parts:
                            for j in range(GROUP):
                                v = rows_[:, bass.ds(g * GROUP + j, 1), 0:D].rearrange("p a (h c) -> p (a h) c", h=HEADS)
                                w = f[:, k, bass.ds(g * GROUP + j, 1), :].rearrange("p a h -> p (a h)").unsqueeze(2).broadcast_to([P, HEADS, HD])
                                ch.add(nc.vector.tensor_tensor(v, v, w, ALU.mult))
                        ch.settle()
                        for k, rows_ in parts[1:]:
                            for j in range(GROUP):
                                at = bass.ds(g * GROUP + j, 1)
                                ch.add(nc.vector.tensor_tensor(own[:, at, 0:D], own[:, at, 0:D], rows_[:, at, 0:D], ALU.add))
                            ch.settle()
                        for j in range(GROUP):
                            at = bass.ds(g * GROUP + j, 1)
                            if agg is None:
                                ch.add(nc.vector.tensor_tensor(x[:, at, :], x[:, at, :], own[:, at, 0:D], ALU.add))
                            else:
                                ch.add(nc.vector.tensor_tensor(agg[:, at, :], own[:, at, 0:D], bias_sb[:].unsqueeze(1), ALU.add))
                        ch.settle()
                else:
                    with ch.loop(TILES, 2) as a:
                        at = bass.ds(a, 1)
                        v, w = own[:, at, 0:D].rearrange("p a d -> p (a d)"), far[:, at, 0:D].rearrange("p a d -> p (a d)")
                        ch.link(nc.vector.tensor_scalar(v, v, end[:, at], None, ALU.mult))
                        ch.link(nc.vector.scalar_tensor_tensor(agg[:, at, :].rearrange("p a d -> p (a d)"), w, spans[:, at], v, ALU.mult, ALU.add))


def turn(core, pe, act_free, turned, src):
    for a in range(TILES):
        pe.wait_ge(act_free, a + 1)
        for k in range(KD):
            last = core.nc.tensor.transpose(core.ps[:, a % GROUP, k * P:(k + 1) * P], src[:, a, k * P:(k + 1) * P], core.c("ident"))
        last.then_inc(turned, 1)


def update_stage(core, agg, ht, wu1, bu1, wu2, bu2):
    with Stage(core, "up") as st:
        nc, ps = core.nc, core.ps
        w_sb, b_sb = st.sb("w", [P, 2, KD, D]), st.sb("b", [P, 2, KD])
        hid = st.sb("hid", [P, KD, HALF])
        loaded, turned, bank_free, ready, done = (st.sem(s) for s in ("loaded", "turned", "bank_free", "ready", "done"))
        BLOCKS = NPAD // HALF
        with st.block() as block:
            @block.sync
            def _(sp):
                for to, of in ((w_sb[:, 0], rows(wu1)), (w_sb[:, 1], rows(wu2)), (b_sb[:, 0], bu1), (b_sb[:, 1], bu2)):
                    sp.dma_start(to, of).then_inc(loaded, 16)

            @block.tensor
            def _(pe):
                turn(core, pe, bank_free, turned, agg)
                pe.wait_ge(loaded, 64)
                pe.wait_ge(bank_free, TILES + GROUP)
                with pe.Fori(0, BLOCKS) as g:
                    for layer in range(2):
                        for m in range(KD):
                            n = layer * KD + m
                            pe.wait_ge(done, g * 4 + (KD if layer else 0))
                            for k in range(KD):
                                src = ht[:, k, bass.ds(g * HALF, HALF)] if layer == 0 else hid[:, k, :]
                                last = nc.tensor.matmul(ps[:, n, 0:HALF], w_sb[:, layer, k, m * P:(m + 1) * P], src, start=(k == 0), stop=(k == KD - 1))
                            last.then_inc(ready, 1)

            @block.scalar
            def _(act):
                act.sem_inc(bank_free, GROUP)
                for a in range(TILES):
                    act.wait_ge(turned, a + 1)
                    nc.scalar.copy(ht[:, :, a * P:(a + 1) * P], ps[:, a % GROUP, 0:D].rearrange("p (k t) -> p k t", k=KD)).then_inc(bank_free, 1)
                act.wait_ge(loaded, 64)
                with act.Fori(0, BLOCKS) as g:
                    for m in range(KD):
                        act.wait_ge(ready, g * 4 + m + 1)
                        nc.scalar.activation(hid[:, m, :], ps[:, m, 0:HALF], ACT.Silu, bias=b_sb[:, 0, m:m + 1]).then_inc(done, 1)
                    for m in range(KD):
                        act.wait_ge(ready, g * 4 + KD + KD)
                        nc.scalar.activation(ht[:, m, bass.ds(g * HALF, HALF)], ps[:, KD + m, 0:HALF], ACT.Identity, bias=b_sb[:, 1, m:m + 1]).then_inc(done, 1)


def batchnorm_stage(core, name, ht, agg, gamma, beta):
    SPLIT = [(k, min(512, N - k)) for k in range(0, N, 512)]
    with Stage(core, name) as st:
        nc, ps, x, xn = core.nc, core.ps, core.x, core.xn
        gb = st.sb("gb", [P, 2, KD])
        stats = st.sb("stats", [P, KD, len(SPLIT), 6])
        mv = st.sb("mv", [P, KD, 2])
        std = st.sb("std", [P, KD])
        lines = st.sb("lines", [P, 2, D])
        scratch = st.sb("scratch", [P, 2, D])
        loaded, chain, turned, bank_free, var_ready, std_ready, coef_ready, spread, values, added, copied = (
            st.sem(s) for s in ("loaded", "chain", "turned", "bank_free", "var_ready", "std_ready", "coef_ready", "spread", "values", "added", "copied"))
        with st.block() as block:
            @block.sync
            def _(sp):
                sp.dma_start(gb[:, 0], gamma).then_inc(loaded, 16)
                sp.dma_start(gb[:, 1], beta).then_inc(loaded, 16)

            @block.tensor
            def _(pe):
                if agg is not None:
                    turn(core, pe, bank_free, turned, agg)
                pe.wait_ge(coef_ready, 1)
                for i in range(2):
                    for k in range(KD):
                        last = nc.tensor.transpose(ps[:, 5 + i, k * P:(k + 1) * P], gb[:, i, k:k + 1].broadcast_to([P, P]), core.c("ident"))
                last.then_inc(spread, 1)
                if agg is None:
                    for a in range(TILES):
                        pe.wait_ge(added, a + 1)
                        for k in range(KD):
                            last = nc.tensor.transpose(ps[:, a % 4, k * P:(k + 1) * P], ht[:, k, a * P:(a + 1) * P], core.c("ident"))
                        last.then_inc(values, 1)

            @block.scalar
            def _(act):
                if agg is not None:
                    act.sem_inc(bank_free, GROUP)
                    for a in range(TILES):
                        act.wait_ge(turned, a + 1)
                        nc.scalar.copy(ht[:, :, a * P:(a + 1) * P], ps[:, a % GROUP, 0:D].rearrange("p (k t) -> p k t", k=KD)).then_inc(bank_free, 1)
                act.wait_ge(var_ready, 1)
                nc.scalar.activation(std[:], std[:], ACT.Sqrt).then_inc(std_ready, 1)

            @block.vector
            def _(dve):
                ch = Chain(dve, chain)
                dve.wait_ge(loaded, 32)
                if agg is None:
                    dve.sem_inc(added, 4)
                else:
                    dve.wait_ge(bank_free, TILES + GROUP)
                for k in range(KD):
                    for b, (at, w) in enumerate(SPLIT):
                        ch.add(nc.vector.bn_stats(stats[:, k, b, :], ht[:, k, at:at + w]))
                ch.settle()
                for k in range(KD):
                    ch.add(nc.vector.bn_aggr(mv[:, k, :], stats[:, k].rearrange("p b s -> p (b s)")))
                ch.settle()
                ch.link(nc.vector.tensor_scalar_add(std[:], mv[:, :, 1], 1e-5))
                dve.sem_inc(var_ready, 1)
                dve.wait_ge(std_ready, 1)
                ch.link(nc.vector.reciprocal(std[:], std[:]))
                ch.link(nc.vector.tensor_tensor(gb[:, 0], gb[:, 0], std[:], ALU.mult))
                ch.link(nc.vector.tensor_tensor(std[:], mv[:, :, 0], gb[:, 0], ALU.mult))
                ch.link(nc.vector.tensor_tensor(gb[:, 1], gb[:, 1], std[:], ALU.subtract))
                dve.sem_inc(coef_ready, 1)
                dve.wait_ge(spread, 1)
                ch.link(nc.vector.tensor_copy(lines[:], ps[:, 5:7, 0:D]))
                for a in range(TILES):
                    if agg is None:
                        dve.wait_ge(values, a + 1)
                        v = ps[:, a % 4, 0:D]
                    else:
                        v = agg[:, a, :]
                    ch.add(nc.vector.tensor_tensor(xn[:, a, :], xn[:, a, :], lines[:, 1, :], ALU.add))
                    ch.link(nc.vector.tensor_tensor(scratch[:, a % 2, :], v, lines[:, 0, :], ALU.mult))
                    if agg is None:
                        dve.sem_inc(added, 1)
                    ch.add(nc.vector.tensor_tensor(x[:, a, :], x[:, a, :], xn[:, a, :], ALU.add))
                    ch.settle()
                    ch.link(nc.vector.tensor_tensor(x[:, a, :], x[:, a, :], scratch[:, a % 2, :], ALU.add))


def store_rows_stage(core, name, rows_sb, table):
    with Stage(core, name) as st:
        stored = st.sem("stored")
        with st.block() as block:
            @block.sync
            def _(sp):
                sp.dma_start(table.rearrange("(a p) d -> p a d", p=P), rows_sb[:]).then_inc(stored, 16)
                sp.wait_ge(stored, 16)


def project3_stage(core, xt, weight, att_src, att_dst, src_table, dst_table):
    with Stage(core, "p3") as st:
        nc, ps = core.nc, core.ps
        w_sb, av = st.sb("w", [P, KD, D]), st.sb("av", [P, 2, D])
        out = st.sb("out", [P, TILES, SEG])
        near = st.sb("near", [P, TILES, HEADS])
        prod = st.sb("prod", [P, 2, D])
        loaded, chain, projected, bank_free, copied, stored = (st.sem(s) for s in ("loaded", "chain", "projected", "bank_free", "copied", "stored"))
        with st.block() as block:
            @block.sync
            def _(sp):
                for to, of in ((w_sb[:], rows(weight)), (av[:, 0], bcast(att_src)), (av[:, 1], bcast(att_dst))):
                    sp.dma_start(to, of).then_inc(loaded, 16)
                sp.wait_ge(bank_free, TILES + GROUP)
                sp.dma_start(src_table.rearrange("(a p) d -> p a d", p=P), out[:]).then_inc(stored, 16)
                sp.dma_start(dst_table.rearrange("(a p) d -> p a d", p=P), near[:]).then_inc(stored, 16)
                sp.wait_ge(stored, 32)

            @block.tensor
            def _(pe):
                pe.sem_inc(bank_free, GROUP)
                pe.wait_ge(loaded, 48)
                for a in range(TILES):
                    pe.wait_ge(bank_free, a + 1)
                    for k in range(KD):
                        last = nc.tensor.matmul(ps[:, a % GROUP, 0:D], xt[:, k, a * P:(a + 1) * P], w_sb[:, k, :], start=(k == 0), stop=(k == KD - 1))
                    last.then_inc(projected, 1)

            @block.scalar
            def _(act):
                for a in range(TILES):
                    act.wait_ge(projected, a + 1)
                    nc.scalar.copy(out[:, a, 0:D], ps[:, a % GROUP, 0:D]).then_inc(copied, 1)

            @block.vector
            def _(dve):
                ch = Chain(dve, chain)
                dve.wait_ge(loaded, 48)
                for a in range(TILES):
                    dve.wait_ge(copied, a + 1)
                    for s in range(2):
                        ch.add(nc.vector.tensor_tensor(prod[:, s, :], ps[:, a % GROUP, 0:D], av[:, s, :], ALU.mult))
                    ch.settle()
                    for s, to in ((0, out[:, a, D:SEG]), (1, near[:, a, :])):
                        ch.add(nc.vector.tensor_reduce(to, prod[:, s, :].rearrange("p (h c) -> p h c", h=HEADS), AX, ALU.add))
                    ch.settle()
                    dve.sem_inc(bank_free, 1)


def gnn_ffn_kernel(nc, a, out):
    dram = lambda name, shape: nc.dram_tensor(name, shape, F32, kind="Internal").ap()
    inv = float(HD) ** -0.5
    with ExitStack() as ctx:
        core = Core(nc, ctx)

        def sb(name, shape, to=ctx):
            return to.enter_context(nc.sbuf_tensor(name, shape, F32))

        base, count, ends = sb("base", [P, 2, TILES]), sb("count", [P, 2, TILES]), sb("ends", [P, 2, ETILES])
        by_dst, by_src = dram("by_dst", (EPAD, D + 2)), dram("by_src", (EPAD, a["edge_attr_20"].shape[1] + 2))
        partial, carry = dram("partial", (EPAD, ROW)), dram("carry", (ETILES, ROW - 1))
        partial_f, carry_f = dram("partial_f", (EPAD, D + 1)), dram("carry_f", (ETILES, D))
        load_stage(core, a["x"], a["consts"])

        with ExitStack() as own:
            split = sb("split", [P, 2, 3, ETILES], own)
            count_stage(core, (a["dst"], a["src"]), split, base, count)
            sort_stage(core, "by_dst", 0, split, base, a["edge_attr_256"], D, by_dst, a["L1_gnn_We"])
            sort_stage(core, "by_src", 1, split, base, a["edge_attr_20"], a["edge_attr_20"].shape[1], by_src)

        with ExitStack() as own:
            xt = sb("xt0", [P, KD, NPAD], own)
            norm_stage(core, "n0", xt)
            l0_gnn_stage(core, xt, a["src"], a["dst"], a["L0_gnn_weight"], a["L0_gnn_attn_l"], a["L0_gnn_attn_r"],
                         dram("xt_table", (NPAD, D)), dram("al_table", (NPAD, 8)))
            norm_stage(core, "n1", xt)
            l0_ffn_stage(core, xt, *(a[f"L0_ffn_{k}"] for k in ("wr", "br", "w1", "b1", "w2", "b2")))
            norm_stage(core, "n2", xt)
            q_table, kv_table = dram("q_table", (NPAD, D)), dram("kv_table", (NPAD, 2 * D))
            project_stage(core, xt, [a[f"L1_gnn_W{k}"] for k in "qkvs"], [a[f"L1_gnn_b{k}"] for k in "qkvs"], q_table, kv_table)
        attend_stage(core, "a1", ends, kv_table, q_table, by_dst, partial, inv)
        carry_stage(core, "c1", partial, carry, SEG, HEADS, inv)
        node_stage(core, "m1", 0, base, count, partial, carry, SEG, HEADS, inv)
        with ExitStack() as own:
            xt = sb("xt1", [P, KD, NPAD], own)
            norm_stage(core, "n3", xt)
            l1_ffn_stage(core, xt, *(a[f"L1_ffn_{k}"] for k in ("router_w", "router_b", "W1", "b1", "W2", "b2")), a["expert_rows"])
            norm_stage(core, "n4", xt)
        x_table = dram("x_table", (NPAD, D))
        store_rows_stage(core, "rows", core.xn, x_table)
        filter_stage(core, "fl", by_src, x_table, *(a[f"L2_gnn_{k}"] for k in ("Wf1", "bf1", "Wf2", "bf2")), partial_f)
        carry_stage(core, "c2", partial_f, carry_f, D, 0, 1.0)
        with ExitStack() as own:
            agg = sb("agg2", [P, TILES, D], own)
            node_stage(core, "m2", 1, base, count, partial_f, carry_f, D, 0, 1.0, agg)
            ht = sb("ht2", [P, KD, NPAD], own)
            update_stage(core, agg, ht, *(a[f"L2_gnn_{k}"] for k in ("Wu1", "bu1", "Wu2", "bu2")))
            batchnorm_stage(core, "b2", ht, None, a["L2_gnn_gamma"], a["L2_gnn_beta"])
        with ExitStack() as own:
            xt = sb("xt2", [P, KD, NPAD], own)
            norm_stage(core, "n5", xt)
            l2_ffn_stage(core, xt, *(a[f"L2_ffn_{k}"] for k in ("Wr", "br", "W1", "bn1", "W2", "bn2", "Wo", "bo")))
            norm_stage(core, "n6", xt)
            src_table, dst_table = dram("src_table", (NPAD, SEG)), dram("dst_table", (NPAD, HEADS))
            project3_stage(core, xt, a["L3_gnn_W"], a["L3_gnn_att_src"], a["L3_gnn_att_dst"], src_table, dst_table)
        attend_stage(core, "a3", ends, src_table, dst_table, None, partial, 1.0)
        carry_stage(core, "c3", partial, carry, SEG, HEADS, 1.0)
        with ExitStack() as own:
            agg = sb("agg3", [P, TILES, D], own)
            node_stage(core, "m3", 0, base, count, partial, carry, SEG, HEADS, 1.0, agg, a["L3_gnn_bias"], (src_table, dst_table))
            ht = sb("ht3", [P, KD, NPAD], own)
            batchnorm_stage(core, "b3", ht, agg, a["L3_gnn_gamma"], a["L3_gnn_beta"])
        with ExitStack() as own:
            xt = sb("xt3", [P, KD, NPAD], own)
            norm_stage(core, "n7", xt)
            l3_ffn_stage(core, xt, *(a[f"L3_ffn_{k}"] for k in ("sW1", "sb1", "sW2", "sb2", "sW3", "eW1", "eb1", "eW2", "eb2", "eW3", "b3", "gW", "gb")))
        with Stage(core, "out") as st:
            stored = st.sem("stored")
            with st.block() as block:
                @block.sync
                def _(sp):
                    full = (TILES - 1) * P
                    sp.dma_start(out[0:full, :].rearrange("(a p) d -> p a d", p=P), core.x[:, 0:TILES - 1, :]).then_inc(stored, 16)
                    sp.dma_start(out[full:N, :], core.x[0:N - full, TILES - 1, :]).then_inc(stored, 16)
                    sp.wait_ge(stored, 32)


def layout(inputs):
    a = {k: np.asarray(v) for k, v in inputs.items()}
    del a["L0_ffn_attention_mask"]
    pad = lambda v, fill: np.concatenate([v, np.full((EPAD - E,) + v.shape[1:], fill, v.dtype)])
    columns = lambda v: np.ascontiguousarray(v.reshape(-1, P).T)
    a["src"], a["dst"] = pad(a["src"], N), pad(a["dst"], N)
    a["edge_attr_20"], a["edge_attr_256"] = pad(a["edge_attr_20"], 0), pad(a["edge_attr_256"], 0)
    for k in ("L0_gnn_attn_l", "L0_gnn_attn_r", "L0_ffn_wr", "L3_gnn_att_src", "L3_gnn_att_dst"):
        a[k] = a[k].reshape(-1)
    for k in ("L1_ffn_b1", "L2_gnn_bf1", "L2_gnn_bu1", "L2_gnn_bu2", "L2_gnn_gamma", "L2_gnn_beta", "L3_gnn_gamma", "L3_gnn_beta",
              "L3_ffn_sb1", "L3_ffn_sb2"):
        a[k] = columns(a[k])
    a["L1_ffn_router_w"] = np.ascontiguousarray(a["L1_ffn_router_w"].T)
    experts, _, hidden = a["L1_ffn_W1"].shape
    a["L1_ffn_W1"] = np.ascontiguousarray(a["L1_ffn_W1"].transpose(1, 0, 2)).reshape(D, -1)
    a["L1_ffn_W2"] = a["L1_ffn_W2"].reshape(-1, D)
    a["expert_rows"] = np.repeat(np.eye(experts, dtype=np.float32), hidden, axis=1)
    for k in ("W1", "W2", "Wo"):
        a[f"L2_ffn_{k}"] = a[f"L2_ffn_{k}"].reshape(-1, D)
    for i in "12":
        a[f"L2_ffn_bn{i}"] = np.stack([columns(a.pop(f"L2_ffn_{k}{i}")) for k in ("b", "g", "be", "m", "v")], axis=1)
    a["L3_ffn_eb1"], a["L3_ffn_eb2"] = np.ascontiguousarray(a["L3_ffn_eb1"].T), np.ascontiguousarray(a["L3_ffn_eb2"].T)
    a["L3_ffn_b3"] = np.concatenate([a.pop("L3_ffn_eb3"), a.pop("L3_ffn_sb3")[None]])
    a["consts"] = constants()
    return a


def kernel(**inputs):
    import concourse.bacc as _bacc
    from concourse.bass_utils import run_bass_kernel_spmd as _run

    nc = _bacc.Bacc("TRN2", target_bir_lowering=False, num_devices=1)
    arrays = {f"in_{k}": np.ascontiguousarray(v) for k, v in layout(inputs).items()}
    args = {k[3:]: nc.dram_tensor(k, v.shape, mybir.dt.from_np(v.dtype), kind="ExternalInput").ap() for k, v in arrays.items()}
    out = nc.dram_tensor("out_dram", (N, D), F32, kind="ExternalOutput").ap()
    gnn_ffn_kernel(nc, args, out)
    return _run(nc, [arrays], core_ids=[0]).results[0]["out_dram"]
```

```python
from contextlib import ExitStack, contextmanager

import numpy as np

import concourse.bass as bass
from concourse import mybir

F32 = mybir.dt.float32
F32R = mybir.dt.float32r
BF16 = mybir.dt.bfloat16
I32 = mybir.dt.int32
ACT = mybir.ActivationFunctionType
ALU = mybir.AluOpType
AX = mybir.AxisListType.X

P = 128
N = 3125
D = 256
KD = D // P
TILES = -(-N // P)
GROUP = 5
GROUPS = TILES // GROUP
NPAD = TILES * P
GTOK = GROUP * P
HALF = GTOK // 2
E = 53125
CT = 16
CHUNK = CT * P
CHUNKS = -(-E // CHUNK)
ETILES = CHUNKS * CT
EPAD = ETILES * P
QT = ETILES // 4
HEADS = 8
HD = D // HEADS
SEG = D + HEADS
ROW = SEG + HEADS + 1
BIG = 1e30
KEEP = (N + 1) // 2 - 2
assert GROUPS * GROUP == TILES and KEEP == int(0.5 * N) - 1 and QT <= P

CONST = {}
_at = 0
for _name, _w in (("ident", P), ("le", P), ("lt", P), ("before", P), ("ones", P), ("iota", P), ("iota25", TILES),
                  ("iota_p", 1), ("iota32", 32), ("valid", TILES), ("node", TILES)):
    CONST[_name] = (_at, _w)
    _at += _w
NCONST = _at


def constants():
    p = np.arange(P)[:, None]
    f = np.arange(P)[None, :]
    node = p + P * np.arange(TILES)[None, :]
    parts = [p == f, p <= f, p < f, f < p, np.ones((P, P)), f + 0 * p, np.arange(TILES)[None, :] + 0 * p,
             p, np.arange(32)[None, :] + 0 * p, node < N, node]
    return np.concatenate([np.asarray(x, np.float32) for x in parts], axis=1)


class Chain:

    def __init__(self, eng, sem):
        self.eng, self.sem, self.n, self.step = eng, sem, 0, None

    def add(self, ins):
        ins.then_inc(self.sem, 1)
        self.n += 1

    def settle(self):
        self.eng.wait_ge(self.sem, self.n if self.step is None else self.step + self.n)

    def link(self, ins):
        self.add(ins)
        self.settle()

    @contextmanager
    def loop(self, count, per):
        before = self.n
        with self.eng.Fori(0, count) as i:
            self.step, self.n = i * per + before, 0
            yield i
            assert self.n == per, (self.n, per)
        self.step, self.n = None, before + count * per


class Moved:

    def __init__(self, sem):
        self.sem, self.before, self.after = sem, 0, 0

    def begin(self, raised):
        self.before, self.after = self.after, self.after + raised
        return self

    def count(self, ins):
        ins.then_inc(self.sem, 16)

    def wait(self, eng, value):
        eng.wait_ge(self.sem, value + self.before)


class Core:

    def __init__(self, nc, ctx):
        self.nc = nc
        self.x = ctx.enter_context(nc.sbuf_tensor("x_sb", [P, TILES, D], F32))
        self.xn = ctx.enter_context(nc.sbuf_tensor("xn_sb", [P, TILES, D], F32))
        self.const = ctx.enter_context(nc.sbuf_tensor("const_sb", [P, NCONST], F32))
        self.ps = ctx.enter_context(nc.psum_tensor("ps", [P, 8, 512], F32))
        self.moved = [Moved(ctx.enter_context(nc.semaphore(f"indirect_rows_moved{k}"))) for k in range(8)]

    def c(self, name):
        a, w = CONST[name]
        return self.const[:, a:a + w]


class Stage:

    def __init__(self, core, name):
        self.core, self.nc, self.name = core, core.nc, name
        self.ctx = ExitStack()
        self.sems = []

    def __enter__(self):
        return self

    def __exit__(self, failed, *_):
        if failed is None:
            for s in self.sems:
                self.nc.gpsimd.sem_clear(s)
            self.nc.all_engine_barrier()
        self.ctx.close()

    def sb(self, name, shape, dt=F32):
        return self.ctx.enter_context(self.nc.sbuf_tensor(f"{self.name}_{name}", shape, dt))

    def sem(self, name):
        self.sems.append(self.ctx.enter_context(self.nc.semaphore(f"{self.name}_{name}")))
        return self.sems[-1]

    def moved(self, k, dmas):
        return self.core.moved[k].begin(16 * dmas)

    def block(self):
        return self.nc.Block()


def rows(w):
    return w.rearrange("(k p) m -> p k m", p=P)


def bcast(v):
    return v.partition_broadcast(P)


def load_stage(core, x, consts):
    with Stage(core, "load") as st:
        nc = core.nc
        loaded, zeroed = st.sem("loaded"), st.sem("zeroed")
        with st.block() as block:
            @block.vector
            def _(dve):
                nc.vector.memset(core.x[:, TILES - 1, :], 0.0).then_inc(zeroed, 1)

            @block.sync
            def _(sp):
                sp.dma_start(core.const[:], consts).then_inc(loaded, 16)
                sp.dma_start(core.x[:, 0:TILES - 1, :],
                             x[0:(TILES - 1) * P, :].rearrange("(a p) d -> p a d", p=P)).then_inc(loaded, 16)
                sp.wait_ge(zeroed, 1)
                sp.dma_start(core.x[0:N - (TILES - 1) * P, TILES - 1, :], x[(TILES - 1) * P:N, :]).then_inc(loaded, 16)
                sp.wait_ge(loaded, 48)


def norm_stage(core, name, xt):
    with Stage(core, name) as st:
        nc, x, xn, ps = core.nc, core.x, core.xn, core.ps
        stats = st.sb("stats", [P, TILES, 6])
        mv = st.sb("mv", [P, TILES, 2])
        std = st.sb("std", [P, TILES])
        rstd = st.sb("rstd", [P, TILES])
        chain, var_ready, std_ready, normed = st.sem("chain"), st.sem("var"), st.sem("std"), st.sem("normed")
        transposed, bank_free = st.sem("transposed"), st.sem("bank_free")
        with st.block() as block:
            @block.vector
            def _(dve):
                ch = Chain(dve, chain)
                with ch.loop(TILES, 1) as a:
                    ch.add(nc.vector.bn_stats(stats[:, bass.ds(a, 1), :].rearrange("p a s -> p (a s)"),
                                              x[:, bass.ds(a, 1), :].rearrange("p a d -> p (a d)")))
                ch.settle()
                for a in range(TILES):
                    ch.add(nc.vector.bn_aggr(mv[:, a, :], stats[:, a, :]))
                ch.settle()
                nc.vector.tensor_scalar_add(rstd[:], mv[:, :, 1], 1e-5).then_inc(var_ready, 1)
                dve.wait_ge(std_ready, 1)
                ch.link(nc.vector.reciprocal(rstd[:], std[:]))
                with dve.Fori(0, TILES) as a:
                    nc.vector.tensor_scalar(xn[:, bass.ds(a, 1), :], x[:, bass.ds(a, 1), :],
                                            mv[:, bass.ds(a, 1), 0], rstd[:, bass.ds(a, 1)],
                                            ALU.subtract, ALU.mult).then_inc(normed, 1)

            @block.tensor
            def _(pe):
                for a in range(TILES):
                    pe.wait_ge(normed, a + 1)
                    pe.wait_ge(bank_free, a + 1)
                    for k in range(KD):
                        last = nc.tensor.transpose(ps[:, a % GROUP, k * P:(k + 1) * P], xn[:, a, k * P:(k + 1) * P], core.c("ident"))
                    last.then_inc(transposed, 1)

            @block.scalar
            def _(act):
                act.sem_inc(bank_free, GROUP)
                act.wait_ge(var_ready, 1)
                nc.scalar.activation(std[:], rstd[:], ACT.Sqrt).then_inc(std_ready, 1)
                with act.Fori(0, GROUPS) as g:
                    for j in range(GROUP):
                        act.wait_ge(transposed, g * GROUP + j + 1)
                        nc.scalar.copy(xt[:, :, bass.ds((g * GROUP + j) * P, P)],
                                       ps[:, j, 0:D].rearrange("p (k t) -> p k t", k=KD)).then_inc(bank_free, 1)


def l0_gnn_stage(core, xt, src, dst, weight, attn_l, attn_r, xt_table, al_table):
    H0, C0 = 4, D // 4
    with Stage(core, "g0") as st:
        nc, ps = core.nc, core.ps
        w = st.sb("w", [P, KD, D])
        av = st.sb("av", [P, 2, D])
        idx = st.sb("idx", [P, 2, TILES], I32)
        own = st.sb("own", [P, TILES, D])
        al = st.sb("al", [P, TILES, 2 * H0])
        prod = st.sb("prod", [P, 2, D])
        far = st.sb("far", [P, TILES, D])
        fa = st.sb("fa", [P, 2, TILES, 2 * H0])
        lg = st.sb("lg", [P, TILES, H0])
        lk = st.sb("lk", [P, TILES, H0])
        mx = st.sb("mx", [P, TILES])
        mix = st.sb("mix", [P, GROUP, C0])
        loaded, chain, projected, bank_free, copied = (st.sem(s) for s in ("loaded", "chain", "projected", "bank_free", "copied"))
        rows_ready, stored, centred, expd = (st.sem(s) for s in ("rows_ready", "stored", "centred", "expd"))
        gathered = st.moved(0, 3 * TILES)
        with st.block() as block:
            @block.sync
            def _(sp):
                sp.dma_start(w[:], rows(weight)).then_inc(loaded, 16)
                sp.dma_start(av[:, 0, :], bcast(attn_l)).then_inc(loaded, 16)
                sp.dma_start(av[:, 1, :], bcast(attn_r)).then_inc(loaded, 16)
                sp.dma_start(idx[:, 0, :], src[0:NPAD].rearrange("(a p) -> p a", p=P), allow_slow_non_contiguous=True).then_inc(loaded, 16)
                sp.dma_start(idx[:, 1, :], dst[0:NPAD].rearrange("(a p) -> p a", p=P), allow_slow_non_contiguous=True).then_inc(loaded, 16)
                sp.wait_ge(rows_ready, 1)
                sp.dma_start(xt_table.rearrange("(a p) d -> p a d", p=P), own[:]).then_inc(stored, 16)
                sp.dma_start(al_table.rearrange("(a p) d -> p a d", p=P), al[:]).then_inc(stored, 16)

            @block.tensor
            def _(pe):
                pe.wait_ge(loaded, 80)
                for a in range(TILES):
                    pe.wait_ge(bank_free, a + 1)
                    for k in range(KD):
                        last = nc.tensor.matmul(ps[:, a % GROUP, 0:D], xt[:, k, a * P:(a + 1) * P], w[:, k, :],
                                                start=(k == 0), stop=(k == KD - 1))
                    last.then_inc(projected, 1)

            @block.scalar
            def _(act):
                act.sem_inc(bank_free, GROUP)
                with act.Fori(0, GROUPS) as g:
                    for j in range(GROUP):
                        act.wait_ge(projected, g * GROUP + j + 1)
                        nc.scalar.copy(own[:, bass.ds(g * GROUP + j, 1), :], ps[:, j, 0:D]).then_inc(copied, 1)
                act.wait_ge(centred, 1)
                nc.scalar.activation(lg[:], lk[:], ACT.Exp).then_inc(expd, 1)

            @block.vector
            def _(dve):
                ch = Chain(dve, chain)
                dve.wait_ge(loaded, 80)
                with ch.loop(GROUPS, 4 * GROUP) as g:
                    for j in range(GROUP):
                        dve.wait_ge(copied, g * GROUP + j + 1)
                        for s in range(2):
                            ch.add(nc.vector.tensor_tensor(prod[:, s, :], ps[:, j, 0:D], av[:, s, :], ALU.mult))
                        ch.settle()
                        for s in range(2):
                            ch.add(nc.vector.tensor_reduce(al[:, bass.ds(g * GROUP + j, 1), s * H0:(s + 1) * H0],
                                                           prod[:, s, :].rearrange("p (h c) -> p h c", h=H0), AX, ALU.add))
                        ch.settle()
                        dve.sem_inc(bank_free, 1)
                dve.sem_inc(rows_ready, 1)
                gathered.wait(dve, 3 * TILES * 16)
                ch.link(nc.vector.tensor_tensor(lg[:], fa[:, 0, :, 0:H0], fa[:, 1, :, H0:2 * H0], ALU.add))
                ch.link(nc.vector.scalar_tensor_tensor(lk[:], lg[:], 0.01, lg[:], ALU.mult, ALU.max))
                ch.link(nc.vector.tensor_reduce(mx[:], lk[:], AX, ALU.max))
                nc.vector.tensor_tensor(lk[:], lk[:], mx[:].unsqueeze(2).broadcast_to([P, TILES, H0]), ALU.subtract).then_inc(centred, 1)
                dve.wait_ge(expd, 1)
                ch.link(nc.vector.tensor_reduce(mx[:], lg[:], AX, ALU.add))
                ch.link(nc.vector.reciprocal(mx[:], mx[:]))
                ch.link(nc.vector.tensor_tensor(lk[:], lg[:], mx[:].unsqueeze(2).broadcast_to([P, TILES, H0]), ALU.mult))
                with ch.loop(GROUPS, GROUP * (H0 + 1)) as g:
                    for h in range(H0):
                        for j in range(GROUP):
                            v = far[:, bass.ds(g * GROUP + j, 1), h * C0:(h + 1) * C0].rearrange("p a d -> p (a d)")
                            s = lk[:, bass.ds(g * GROUP + j, 1), h]
                            if h == 0:
                                ch.add(nc.vector.tensor_scalar(mix[:, j, :], v, s, None, ALU.mult))
                            else:
                                ch.add(nc.vector.scalar_tensor_tensor(mix[:, j, :], v, s, mix[:, j, :], ALU.mult, ALU.add))
                        ch.settle()
                    for j in range(GROUP):
                        xa = core.x[:, bass.ds(g * GROUP + j, 1), :].rearrange("p a (h c) -> p (a h) c", h=H0)
                        ch.add(nc.vector.tensor_tensor(xa, xa, mix[:, j, :].unsqueeze(1).broadcast_to([P, H0, C0]), ALU.add))
                    ch.settle()

            @block.gpsimd
            def _(pool):
                pool.wait_ge(loaded, 80)
                pool.wait_ge(stored, 32)
                for a in range(TILES):
                    for to, table, e in ((far[:, a, :], xt_table, 1), (fa[:, 0, a, :], al_table, 0), (fa[:, 1, a, :], al_table, 1)):
                        gathered.count(nc.gpsimd.indirect_dma_start(out=to, out_offset=None, in_=table,
                                                     in_offset=bass.IndirectOffsetOnAxis(ap=idx[:, e, a:a + 1], axis=0),
                                                     bounds_check=NPAD - 1, oob_is_err=False))


def l0_ffn_stage(core, xt, wr, br, w1, b1, w2, b2):
    H = w1.shape[1]
    MH = H // P
    HID, OUT = (0, 1, 2, 3), (4, 5, 6, 4, 5)
    with Stage(core, "f0") as st:
        nc, ps, x = core.nc, core.ps, core.x
        wr_sb, br_sb = st.sb("wr", [P, KD]), st.sb("br", [P, 1])
        w1_sb, b1_sb, w2_sb, b2_sb = st.sb("w1", [P, KD, H]), st.sb("b1", [P, MH]), st.sb("w2", [P, MH, D]), st.sb("b2", [1, D])
        wgt, key = st.sb("wgt", [P, TILES]), st.sb("key", [P, TILES])
        key_row = st.sb("key_row", [P, NPAD])
        hit = st.sb("hit", [P, NPAD], BF16)
        hits = st.sb("hits", [P, TILES, 4])
        rank = st.sb("rank", [P, TILES])
        hid = st.sb("hid", [P, MH, GTOK])
        y = st.sb("y", [P, TILES, D])
        loaded, chain, routed, keyed, spread, spread_free = (st.sem(s) for s in ("loaded", "chain", "routed", "keyed", "spread", "spread_free"))
        hid_ready, hid_free, act_done, out_ready, out_free, y_ready = (st.sem(s) for s in ("hid_ready", "hid_free", "act_done", "out_ready", "out_free", "y_ready"))
        with st.block() as block:
            @block.sync
            def _(sp):
                sp.dma_start(wr_sb[:], wr.rearrange("(k p) -> p k", p=P), allow_slow_non_contiguous=True).then_inc(loaded, 16)
                sp.dma_start(br_sb[:], bcast(br)).then_inc(loaded, 16)
                sp.dma_start(w1_sb[:], rows(w1)).then_inc(loaded, 16)
                sp.dma_start(b1_sb[:], b1.rearrange("(k p) -> p k", p=P), allow_slow_non_contiguous=True).then_inc(loaded, 16)
                sp.dma_start(w2_sb[:], rows(w2)).then_inc(loaded, 16)
                sp.dma_start(b2_sb[:], b2.rearrange("(o d) -> o d", o=1)).then_inc(loaded, 16)

            @block.tensor
            def _(pe):
                pe.sem_inc(out_ready, 1)
                pe.wait_ge(loaded, 96)
                for a in range(TILES):
                    for k in range(KD):
                        last = nc.tensor.matmul(ps[:, 7, a:a + 1], xt[:, k, a * P:(a + 1) * P], wr_sb[:, k:k + 1],
                                                start=(k == 0), stop=(k == KD - 1))
                last.then_inc(routed, 1)
                pe.wait_ge(keyed, 1)
                for a in range(TILES):
                    if a >= 4:
                        pe.wait_ge(spread_free, a - 3)
                    nc.tensor.transpose(ps[:, a % 4, 0:P], key[:, a:a + 1].broadcast_to([P, P]), core.c("ident")).then_inc(spread, 1)
                pe.wait_ge(spread_free, TILES)
                with pe.Fori(0, GROUPS) as g:
                    for m in range(MH):
                        for half in range(2):
                            n = m * 2 + half
                            pe.wait_ge(hid_free, g * 2 * MH + n + 1)
                            for k in range(KD):
                                last = nc.tensor.matmul(ps[:, HID[n % 4], 0:HALF], w1_sb[:, k, m * P:(m + 1) * P],
                                                        xt[:, k, bass.ds(g * GTOK + half * HALF, HALF)],
                                                        start=(k == 0), stop=(k == KD - 1))
                            last.then_inc(hid_ready, 1)
                    pe.wait_ge(act_done, (g + 1) * 2 * MH)
                    for j in range(GROUP):
                        pe.wait_ge(out_free, g * GROUP + j + 1)
                        nc.tensor.matmul(ps[:, OUT[j], 0:D], core.c("ones")[0:1, :], b2_sb[:], start=True, stop=False)
                        for m in range(MH):
                            last = nc.tensor.matmul(ps[:, OUT[j], 0:D], hid[:, m, j * P:(j + 1) * P], w2_sb[:, m, :],
                                                    start=False, stop=(m == MH - 1))
                        last.then_inc(out_ready, 1)

            @block.scalar
            def _(act):
                act.sem_inc(hid_free, 4)
                act.sem_inc(out_free, 2)
                for a in range(TILES):
                    act.wait_ge(spread, a + 1)
                    nc.scalar.copy(key_row[:, a * P:(a + 1) * P], ps[:, a % 4, 0:P]).then_inc(spread_free, 1)
                act.wait_ge(loaded, 96)
                with act.Fori(0, GROUPS) as g:
                    act.wait_ge(out_ready, g * GROUP + 1)
                    for m in range(MH):
                        for half in range(2):
                            n = m * 2 + half
                            act.wait_ge(hid_ready, g * 2 * MH + n + 1)
                            nc.scalar.activation(hid[:, m, half * HALF:(half + 1) * HALF], ps[:, HID[n % 4], 0:HALF],
                                                 ACT.Gelu_apprx_tanh, bias=b1_sb[:, m:m + 1]).then_inc(act_done, 1)
                            act.wait_ge(act_done, g * 2 * MH + n + 1)
                            act.sem_inc(hid_free, 1)
                    for j in range(GROUP):
                        act.wait_ge(out_ready, g * GROUP + j + 1 + 1)
                        nc.scalar.copy(y[:, bass.ds(g * GROUP + j, 1), :], ps[:, OUT[j], 0:D]).then_inc(y_ready, 1)
                        act.wait_ge(y_ready, g * GROUP + j + 1)
                        act.sem_inc(out_free, 1)

            @block.vector
            def _(dve):
                ch = Chain(dve, chain)
                dve.wait_ge(loaded, 96)
                dve.wait_ge(routed, 1)
                ch.link(nc.vector.tensor_scalar(wgt[:], ps[:, 7, 0:TILES], br_sb[:], None, ALU.add))
                ch.link(nc.vector.tensor_tensor(key[:], wgt[:], core.c("valid"), ALU.mult))
                ch.link(nc.vector.tensor_scalar(rank[:], core.c("valid"), 1.0, BIG, ALU.subtract, ALU.mult))
                nc.vector.tensor_tensor(key[:], key[:], rank[:], ALU.add).then_inc(keyed, 1)
                dve.wait_ge(keyed, 1)
                ch.link(nc.vector.memset(hits[:], 0.0))
                dve.wait_ge(spread_free, TILES)
                for a in range(TILES):
                    own = key[:, a:a + 1]
                    if a > 0:
                        ch.add(nc.vector.tensor_scalar(hit[:, 0:a * P], key_row[:, 0:a * P], own, 0.0, ALU.is_ge, ALU.add,
                                                       accum_out=hits[:, a, 0:1]))
                    if a < TILES - 1:
                        ch.add(nc.vector.tensor_scalar(hit[:, (a + 1) * P:], key_row[:, (a + 1) * P:], own, 0.0, ALU.is_gt, ALU.add,
                                                       accum_out=hits[:, a, 1:2]))
                    ch.add(nc.vector.tensor_scalar(hit[:, a * P:(a + 1) * P], key_row[:, a * P:(a + 1) * P], own, 0.0,
                                                   ALU.is_gt, ALU.add, accum_out=hits[:, a, 2:3]))
                    ch.settle()
                    ch.link(nc.vector.scalar_tensor_tensor(hit[:, a * P:(a + 1) * P], key_row[:, a * P:(a + 1) * P], own,
                                                           core.c("before"), ALU.is_equal, ALU.mult, accum_out=hits[:, a, 3:4]))
                ch.link(nc.vector.tensor_reduce(rank[:], hits[:], AX, ALU.add))
                ch.link(nc.vector.scalar_tensor_tensor(wgt[:], rank[:], float(KEEP), wgt[:], ALU.is_lt, ALU.mult))
                with ch.loop(TILES, 2) as a:
                    dve.wait_ge(y_ready, a + 1)
                    xa = x[:, bass.ds(a, 1), :].rearrange("p a d -> p (a d)")
                    ya = y[:, bass.ds(a, 1), :].rearrange("p a d -> p (a d)")
                    ch.link(nc.vector.scalar_tensor_tensor(ya, ya, wgt[:, bass.ds(a, 1)],
                                                           core.xn[:, bass.ds(a, 1), :].rearrange("p a d -> p (a d)"), ALU.mult, ALU.add))
                    ch.link(nc.vector.tensor_tensor(xa, xa, ya, ALU.add))


def l1_ffn_stage(core, xt, router_wt, router_b, w1, b1t, w2, b2, sel):
    NE = router_wt.shape[1]
    H = w1.shape[1]
    MH = H // P
    HID, OUT = (0, 1, 2, 3), (4, 5, 6, 4, 5)
    with Stage(core, "f1") as st:
        nc, ps, x = core.nc, core.ps, core.x
        rw, rb = st.sb("rw", [P, KD, NE]), st.sb("rb", [P, NE])
        w1_sb, b1_sb, w2_sb, b2_sb, sel_sb = (st.sb("w1", [P, KD, H]), st.sb("b1", [P, MH]), st.sb("w2", [P, MH, D]),
                                              st.sb("b2", [NE, D]), st.sb("sel", [NE, H]))
        lg, top, one_hot = st.sb("lg", [P, TILES, NE]), st.sb("top", [P, TILES]), st.sb("one_hot", [P, TILES, NE])
        choice = st.sb("choice", [NE, NPAD])
        sink = st.sb("sink", [NE, NPAD])
        choice_g = st.sb("choice_g", [NE, GTOK])
        hid = st.sb("hid", [P, MH, GTOK])
        loaded, chain, routed, chosen, turned, turned_free = (st.sem(s) for s in ("loaded", "chain", "routed", "chosen", "turned", "turned_free"))
        sunk, hid_ready, hid_free, out_ready, out_free, choice_ready = (st.sem(s) for s in ("sunk", "hid_ready", "hid_free", "out_ready", "out_free", "choice_ready"))
        FIRST = 13
        with st.block() as block:
            @block.sync
            def _(sp):
                sp.dma_start(rw[:], rows(router_wt)).then_inc(loaded, 16)
                sp.dma_start(rb[:], bcast(router_b)).then_inc(loaded, 16)
                sp.dma_start(w1_sb[:], rows(w1)).then_inc(loaded, 16)
                sp.dma_start(b1_sb[:], b1t).then_inc(loaded, 16)
                sp.dma_start(w2_sb[:], rows(w2)).then_inc(loaded, 16)
                sp.dma_start(b2_sb[:], b2).then_inc(loaded, 16)
                sp.dma_start(sel_sb[:], sel).then_inc(loaded, 16)

            @block.tensor
            def _(pe):
                pe.sem_inc(out_ready, 1)
                pe.wait_ge(loaded, 112)
                for a in range(TILES):
                    at = ps[:, 6, a * NE:(a + 1) * NE] if a < FIRST else ps[:, 7, (a - FIRST) * NE:(a - FIRST + 1) * NE]
                    for k in range(KD):
                        last = nc.tensor.matmul(at, xt[:, k, a * P:(a + 1) * P], rw[:, k, :], start=(k == 0), stop=(k == KD - 1))
                last.then_inc(routed, 1)
                pe.wait_ge(chosen, 1)
                for a in range(TILES):
                    if a >= 4:
                        pe.wait_ge(turned_free, a - 3)
                    nc.tensor.transpose(ps[0:NE, a % 4, 0:P], one_hot[:, a, :], core.c("ident")).then_inc(turned, 1)
                pe.wait_ge(turned_free, TILES)
                pe.wait_ge(sunk, 1)
                with pe.Fori(0, GROUPS) as g:
                    for m in range(MH):
                        for half in range(2):
                            n = m * 2 + half
                            pe.wait_ge(hid_free, g * 2 * MH + n + 1)
                            cols = bass.ds(g * GTOK + half * HALF, HALF)
                            for k in range(KD):
                                nc.tensor.matmul(ps[:, HID[n % 4], 0:HALF], w1_sb[:, k, m * P:(m + 1) * P], xt[:, k, cols],
                                                 start=(k == 0), stop=False)
                            nc.tensor.matmul(ps[:, HID[n % 4], 0:HALF], sel_sb[:, m * P:(m + 1) * P], sink[:, cols],
                                             start=False, stop=True).then_inc(hid_ready, 1)
                    pe.wait_ge(hid_free, (g + 1) * 2 * MH + 4)
                    pe.wait_ge(choice_ready, g + 1)
                    for j in range(GROUP):
                        pe.wait_ge(out_free, g * GROUP + j + 1)
                        nc.tensor.matmul(ps[:, OUT[j], 0:D], choice_g[:, j * P:(j + 1) * P], b2_sb[:], start=True, stop=False)
                        for m in range(MH):
                            last = nc.tensor.matmul(ps[:, OUT[j], 0:D], hid[:, m, j * P:(j + 1) * P], w2_sb[:, m, :],
                                                    start=False, stop=(m == MH - 1))
                        last.then_inc(out_ready, 1)

            @block.scalar
            def _(act):
                act.sem_inc(hid_free, 4)
                act.sem_inc(out_free, 2)
                act.wait_ge(loaded, 112)
                for a in range(TILES):
                    act.wait_ge(turned, a + 1)
                    nc.scalar.copy(choice[:, a * P:(a + 1) * P], ps[0:NE, a % 4, 0:P]).then_inc(turned_free, 1)
                act.wait_ge(turned_free, TILES)
                with act.Fori(0, GROUPS) as g:
                    act.wait_ge(out_ready, g * GROUP + 1)
                    nc.scalar.copy(choice_g[:], choice[:, bass.ds(g * GTOK, GTOK)]).then_inc(choice_ready, 1)
                    for m in range(MH):
                        for half in range(2):
                            n = m * 2 + half
                            act.wait_ge(hid_ready, g * 2 * MH + n + 1)
                            nc.scalar.activation(hid[:, m, half * HALF:(half + 1) * HALF], ps[:, HID[n % 4], 0:HALF],
                                                 ACT.Relu, bias=b1_sb[:, m:m + 1]).then_inc(hid_free, 1)

            @block.vector
            def _(dve):
                ch = Chain(dve, chain)
                dve.wait_ge(loaded, 112)
                dve.wait_ge(routed, 1)
                for a0, a1, bank in ((0, FIRST, 6), (FIRST, TILES, 7)):
                    ch.add(nc.vector.tensor_tensor(lg[:, a0:a1, :], ps[:, bank, 0:(a1 - a0) * NE].rearrange("p (a e) -> p a e", e=NE),
                                                   rb[:].unsqueeze(1).broadcast_to([P, a1 - a0, NE]), ALU.add))
                ch.settle()
                ch.link(nc.vector.tensor_reduce(top[:], lg[:], AX, ALU.max))
                ch.link(nc.vector.tensor_tensor(one_hot[:], lg[:], top[:].unsqueeze(2).broadcast_to([P, TILES, NE]), ALU.is_equal))
                ch.link(nc.vector.scalar_tensor_tensor(lg[:], one_hot[:], -2.0 * NE, core.c("iota32").unsqueeze(1).broadcast_to([P, TILES, NE]),
                                                       ALU.mult, ALU.add))
                ch.link(nc.vector.tensor_reduce(top[:], lg[:], AX, ALU.min))
                nc.vector.tensor_tensor(one_hot[:], lg[:], top[:].unsqueeze(2).broadcast_to([P, TILES, NE]), ALU.is_equal).then_inc(chosen, 1)
                dve.wait_ge(turned_free, TILES)
                nc.vector.tensor_scalar(sink[:], choice[:], 1.0, BIG, ALU.subtract, ALU.mult).then_inc(sunk, 1)
                with dve.Fori(0, GROUPS) as g:
                    for j in range(GROUP):
                        dve.wait_ge(out_ready, g * GROUP + j + 1 + 1)
                        xa = x[:, bass.ds(g * GROUP + j, 1), :].rearrange("p a d -> p (a d)")
                        nc.vector.scalar_tensor_tensor(xa, ps[:, OUT[j], 0:D], 0.0, xa, ALU.max, ALU.add).then_inc(out_free, 1)


def gate_bias(core, pe, ps, cw, cwt, turned, turned_free, bias, n, bias_ready, bias_free):
    nc = core.nc
    for a in range(TILES):
        if a >= 4:
            pe.wait_ge(turned_free, a - 3)
        nc.tensor.transpose(ps[0:n, a % 4, 0:P], cw[:, a, :], core.c("ident")).then_inc(turned, 1)
    pe.wait_ge(turned_free, TILES)
    for a in range(TILES):
        if a >= 4:
            pe.wait_ge(bias_free, a - 3)
        nc.tensor.matmul(ps[:, a % 4, 0:D], cwt[:, a * P:(a + 1) * P], bias, start=True, stop=True).then_inc(bias_ready, 1)
    pe.wait_ge(bias_free, TILES)


def l2_ffn_stage(core, xt, wr, br, w1, bn1, w2, bn2, wo, bo):
    NE = wr.shape[1]
    EM = NE * KD
    with Stage(core, "f2") as st:
        nc, ps, x = core.nc, core.ps, core.x
        wr_sb, br_sb, bo_sb = st.sb("wr", [P, KD, NE]), st.sb("br", [P, NE]), st.sb("bo", [NE, D])
        w_sb = st.sb("w", [P, 3, NE * KD, D])
        bn = st.sb("bn", [P, 2, 5, EM])
        lg, top, cw = st.sb("lg", [P, TILES, NE]), st.sb("top", [P, TILES]), st.sb("cw", [P, TILES, NE])
        cwt = st.sb("cwt", [NE, NPAD])
        hid = st.sb("hid", [P, 2, 2, KD, GTOK])
        loaded, chain, routed, expd, gated, turned, turned_free = (st.sem(s) for s in ("loaded", "chain", "routed", "expd", "gated", "turned", "turned_free"))
        bias_ready, bias_free, var_ready, std_ready, bn_ready = (st.sem(s) for s in ("bias_ready", "bias_free", "var_ready", "std_ready", "bn_ready"))
        hid_ready, hid_free, out_ready, out_free, expert_out = (st.sem(s) for s in ("hid_ready", "hid_free", "out_ready", "out_free", "expert_out"))
        with st.block() as block:
            @block.sync
            def _(sp):
                sp.dma_start(wr_sb[:], rows(wr)).then_inc(loaded, 16)
                sp.dma_start(br_sb[:], bcast(br)).then_inc(loaded, 16)
                sp.dma_start(bo_sb[:], bo).then_inc(loaded, 16)
                sp.dma_start(bn[:, 0], bn1).then_inc(loaded, 16)
                sp.dma_start(bn[:, 1], bn2).then_inc(loaded, 16)
                for i, w in enumerate((w1, w2, wo)):
                    sp.dma_start(w_sb[:, i], rows(w)).then_inc(loaded, 16)

            @block.tensor
            def _(pe):
                pe.sem_inc(out_ready, 1)
                pe.wait_ge(loaded, 128)
                for a in range(TILES):
                    for k in range(KD):
                        last = nc.tensor.matmul(ps[:, 7, a * NE:(a + 1) * NE], xt[:, k, a * P:(a + 1) * P], wr_sb[:, k, :],
                                                start=(k == 0), stop=(k == KD - 1))
                last.then_inc(routed, 1)
                pe.wait_ge(gated, 1)
                gate_bias(core, pe, ps, cw, cwt, turned, turned_free, bo_sb[:], NE, bias_ready, bias_free)

                def hidden(g, e, layer):
                    for m in range(KD):
                        for half in range(2):
                            n = (e * 2 + layer) * 4 + m * 2 + half
                            pe.wait_ge(hid_free, g * NE * 8 + n + 1)
                            for k in range(KD):
                                cols = bass.ds(g * GTOK + half * HALF, HALF) if layer == 0 else slice(half * HALF, (half + 1) * HALF)
                                src = xt[:, k, cols] if layer == 0 else hid[:, e % 2, 0, k, cols]
                                last = nc.tensor.matmul(ps[:, n % 4, 0:HALF], w_sb[:, layer, e * KD + k, m * P:(m + 1) * P], src,
                                                        start=(k == 0), stop=(k == KD - 1))
                            last.then_inc(hid_ready, 1)

                def output(g, e):
                    pe.wait_ge(hid_free, g * NE * 8 + (e * 2 + 2) * 4 + 4)
                    for j in range(GROUP):
                        n = e * GROUP + j
                        pe.wait_ge(out_free, g * NE * GROUP + n + 1)
                        for k in range(KD):
                            last = nc.tensor.matmul(ps[:, 4 + n % 4, 0:D], hid[:, e % 2, 1, k, j * P:(j + 1) * P],
                                                    w_sb[:, 2, e * KD + k, :], start=(k == 0), stop=(k == KD - 1))
                        last.then_inc(out_ready, 1)

                with pe.Fori(0, GROUPS) as g:
                    for e in range(NE):
                        hidden(g, e, 0)
                        if e > 0:
                            output(g, e - 1)
                        pe.wait_ge(hid_free, g * NE * 8 + (e * 2 + 1) * 4 + 4)
                        hidden(g, e, 1)
                    output(g, NE - 1)

            @block.scalar
            def _(act):
                act.sem_inc(hid_free, 4)
                act.sem_inc(out_free, 4)
                act.wait_ge(var_ready, 1)
                nc.scalar.activation(bn[:, :, 4, :], bn[:, :, 4, :], ACT.Sqrt).then_inc(std_ready, 1)
                act.wait_ge(routed, 2)
                nc.scalar.activation(cw[:], lg[:], ACT.Exp).then_inc(expd, 1)
                for a in range(TILES):
                    act.wait_ge(turned, a + 1)
                    nc.scalar.copy(cwt[:, a * P:(a + 1) * P], ps[0:NE, a % 4, 0:P]).then_inc(turned_free, 1)
                act.wait_ge(bn_ready, 1)
                with act.Fori(0, GROUPS) as g:
                    for e in range(NE):
                        for layer in range(2):
                            if layer == 0 and e >= 2:
                                act.wait_ge(out_ready, g * NE * GROUP + (e - 1) * GROUP + 1)
                            if layer == 0 and e < 2:
                                act.wait_ge(out_ready, g * NE * GROUP + 1)
                            for m in range(KD):
                                for half in range(2):
                                    n = (e * 2 + layer) * 4 + m * 2 + half
                                    act.wait_ge(hid_ready, g * NE * 8 + n + 1)
                                    nc.scalar.activation(hid[:, e % 2, layer, m, half * HALF:(half + 1) * HALF], ps[:, n % 4, 0:HALF],
                                                         ACT.Relu, bias=bn[:, layer, 2, e * KD + m:e * KD + m + 1],
                                                         scale=bn[:, layer, 1, e * KD + m:e * KD + m + 1]).then_inc(hid_free, 1)

            @block.vector
            def _(dve):
                ch = Chain(dve, chain)
                dve.wait_ge(loaded, 128)
                ch.link(nc.vector.tensor_scalar_add(bn[:, :, 4, :], bn[:, :, 4, :], 1e-3))
                dve.sem_inc(var_ready, 1)
                dve.wait_ge(std_ready, 1)
                ch.link(nc.vector.reciprocal(bn[:, :, 4, :], bn[:, :, 4, :]))
                ch.link(nc.vector.tensor_tensor(bn[:, :, 1, :], bn[:, :, 1, :], bn[:, :, 4, :], ALU.mult))
                ch.link(nc.vector.tensor_tensor(bn[:, :, 0, :], bn[:, :, 0, :], bn[:, :, 3, :], ALU.subtract))
                ch.link(nc.vector.tensor_tensor(bn[:, :, 0, :], bn[:, :, 0, :], bn[:, :, 1, :], ALU.mult))
                ch.link(nc.vector.tensor_tensor(bn[:, :, 2, :], bn[:, :, 2, :], bn[:, :, 0, :], ALU.add))
                dve.sem_inc(bn_ready, 1)
                dve.wait_ge(routed, 1)
                ch.link(nc.vector.tensor_tensor(lg[:], ps[:, 7, 0:TILES * NE].rearrange("p (a e) -> p a e", e=NE),
                                                br_sb[:].unsqueeze(1).broadcast_to([P, TILES, NE]), ALU.add))
                ch.link(nc.vector.tensor_reduce(top[:], lg[:], AX, ALU.max))
                ch.link(nc.vector.tensor_tensor(lg[:], lg[:], top[:].unsqueeze(2).broadcast_to([P, TILES, NE]), ALU.subtract))
                dve.sem_inc(routed, 1)
                dve.wait_ge(expd, 1)
                ch.link(nc.vector.tensor_reduce(top[:], cw[:], AX, ALU.add))
                ch.link(nc.vector.reciprocal(top[:], top[:]))
                ch.link(nc.vector.tensor_tensor(cw[:], cw[:], top[:].unsqueeze(2).broadcast_to([P, TILES, NE]), ALU.mult))
                dve.sem_inc(gated, 1)
                for a in range(TILES):
                    dve.wait_ge(bias_ready, a + 1)
                    nc.vector.tensor_tensor(x[:, a, :], ps[:, a % 4, 0:D], x[:, a, :], ALU.add).then_inc(bias_free, 1)
                dve.wait_ge(bias_free, TILES)
                with dve.Fori(0, GROUPS) as g:
                    for e in range(NE):
                        if e > 0:
                            dve.wait_ge(out_free, g * NE * GROUP + e * GROUP + 4)
                        for j in range(GROUP):
                            n = e * GROUP + j
                            dve.wait_ge(out_ready, g * NE * GROUP + n + 1 + 1)
                            xa = x[:, bass.ds(g * GROUP + j, 1), :].rearrange("p a d -> p (a d)")
                            nc.vector.scalar_tensor_tensor(xa, ps[:, 4 + n % 4, 0:D], cw[:, bass.ds(g * GROUP + j, 1), e], xa,
                                                           ALU.mult, ALU.add).then_inc(out_free, 1)


def l3_ffn_stage(core, xt, sw1, sb1, sw2, sb2, sw3, ew1, eb1, ew2, eb2, ew3, b3, gw, gb):
    NE, EH1, EH2 = 4, 128, 64
    NC = NE + 1
    with Stage(core, "f3") as st:
        nc, ps, x = core.nc, core.ps, core.x
        gw_sb, gb_sb, b3_sb = st.sb("gw", [P, KD, NE]), st.sb("gb", [P, NE]), st.sb("b3", [NC, D])
        sw1_sb, sw2_sb, sw3_sb = st.sb("sw1", [P, KD, D]), st.sb("sw2", [P, KD, P]), st.sb("sw3", [P, D])
        ew1_sb, ew2_sb, ew3_sb = st.sb("ew1", [P, NE, KD, EH1]), st.sb("ew2", [P, NE, EH2]), st.sb("ew3", [EH2, NE, D])
        sb1_sb, sb2_sb, eb1_sb, eb2_sb = st.sb("sb1", [P, KD]), st.sb("sb2", [P, 1]), st.sb("eb1", [P, NE]), st.sb("eb2", [EH2, NE])
        lg, top, gate, first, rest = (st.sb("lg", [P, TILES, NE]), st.sb("top", [P, 2, TILES]), st.sb("gate", [P, TILES, NE]),
                                      st.sb("first", [P, TILES, NE]), st.sb("rest", [P, TILES, NE]))
        cw, cwt = st.sb("cw", [P, TILES, NC]), st.sb("cwt", [NC, NPAD])
        h1 = st.sb("h1", [P, 3, 2, GTOK])
        h2 = st.sb("h2", [P, 3, GTOK])
        names = ("loaded", "chain", "routed", "expd", "gated", "turned", "turned_free", "bias_ready", "bias_free",
                 "hid_ready", "hid_free", "out_ready", "out_free")
        loaded, chain, routed, expd, gated, turned, turned_free, bias_ready, bias_free, hid_ready, hid_free, out_ready, out_free = map(st.sem, names)
        blocks = {(-1, 0): [0, 1], (-1, 1): [0]}
        for e in range(NE):
            blocks[(e, 0)] = blocks[(e, 1)] = [0]
        order = [(-1, 0), (0, 0), (-1, 1), (1, 0), (0, 1), (2, 0), (1, 1), (3, 0), (2, 1), (3, 1)]
        first_use, uses = {}, 0
        for key in order:
            first_use[key] = uses
            uses += 2 * len(blocks[key])
        outs = [-1, 0, 1, 2, 3]
        slot = {-1: 2, 0: 0, 1: 1, 2: 0, 3: 1}
        assert uses == 22
        HIDB = [i % 4 for i in range(20)] + [0, 1]
        OUTS = GROUP * NC
        OUTB = [4 + i % 3 for i in range(OUTS - 1)] + [5]
        with st.block() as block:
            @block.sync
            def _(sp):
                for to, of in ((gw_sb, rows(gw)), (gb_sb, bcast(gb)), (b3_sb, b3), (sw1_sb, rows(sw1)), (sw2_sb, rows(sw2)), (sw3_sb, sw3),
                               (ew2_sb, ew2.rearrange("e p m -> p e m")), (ew3_sb, ew3.rearrange("e p m -> p e m")),
                               (sb1_sb, sb1), (sb2_sb, sb2), (eb1_sb, eb1), (eb2_sb, eb2)):
                    sp.dma_start(to[:], of).then_inc(loaded, 16)
                for e in range(NE):
                    sp.dma_start(ew1_sb[:, e], rows(ew1[e])).then_inc(loaded, 16)

            @block.tensor
            def _(pe):
                pe.sem_inc(out_ready, 1)
                pe.wait_ge(loaded, 256)
                for a in range(TILES):
                    for k in range(KD):
                        last = nc.tensor.matmul(ps[:, 7, a * NE:(a + 1) * NE], xt[:, k, a * P:(a + 1) * P], gw_sb[:, k, :],
                                                start=(k == 0), stop=(k == KD - 1))
                last.then_inc(routed, 1)
                pe.wait_ge(gated, 1)
                gate_bias(core, pe, ps, cw, cwt, turned, turned_free, b3_sb[:], NC, bias_ready, bias_free)

                def hidden(g, part, layer):
                    s = slot[part]
                    if layer == 1:
                        pe.wait_ge(hid_free, g * uses + first_use[(part, 0)] + 2 * len(blocks[(part, 0)]) + 2)
                    for m in blocks[(part, layer)]:
                        for half in range(2):
                            n = first_use[(part, layer)] + m * 2 + half
                            pe.wait_ge(hid_free, g * uses + n + 1)
                            cols = slice(half * HALF, (half + 1) * HALF)
                            if layer == 0:
                                w = [(sw1_sb[:, k, m * P:(m + 1) * P] if part < 0 else ew1_sb[:, part, k, :]) for k in range(KD)]
                                v = [xt[:, k, bass.ds(g * GTOK + half * HALF, HALF)] for k in range(KD)]
                            elif part < 0:
                                w = [sw2_sb[:, k, :] for k in range(KD)]
                                v = [h1[:, s, k, cols] for k in range(KD)]
                            else:
                                w, v = [ew2_sb[:, part, :]], [h1[:, s, 0, cols]]
                            rows_out = EH2 if (part >= 0 and layer == 1) else P
                            for k in range(len(w)):
                                last = nc.tensor.matmul(ps[0:rows_out, HIDB[n], 0:HALF], w[k], v[k], start=(k == 0), stop=(k == len(w) - 1))
                            last.then_inc(hid_ready, 1)

                def output(g, i):
                    part = outs[i]
                    s = slot[part]
                    pe.wait_ge(hid_free, g * uses + first_use[(part, 1)] + 2 + 2)
                    for j in range(GROUP):
                        n = i * GROUP + j
                        pe.wait_ge(out_free, g * OUTS + n + 1)
                        if part < 0:
                            w, v = h2[:, s, j * P:(j + 1) * P], sw3_sb[:]
                        else:
                            w, v = h2[0:EH2, s, j * P:(j + 1) * P], ew3_sb[:, part, :]
                        nc.tensor.matmul(ps[:, OUTB[n], 0:D], w, v, start=True, stop=True).then_inc(out_ready, 1)

                with pe.Fori(0, GROUPS) as g:
                    hidden(g, -1, 0)
                    hidden(g, 0, 0)
                    hidden(g, -1, 1)
                    hidden(g, 1, 0)
                    output(g, 0)
                    hidden(g, 0, 1)
                    hidden(g, 2, 0)
                    output(g, 1)
                    hidden(g, 1, 1)
                    hidden(g, 3, 0)
                    output(g, 2)
                    hidden(g, 2, 1)
                    output(g, 3)
                    hidden(g, 3, 1)
                    output(g, 4)

            @block.scalar
            def _(act):
                act.sem_inc(hid_free, 2)
                act.sem_inc(out_free, 2)
                act.wait_ge(routed, 2)
                nc.scalar.activation(gate[:], lg[:], ACT.Exp).then_inc(expd, 1)
                act.wait_ge(expd, 2)
                nc.scalar.activation(rest[:], lg[:], ACT.Exp).then_inc(expd, 1)
                for a in range(TILES):
                    act.wait_ge(turned, a + 1)
                    nc.scalar.copy(cwt[:, a * P:(a + 1) * P], ps[0:NC, a % 4, 0:P]).then_inc(turned_free, 1)
                act.wait_ge(loaded, 256)
                with act.Fori(0, GROUPS) as g:
                    act.wait_ge(out_ready, g * OUTS + 1)
                    for part, layer in order:
                        s = slot[part]
                        if part >= 2 and layer == 0:
                            act.wait_ge(out_ready, g * OUTS + GROUP * (outs.index(part - 2) + 1) + 1)
                        for m in blocks[(part, layer)]:
                            for half in range(2):
                                n = first_use[(part, layer)] + m * 2 + half
                                cols = slice(half * HALF, (half + 1) * HALF)
                                act.wait_ge(hid_ready, g * uses + n + 1)
                                if layer == 0:
                                    to, b = h1[:, s, m, cols], (sb1_sb[:, m:m + 1] if part < 0 else eb1_sb[:, part:part + 1])
                                elif part < 0:
                                    to, b = h2[:, s, cols], sb2_sb[:]
                                else:
                                    to, b = h2[0:EH2, s, cols], eb2_sb[:, part:part + 1]
                                nc.scalar.activation(to, ps[0:to.shape[0], HIDB[n], 0:HALF], ACT.Relu, bias=b).then_inc(hid_free, 1)

            @block.vector
            def _(dve):
                ch = Chain(dve, chain)
                b = lambda v: v.unsqueeze(2).broadcast_to([P, TILES, NE])
                iota = core.c("iota32")[:, 0:NE].unsqueeze(1).broadcast_to([P, TILES, NE])
                dve.wait_ge(loaded, 256)
                dve.wait_ge(routed, 1)
                ch.link(nc.vector.tensor_tensor(lg[:], ps[:, 7, 0:TILES * NE].rearrange("p (a e) -> p a e", e=NE),
                                                gb_sb[:].unsqueeze(1).broadcast_to([P, TILES, NE]), ALU.add))
                ch.link(nc.vector.tensor_reduce(top[:, 0], lg[:], AX, ALU.max))
                ch.link(nc.vector.tensor_tensor(lg[:], lg[:], b(top[:, 0]), ALU.subtract))
                dve.sem_inc(routed, 1)
                dve.wait_ge(expd, 1)
                ch.link(nc.vector.tensor_reduce(top[:, 0], gate[:], AX, ALU.add))
                ch.link(nc.vector.reciprocal(top[:, 0], top[:, 0]))
                ch.link(nc.vector.tensor_tensor(gate[:], gate[:], b(top[:, 0]), ALU.mult))

                def pick(values, best, to):
                    ch.link(nc.vector.tensor_reduce(best, values, AX, ALU.max))
                    ch.link(nc.vector.tensor_tensor(to, values, b(best), ALU.is_equal))
                    ch.link(nc.vector.scalar_tensor_tensor(lg[:], to, -2.0 * NE, iota, ALU.mult, ALU.add))
                    ch.link(nc.vector.tensor_reduce(top[:, 1], lg[:], AX, ALU.min))
                    ch.link(nc.vector.tensor_tensor(to, lg[:], b(top[:, 1]), ALU.is_equal))

                pick(gate[:], top[:, 0], first[:])
                ch.link(nc.vector.scalar_tensor_tensor(rest[:], first[:], -4.0, gate[:], ALU.mult, ALU.add))
                ch.link(nc.vector.tensor_reduce(top[:, 1], rest[:], AX, ALU.max))
                pick(rest[:], top[:, 1], cw[:, :, 0:NE])
                ch.link(nc.vector.tensor_tensor(first[:], first[:], cw[:, :, 0:NE], ALU.add))
                ch.link(nc.vector.tensor_tensor(lg[:], gate[:], b(top[:, 0]), ALU.subtract))
                dve.sem_inc(expd, 1)
                dve.wait_ge(expd, 3)
                ch.link(nc.vector.tensor_tensor(rest[:], rest[:], first[:], ALU.mult))
                ch.link(nc.vector.tensor_reduce(top[:, 1], rest[:], AX, ALU.add))
                ch.link(nc.vector.reciprocal(top[:, 1], top[:, 1]))
                ch.link(nc.vector.memset(cw[:], 1.0))
                ch.link(nc.vector.tensor_tensor(cw[:, :, 0:NE], rest[:], b(top[:, 1]), ALU.mult))
                dve.sem_inc(gated, 1)
                for a in range(TILES):
                    dve.wait_ge(bias_ready, a + 1)
                    nc.vector.tensor_tensor(x[:, a, :], ps[:, a % 4, 0:D], x[:, a, :], ALU.add).then_inc(bias_free, 1)
                dve.wait_ge(bias_free, TILES)
                with dve.Fori(0, GROUPS) as g:
                    for i, part in enumerate(outs):
                        c = NE if part < 0 else part
                        if i > 0:
                            dve.wait_ge(out_free, g * OUTS + i * GROUP + 2)
                        for j in range(GROUP):
                            n = i * GROUP + j
                            dve.wait_ge(out_ready, g * OUTS + n + 1 + 1)
                            xa = x[:, bass.ds(g * GROUP + j, 1), :].rearrange("p a d -> p (a d)")
                            nc.vector.scalar_tensor_tensor(xa, ps[:, OUTB[n], 0:D], cw[:, bass.ds(g * GROUP + j, 1), c], xa,
                                                           ALU.mult, ALU.add).then_inc(out_free, 1)


def count_stage(core, keys, split, base, count):
    with Stage(core, "count") as st:
        nc, ps = core.nc, core.ps
        raw = st.sb("raw", [P, 2, 3, ETILES], I32)
        lo_hot = st.sb("lo_hot", [P, 2, CT, P], BF16)
        hi_hot = st.sb("hi_hot", [P, 2, CT, TILES], BF16)
        zero = st.sb("zero", [P, P], BF16)
        total = st.sb("total", [P, 2, TILES])
        run = st.sb("run", [P, 2, TILES])
        loaded, chain, hot, used, opened, counted, summed = (st.sem(s) for s in ("loaded", "chain", "hot", "used", "opened", "counted", "summed"))
        iota = core.c("iota").unsqueeze(1).broadcast_to([P, CT, P])
        iota25 = core.c("iota25").unsqueeze(1).broadcast_to([P, CT, TILES])
        with st.block() as block:
            @block.sync
            def _(sp):
                for s in range(2):
                    sp.dma_start(raw[:, s, 0, :].rearrange("p (c t) -> p c t", t=CT),
                                 keys[s].rearrange("(c p t) -> p c t", p=P, t=CT)).then_inc(loaded, 16)

            @block.vector
            def _(dve):
                ch = Chain(dve, chain)
                ch.add(nc.vector.memset(zero[:], 0.0))
                dve.wait_ge(loaded, 32)
                ch.add(nc.vector.tensor_scalar(raw[:, :, 1, :], raw[:, :, 0, :], P - 1, None, ALU.bitwise_and))
                ch.add(nc.vector.tensor_scalar(raw[:, :, 2, :], raw[:, :, 0, :], 7, None, ALU.logical_shift_right))
                ch.settle()
                ch.link(nc.vector.tensor_copy(split[:], raw[:]))
                dve.sem_inc(opened, 1)
                for s in range(2):
                    with ch.loop(CHUNKS // 2, 4) as i:
                        for q in range(2):
                            dve.wait_ge(used, i * 2 + q + s * CHUNKS + 1)
                            at = bass.ds((i * 2 + q) * CT, CT)
                            ch.add(nc.vector.tensor_tensor(lo_hot[:, q], iota, split[:, s, 1, at].unsqueeze(2).broadcast_to([P, CT, P]), ALU.is_equal))
                            ch.add(nc.vector.tensor_tensor(hi_hot[:, q], iota25, split[:, s, 2, at].unsqueeze(2).broadcast_to([P, CT, TILES]), ALU.is_equal))
                            ch.settle()
                            dve.sem_inc(hot, 1)
                dve.wait_ge(counted, 2)
                ch.link(nc.vector.tensor_copy(count[:], ps[:, 0:2, 0:TILES]))
                dve.sem_inc(opened, 1)
                dve.wait_ge(summed, 1)
                ch.link(nc.vector.tensor_copy(total[:], ps[:, 4:6, 0:TILES]))
                for s in range(2):
                    ch.add(nc.vector.tensor_tensor_scan(run[:, s], total[:, s], total[:, s], 0.0, ALU.add, ALU.max))
                ch.settle()
                ch.link(nc.vector.tensor_tensor(run[:], run[:], total[:], ALU.subtract))
                ch.link(nc.vector.tensor_tensor(base[:], ps[:, 2:4, 0:TILES], run[:], ALU.add))

            @block.tensor
            def _(pe):
                pe.sem_inc(used, 2)
                pe.wait_ge(opened, 1)
                for s in range(2):
                    nc.tensor.matmul(ps[:, s, 0:TILES], zero[:], zero[:, 0:TILES], start=True, stop=False)
                    with pe.Fori(0, CHUNKS // 2) as i:
                        for q in range(2):
                            pe.wait_ge(hot, i * 2 + q + s * CHUNKS + 1)
                            for t in range(CT):
                                last = nc.tensor.matmul(ps[:, s, 0:TILES], lo_hot[:, q, t, :], hi_hot[:, q, t, :], start=False, stop=False)
                            last.then_inc(used, 1)
                    nc.tensor.matmul(ps[:, s, 0:TILES], zero[:], zero[:, 0:TILES], start=False, stop=True).then_inc(counted, 1)
                pe.wait_ge(opened, 2)
                for s in range(2):
                    nc.tensor.matmul(ps[:, 2 + s, 0:TILES], core.c("lt"), count[:, s], start=True, stop=True)
                    last = nc.tensor.matmul(ps[:, 4 + s, 0:TILES], core.c("ones"), count[:, s], start=True, stop=True)
                last.then_inc(summed, 1)


def sort_stage(core, split, base, attributes, rbf, by_dst, by_src):
    NG = rbf.shape[1]
    PAIRS = CHUNKS // 2
    with Stage(core, "sort") as st:
        nc, ps = core.nc, core.ps
        own = st.sb("own", [P, 2, 2, 3, CT])
        lo_hot = st.sb("lo_hot", [P, 2, 2, CT, P])
        hi_hot = st.sb("hi_hot", [P, 2, 2, CT, TILES])
        lo_hot_t = st.sb("lo_hot_t", [P, 2, 2, P])
        running = st.sb("running", [P, 2, 2, TILES])
        scrap = st.sb("scrap", [P, 4, P])
        picked = st.sb("picked", [P, 2, CT, TILES])
        rank = st.sb("rank", [P, 2, CT])
        before = st.sb("before", [P, 2, CT])
        place = st.sb("place", [P, 2, 2, CT], I32)
        row = [st.sb("row_dst", [P, 2, CT, D + 2]), st.sb("row_src", [P, 2, CT, NG + 2])]
        width = (D, NG)
        loaded = [st.sem("loaded0"), st.sem("loaded1")]
        scattered = [st.moved(q, CHUNKS // 2 * 2 * CT) for q in range(2)]
        names = ("chain", "hot", "keys_turned", "ranked", "hot_turned", "hot_copied", "snapped", "looked", "look_free",
                 "counted", "placed", "row_free", "pool_passed")
        (chain, hot, keys_turned, ranked, hot_turned, hot_copied, snapped, looked, look_free,
         counted, placed, row_free, pool_passed) = map(st.sem, names)
        RUN, LOOK, KEYS, HOT = 0, (1, 2), (3, 4), (5, 6)
        ident = core.c("ident")

        def pairs(eng, body, loop=None):
            with (loop or (lambda: eng.Fori(0, PAIRS - 1)))() as i:
                body(i, True)
            body(PAIRS - 1, False)

        with st.block() as block:
            @block.sync
            def _(sp):
                def chunk(i, q, first):
                    c = i * 2 + q
                    of = lambda rows_: rows_[bass.ds(c * CHUNK, CHUNK), :].rearrange("(p t) d -> p t d", t=CT)
                    if not first:
                        scattered[q].wait(sp, i * 2 * CT * 16)
                    sp.sem_inc(row_free, 1)
                    sp.dma_start(row[0][:, q, :, 0:D], of(attributes)).then_inc(loaded[q], 16)
                    sp.dma_start(row[1][:, q, :, 0:NG], of(rbf)).then_inc(loaded[q], 16)

                for q in range(2):
                    chunk(0, q, True)
                with sp.Fori(0, PAIRS - 1) as i:
                    for q in range(2):
                        chunk(i + 1, q, False)
                for q in range(2):
                    scattered[q].wait(sp, PAIRS * 2 * CT * 16)

            @block.gpsimd
            def _(pool):
                with pool.Fori(0, PAIRS) as i:
                    for q in range(2):
                        c = i * 2 + q
                        pool.wait_ge(placed, c + 1)
                        pool.wait_ge(loaded[q], (i + 1) * 32)
                        pool.sem_inc(pool_passed, 1)
                        for t in range(CT):
                            for s, table in ((0, by_dst), (1, by_src)):
                                scattered[q].count(nc.gpsimd.indirect_dma_start(out=table, out_offset=bass.IndirectOffsetOnAxis(ap=place[:, q, s, t:t + 1], axis=0),
                                                             in_=row[s][:, q, t, :], in_offset=None,
                                                             bounds_check=EPAD - 1, oob_is_err=False))

            @block.tensor
            def _(pe):
                pe.sem_inc(looked, 1)

                def turn(q, t, i):
                    if t == 0:
                        pe.wait_ge(hot, i * 2 + q + 1)
                    for s in range(2):
                        last = nc.tensor.transpose(ps[:, HOT[t % 2], s * P:(s + 1) * P], lo_hot[:, q, s, t, :], ident)
                    last.then_inc(hot_turned, 1)

                turn(0, 0, 0)
                nc.tensor.matmul(ps[:, RUN, 0:2 * TILES], ident, base[:].rearrange("p s a -> p (s a)"), start=True, stop=True, skip_group_check=True).then_inc(counted, 1)

                def body(i, more):
                    for q in range(2):
                        c = i * 2 + q
                        for t in range(CT):
                            n = c * CT + t
                            if t % 2 == 0:
                                pe.wait_ge(ranked, c * (CT // 2) + t // 2 + 1)
                                for u in range(4):
                                    last = nc.tensor.transpose(ps[:, KEYS[t // 2 % 2], u * P:(u + 1) * P],
                                                               own[:, q, u % 2, 0, t + u // 2:t + u // 2 + 1].broadcast_to([P, P]), ident)
                                last.then_inc(keys_turned, 1)
                            pe.wait_ge(snapped, n + 1)
                            for s in range(2):
                                last = nc.tensor.matmul(ps[:, RUN, s * TILES:(s + 1) * TILES], lo_hot[:, q, s, t, :], hi_hot[:, q, s, t, :],
                                                        start=False, stop=True, skip_group_check=True)
                            last.then_inc(counted, 1)
                            if t < CT - 1:
                                turn(q, t + 1, i)
                            elif more or q == 0:
                                turn(1 - q, 0, i + q)
                            pe.wait_ge(hot_copied, n + 1)
                            if t == 0:
                                pe.wait_ge(look_free, c + 1)
                            for s in range(2):
                                last = nc.tensor.matmul(ps[:, LOOK[s], t * TILES:(t + 1) * TILES], lo_hot_t[:, t % 2, s, :], running[:, t % 2, s, :],
                                                        start=True, stop=True)
                            last.then_inc(looked, 1)

                pairs(pe, body)

            @block.scalar
            def _(act):
                def take(t, n, first=False):
                    act.wait_ge(counted, n + 1)
                    if not first:
                        act.wait_ge(looked, n)
                    nc.scalar.copy(running[:, t % 2], ps[:, RUN, 0:2 * TILES].rearrange("p (s a) -> p s a", s=2)).then_inc(snapped, 1)
                    act.wait_ge(hot_turned, n + 1)
                    nc.scalar.copy(lo_hot_t[:, t % 2], ps[:, HOT[t % 2], 0:2 * P].rearrange("p (s e) -> p s e", s=2)).then_inc(hot_copied, 1)

                take(0, 0, True)

                def body(i, more):
                    for t in range(2 * CT):
                        if more or t < 2 * CT - 1:
                            take(t + 1, i * 2 * CT + t + 1)

                pairs(act, body)

            @block.vector
            def _(dve):
                ch = Chain(dve, chain)
                dve.sem_inc(ranked, 2)
                dve.sem_inc(look_free, 1)

                def start_hot(q, i):
                    c = i * 2 + q
                    ch.link(nc.vector.tensor_scalar(own[:, q], split[:, :, :, bass.ds(c * CT, CT)], 1.0, None, ALU.mult))
                    for s in range(2):
                        ch.add(nc.vector.tensor_tensor(hi_hot[:, q, s], core.c("iota25").unsqueeze(1).broadcast_to([P, CT, TILES]),
                                                       own[:, q, s, 2].unsqueeze(2).broadcast_to([P, CT, TILES]), ALU.is_equal))

                def one_hot(q, t):
                    for s in range(2):
                        ch.add(nc.vector.tensor_scalar(lo_hot[:, q, s, t, :], core.c("iota"), own[:, q, s, 1, t:t + 1], None, ALU.is_equal))

                start_hot(0, 0)
                for t in range(CT):
                    one_hot(0, t)
                ch.settle()
                dve.sem_inc(hot, 1)

                def body(i, more):
                    for q in range(2):
                        c = i * 2 + q
                        ahead = more or q == 0
                        if ahead:
                            dve.wait_ge(counted, c * CT + 1)
                            start_hot(1 - q, i + q)
                        dve.wait_ge(row_free, c + 1)
                        for s in range(2):
                            for e in range(2):
                                ch.add(nc.vector.tensor_scalar(row[s][:, q, :, width[s] + e], split[:, (s + e) % 2, 0, bass.ds(c * CT, CT)], 1.0, None, ALU.mult))
                        for t in range(CT):
                            if ahead:
                                one_hot(1 - q, t)
                                if t == CT - 1:
                                    ch.settle()
                                    dve.sem_inc(hot, 1)
                            if t % 2 == 0:
                                dve.wait_ge(keys_turned, c * (CT // 2) + t // 2 + 1)
                            for s in range(2):
                                u = t % 2 * 2 + s
                                ch.add(nc.vector.scalar_tensor_tensor(scrap[:, u], ps[:, KEYS[t // 2 % 2], u * P:(u + 1) * P], own[:, q, s, 0, t:t + 1],
                                                                      core.c("before"), ALU.is_equal, ALU.mult, accum_out=rank[:, s, t:t + 1]))
                            if t % 2 == 1:
                                ch.settle()
                                dve.sem_inc(ranked, 1)
                        dve.wait_ge(looked, c * CT + CT + 1)
                        ch.link(nc.vector.tensor_tensor(picked[:], ps[:, LOOK[0]:LOOK[1] + 1, 0:CT * TILES].rearrange("p s (t a) -> p s t a", a=TILES), hi_hot[:, q], ALU.mult))
                        dve.sem_inc(look_free, 1)
                        ch.link(nc.vector.tensor_reduce(before[:], picked[:], AX, ALU.add))
                        ch.link(nc.vector.tensor_tensor(before[:], before[:], rank[:], ALU.add))
                        ch.link(nc.vector.tensor_copy(place[:, q], before[:]))
                        dve.sem_inc(placed, 1)

                pairs(dve, body, lambda: ch.loop(PAIRS - 1, 2 * (3 + 2 * CT + 4 + 2 * CT + 4)))


def project_stage(core, xt, weights, biases, q_table, kv_table):
    with Stage(core, "p1") as st:
        nc, ps, x = core.nc, core.ps, core.x
        w_sb, b_sb = st.sb("w", [P, 4, KD, D]), st.sb("b", [P, 4, D])
        out = st.sb("out", [P, 3, TILES, D])
        skip = st.sb("skip", [P, D])
        loaded, chain, projected, bank_free, stored = (st.sem(s) for s in ("loaded", "chain", "projected", "bank_free", "stored"))
        with st.block() as block:
            @block.sync
            def _(sp):
                for i in range(4):
                    sp.dma_start(w_sb[:, i], rows(weights[i])).then_inc(loaded, 16)
                    sp.dma_start(b_sb[:, i], bcast(biases[i])).then_inc(loaded, 16)
                sp.wait_ge(bank_free, 4 * TILES + 4)
                sp.dma_start(q_table.rearrange("(a p) d -> p a d", p=P), out[:, 0]).then_inc(stored, 16)
                for i in range(2):
                    sp.dma_start(kv_table[:, i * D:(i + 1) * D].rearrange("(a p) d -> p a d", p=P), out[:, 1 + i]).then_inc(stored, 16)
                sp.wait_ge(stored, 48)

            @block.tensor
            def _(pe):
                pe.sem_inc(bank_free, 4)
                pe.wait_ge(loaded, 128)
                for a in range(TILES):
                    for i in range(4):
                        pe.wait_ge(bank_free, a * 4 + i + 1)
                        for k in range(KD):
                            last = nc.tensor.matmul(ps[:, i, 0:D], xt[:, k, a * P:(a + 1) * P], w_sb[:, i, k, :], start=(k == 0), stop=(k == KD - 1))
                        last.then_inc(projected, 1)

            @block.vector
            def _(dve):
                ch = Chain(dve, chain)
                dve.wait_ge(loaded, 128)
                with ch.loop(TILES, 2) as a:
                    for i in range(3):
                        dve.wait_ge(projected, a * 4 + i + 1)
                        nc.vector.tensor_tensor(out[:, i, bass.ds(a, 1), :].rearrange("p a d -> p (a d)"), ps[:, i, 0:D], b_sb[:, i], ALU.add).then_inc(bank_free, 1)
                    dve.wait_ge(projected, a * 4 + 4)
                    ch.link(nc.vector.tensor_tensor(skip[:], ps[:, 3, 0:D], b_sb[:, 3], ALU.add))
                    dve.sem_inc(bank_free, 1)
                    xa = x[:, bass.ds(a, 1), :].rearrange("p a d -> p (a d)")
                    ch.link(nc.vector.tensor_tensor(xa, xa, skip[:], ALU.add))


def attend_stage(core, name, ends, src_table, dst_table, edge_rows, partial, scale, edge_weight=None):
    SW = src_table.shape[1]
    TABLES = 2 if edge_rows is not None else 1
    SAMEQ = 1 if edge_rows is not None else 8
    STEPS = 3 if edge_rows is not None else 2
    QUARTERS, BODY, LAG, AHEAD = CHUNKS * 4, 8, 5, 2
    RINGQ = 4 if edge_rows is not None else 8
    with Stage(core, name) as st:
        nc, ps = core.nc, core.ps
        if edge_rows is not None:
            edge = st.sb("edge", [P, 4, 4, D + 2])
            values = st.sb("values", [P, BODY, 4, D])
            prod = st.sb("prod", [P, 4, D])
            w_sb = st.sb("w", [P, KD, D])
            edge_t = st.sb("edge_t", [P, 2, KD, P])
            edge_loaded = [st.sem(f"edge_loaded{k}") for k in range(4)]
            w_loaded, edge_turned, edge_copied, projected, e_free = (st.sem(x) for x in ("w_loaded", "edge_turned", "edge_copied", "projected", "e_free"))
            keyed, queried, scored = (st.sem(x) for x in ("keyed", "queried", "scored"))
        far = st.sb("far", [P, RINGQ, 4, SW])
        if edge_rows is not None:
            near = st.sb("near", [P, RINGQ, 4, D])
        else:
            first = st.sb("first", [P, ETILES, HEADS])
            first_loaded, near_ready = st.sem("first_loaded"), st.sem("near_ready")
        index = st.sb("index", [P, BODY, 2, 4], I32)
        node = st.sb("node", [P, BODY, 4])
        alpha = st.sb("alpha", [P, 2, CT, HEADS])
        raw = st.sb("raw", [P, 4, HEADS])
        node_by_head = st.sb("node_by_head", [P, CT, HEADS])
        node_t = st.sb("node_t", [P, P])
        fresh = st.sb("fresh", [P, P + 1])
        up, down = st.sb("up", [P, P]), st.sb("down", [P, P])
        tops = st.sb("tops", [P, 2, CT, HEADS])
        centre = st.sb("centre", [P, CT, HEADS])
        weight = st.sb("weight", [P, 2, CT, HEADS])
        same = st.sb("same", [P, SAMEQ, 4, P])
        msg = st.sb("msg", [P, 4, SEG])
        out = st.sb("out", [P, 2, 4, ROW])
        gathered = [st.moved(k, QUARTERS // RINGQ * TABLES * 4) for k in range(RINGQ)]
        stored = [st.sem("stored0"), st.sem("stored1")]
        chain, indexed, ring_free, alpha_ready, turned, node_copied, top_ready, top_turned = (
            st.sem(x) for x in ("chain", "indexed", "ring_free", "alpha_ready", "turned", "node_copied", "top_ready", "top_turned"))
        centred, weighed, keys_turned, msg_ready, summed, copied, marked, pool_passed = (
            st.sem(x) for x in ("centred", "weighed", "keys_turned", "msg_ready", "summed", "copied", "marked", "pool_passed"))
        same_made = st.sem("same_made")
        SCORES, NODES, TOPS = (ps[:, 0, k * P:(k + 1) * P] for k in range(3))
        KEYS, TURNED, PROJ, SUMS = (1, 2), 3, (4, 5), (6, 7)
        BODIES = QUARTERS // BODY
        ident = core.c("ident")

        def run(eng, quarter, loop=None):
            for b in range(BODY):
                quarter(0, b, True, b >= LAG)
            with (loop or (lambda: eng.Fori(0, BODIES - 2)))() as i:
                for b in range(BODY):
                    quarter(i + 1, b, True, True)
            for b in range(BODY):
                quarter(BODIES - 1, b, True, True)
            for b in range(LAG):
                quarter(BODIES, b, False, True)

        def chunk_before(i, b):
            if b % 4 or isinstance(i, int) and not 0 <= i * 2 + b // 4 - 1 < CHUNKS:
                return None
            return i * 2 + b // 4 - 1

        def slot_of(b):
            return (b - LAG) % BODY

        with st.block() as block:
            @block.sync
            def _(sp):
                if edge_rows is None:
                    sp.dma_start(first[:], dst_table).then_inc(first_loaded, 16)
                else:
                    sp.dma_start(w_sb[:], rows(edge_weight)).then_inc(w_loaded, 16)
                    with sp.Fori(0, BODIES) as i:
                        for b in range(BODY):
                            m = i * BODY + b
                            sp.wait_ge(edge_turned, m * 4 + 4)
                            sp.dma_start(edge[:, b % 4], edge_rows[bass.ds(m * (4 * P), 4 * P), :].rearrange("(t p) d -> p t d", p=P)).then_inc(edge_loaded[b % 4], 16)

            @block.gpsimd
            def _(pool):
                with pool.Fori(0, BODIES) as i:
                    for b in range(BODY):
                        m = i * BODY + b
                        pool.wait_ge(indexed, m + 1)
                        pool.wait_ge(ring_free, m + 1)
                        pool.sem_inc(pool_passed, 1)
                        for u in range(4):
                            for to, table, e in (((near, dst_table, 0),) if edge_rows is not None else ()) + ((far, src_table, 1),):
                                gathered[b % RINGQ].count(nc.gpsimd.indirect_dma_start(out=to[:, b % RINGQ, u, :], out_offset=None, in_=table,
                                                             in_offset=bass.IndirectOffsetOnAxis(ap=index[:, b, e, u:u + 1], axis=0),
                                                             bounds_check=NPAD - 1, oob_is_err=False))

            @block.tensor
            def _(pe):
                def turn_edges(i, b, u):
                    if u == 0:
                        pe.wait_ge(indexed, i * BODY + b + 1)
                    for k in range(KD):
                        last = nc.tensor.transpose(ps[:, TURNED, k * P:(k + 1) * P], edge[:, b % 4, u, k * P:(k + 1) * P], ident)
                    last.then_inc(edge_turned, 1)

                def turn_keys(s):
                    for u in range(4):
                        last = nc.tensor.transpose(ps[:, KEYS[s % 2], u * P:(u + 1) * P], node[:, s, u:u + 1].broadcast_to([P, P]), ident)
                    last.then_inc(keys_turned, 1)

                def project(i, b, u):
                    n = i * (4 * BODY) + b * 4 + u
                    pe.wait_ge(edge_copied, n + 1)
                    pe.wait_ge(e_free, n + 1)
                    for k in range(KD):
                        last = nc.tensor.matmul(ps[:, PROJ[u % 2], 0:D], edge_t[:, u % 2, k, :], w_sb[:, k, :], start=(k == 0), stop=(k == KD - 1))
                    last.then_inc(projected, 1)

                if edge_rows is not None:
                    pe.sem_inc(edge_turned, 16)
                    pe.sem_inc(projected, 1)
                    pe.wait_ge(w_loaded, 16)
                    turn_edges(0, 0, 0)
                    project(0, 0, 0)
                else:
                    pe.wait_ge(first_loaded, 16)
                    pe.wait_ge(indexed, 1)
                    turn_keys(0)

                def quarter(i, b, scores, sums):
                    c = chunk_before(i, b)
                    if c is not None:
                        h = (b // 4 - 1) % 2
                        pe.wait_ge(alpha_ready, c + 1)
                        nc.tensor.transpose(SCORES, alpha[:, h].rearrange("p t h -> p (t h)"), ident)
                        nc.tensor.transpose(NODES, node_by_head[:].rearrange("p t h -> p (t h)"), ident).then_inc(turned, 1)
                    if edge_rows is None and scores:
                        pe.wait_ge(same_made, i * BODY + b + 1)
                        for u in range(4):
                            last = nc.tensor.matmul(ps[:, PROJ[b % 2], u * HEADS:(u + 1) * HEADS], same[:, b, u, :],
                                                    first[:, bass.ds(i * (4 * BODY) + b * 4 + u, 1), :], start=True, stop=True)
                        last.then_inc(near_ready, 1)
                    for u in range(4):
                        n = i * (4 * BODY) + (b - LAG) * 4 + u
                        ahead = edge_rows is not None and scores and not (isinstance(i, int) and i * BODY + b == QUARTERS - 1 and u == 3)
                        nxt = (i + (b * 4 + u + 1) // (4 * BODY), (b + (u + 1) // 4) % BODY, (u + 1) % 4)
                        if ahead:
                            turn_edges(*nxt)
                            project(*nxt)
                        if u == 1 and c is not None:
                            pe.wait_ge(top_ready, c + 1)
                            nc.tensor.transpose(TOPS, down[:], ident).then_inc(top_turned, 1)
                        if sums:
                            pe.wait_ge(msg_ready, n * STEPS + STEPS)
                            pe.wait_ge(copied, n + 1)
                            nc.tensor.matmul(ps[:, SUMS[u % 2], 0:SEG], same[:, slot_of(b) % SAMEQ, u, :], msg[:, u, :], start=True, stop=True).then_inc(summed, 1)
                    if edge_rows is not None:
                        if not isinstance(i, int) or 0 <= i * BODY + b - LAG + 1 < QUARTERS:
                            turn_keys((b - LAG + 1) % BODY)
                    elif not isinstance(i, int) or i * BODY + b + 1 < QUARTERS:
                        pe.wait_ge(indexed, i * BODY + b + 2)
                        turn_keys((b + 1) % BODY)

                run(pe, quarter)

            @block.scalar
            def _(act):
                act.sem_inc(copied, 2)
                for s in range(2):
                    act.sem_inc(stored[s], 16)

                def copy_edges(i, b, u, first=False):
                    n = i * (4 * BODY) + b * 4 + u
                    act.wait_ge(edge_turned, n + 1 + 16)
                    if not first:
                        act.wait_ge(projected, n)
                    nc.scalar.copy(edge_t[:, u % 2], ps[:, TURNED, 0:D].rearrange("p (k e) -> p k e", k=KD)).then_inc(edge_copied, 1)

                if edge_rows is not None:
                    copy_edges(0, 0, 0, True)

                def quarter(i, b, scores, sums):
                    c = chunk_before(i, b)
                    if c is not None:
                        act.wait_ge(turned, c + 1)
                        nc.scalar.copy(node_t[:], NODES).then_inc(node_copied, 1)
                    s = slot_of(b) % 2
                    m = i * BODY + b - LAG
                    for u in range(4):
                        if edge_rows is not None and scores and not (isinstance(i, int) and i * BODY + b == QUARTERS - 1 and u == 3):
                            copy_edges(i + (b * 4 + u + 1) // (4 * BODY), (b + (u + 1) // 4) % BODY, (u + 1) % 4)
                        if sums:
                            if u == 0:
                                act.wait_ge(stored[s], (i * 4 + (b - LAG) // 2) * 16 + 16)
                            act.wait_ge(summed, m * 4 + u + 1)
                            nc.scalar.copy(out[:, s, u, 0:SEG], ps[:, SUMS[u % 2], 0:SEG]).then_inc(copied, 1)
                        if u == 2 and c is not None:
                            act.wait_ge(centred, c + 1)
                            nc.scalar.activation(weight[:, (b // 4 - 1) % 2], centre[:], ACT.Exp, scale=scale).then_inc(weighed, 1)
                    if sums:
                        act.wait_ge(copied, m * 4 + 4 + 2)
                        act.wait_ge(marked, m * 2 + 2)
                        act.dma_start(partial[bass.ds(m * (4 * P), 4 * P), :].rearrange("(t p) d -> p t d", p=P), out[:, s]).then_inc(stored[s], 16)

                run(act, quarter)
                for s in range(2):
                    act.wait_ge(stored[s], QUARTERS // 2 * 16 + 16)

            @block.vector
            def _(dve):
                ch = Chain(dve, chain)
                dve.sem_inc(ring_free, RINGQ)
                if edge_rows is not None:
                    dve.sem_inc(e_free, 2)
                    dve.sem_inc(scored, 3)
                ch.link(nc.vector.memset(fresh[:], 0.0))
                heads = lambda v: v.rearrange("p (h c) -> p h c", h=HEADS)

                def prepare(i, b):
                    at = bass.ds(i * (4 * BODY) + b * 4, 4)
                    if edge_rows is not None:
                        dve.wait_ge(edge_loaded[b % 4], (i * 2 + b // 4) * 16 + 16)
                        both = edge[:, b % 4, :, D:D + 2].rearrange("p t e -> p e t")
                        ch.add(nc.vector.tensor_scalar(ends[:, :, at], both, 1.0, None, ALU.mult))
                        ch.add(nc.vector.tensor_copy(index[:, b], both))
                        ch.add(nc.vector.tensor_copy(node[:, b], edge[:, b % 4, :, D]))
                    else:
                        ch.add(nc.vector.tensor_scalar(index[:, b], ends[:, :, at], 1.0, None, ALU.mult))
                        ch.add(nc.vector.tensor_scalar(node[:, b], ends[:, 0, at], 1.0, None, ALU.mult))
                    ch.settle()
                    dve.sem_inc(indexed, 1)

                def sum_score(i, b, u):
                    dve.wait_ge(queried, i * (4 * BODY) + b * 4 + u + 1)
                    nc.vector.tensor_reduce(alpha[:, b // 4, (b % 4) * 4 + u, :], heads(prod[:, u, :]), AX, ALU.add).then_inc(scored, 1)

                def quarter(i, b, scores, sums):
                    c = chunk_before(i, b)
                    h = (b // 4 - 1) % 2
                    r, s = b % RINGQ, slot_of(b)
                    if not isinstance(i, int) or i * BODY + b + AHEAD < QUARTERS:
                        prepare(i + (b + AHEAD) // BODY, (b + AHEAD) % BODY)
                    if scores:
                        if edge_rows is None:
                            dve.wait_ge(keys_turned, i * BODY + b + 1)
                            for u in range(4):
                                ch.add(nc.vector.scalar_tensor_tensor(same[:, b, u, :], ps[:, KEYS[b % 2], u * P:(u + 1) * P], node[:, b, u:u + 1],
                                                                      core.c("le"), ALU.is_equal, ALU.mult))
                            ch.settle()
                            dve.sem_inc(same_made, 1)
                        else:
                            gathered[r].wait(dve, (i * (BODY // RINGQ) + b // RINGQ) * 128 + 128)
                    if sums and (b - LAG) % 4 == 0:
                        dve.wait_ge(weighed, i * 2 + (b - LAG) // 4 + 1)
                    for u in range(4):
                        n = i * (4 * BODY) + (b - LAG) * 4 + u
                        if scores and edge_rows is not None:
                            p_, e_ = prod[:, u, :], ps[:, PROJ[u % 2], 0:D]
                            k = i * (4 * BODY) + b * 4 + u
                            dve.wait_ge(projected, k + 2)
                            dve.wait_ge(scored, k + 1)
                            nc.vector.tensor_tensor(p_, e_, far[:, r, u, 0:D], ALU.add).then_inc(keyed, 1)
                            if u > 0:
                                sum_score(i, b, u - 1)
                        if sums:
                            if u == 0:
                                if edge_rows is not None:
                                    dve.wait_ge(keys_turned, i * BODY + b - LAG + 1)
                                dve.wait_ge(stored[s % 2], (i * 4 + (b - LAG) // 2) * 16 + 16)
                                at = slice((s % 4) * 4, (s % 4) * 4 + 4)
                                nc.vector.tensor_copy(out[:, s % 2, :, SEG:ROW - 1], tops[:, s // 4, at, :]).then_inc(marked, 1)
                                nc.vector.tensor_copy(out[:, s % 2, :, ROW - 1], node[:, s]).then_inc(marked, 1)
                            if not (isinstance(i, int) and n < 4):
                                dve.wait_ge(summed, n - 3)
                            if edge_rows is not None:
                                nc.vector.scalar_tensor_tensor(same[:, 0, u, :], ps[:, KEYS[s % 2], u * P:(u + 1) * P], node[:, s, u:u + 1],
                                                               core.c("le"), ALU.is_equal, ALU.mult).then_inc(msg_ready, 1)
                            value = values[:, s, u] if edge_rows is not None else far[:, s, u, 0:D]
                            w = weight[:, s // 4, (s % 4) * 4 + u, :]
                            nc.vector.tensor_copy(msg[:, u, D:SEG], w).then_inc(msg_ready, 1)
                            nc.vector.tensor_tensor(heads(msg[:, u, 0:D]), heads(value), w.unsqueeze(2).broadcast_to([P, HEADS, HD]), ALU.mult).then_inc(msg_ready, 1)
                        if scores and edge_rows is not None:
                            dve.wait_ge(keyed, k + 1)
                            nc.vector.tensor_tensor(p_, p_, near[:, r, u, :], ALU.mult).then_inc(queried, 1)
                            nc.vector.tensor_tensor(values[:, b, u], e_, far[:, r, u, D:2 * D], ALU.add).then_inc(e_free, 1)
                            if u == 3:
                                sum_score(i, b, u)
                        if c is not None and u == 0:
                            dve.wait_ge(node_copied, c + 1)
                            ch.link(nc.vector.tensor_tensor(fresh[:, 1:P], node_t[:, 1:P], node_t[:, 0:P - 1], ALU.not_equal))
                            ch.link(nc.vector.tensor_scalar(fresh[:, 1:P], fresh[:, 1:P], -BIG, None, ALU.mult))
                            ch.link(nc.vector.tensor_tensor_scan(up[:], fresh[:, 0:P], SCORES, -BIG, ALU.add, ALU.max))
                            ch.link(nc.vector.tensor_tensor_scan(down[:, ::-1], fresh[:, 1:P + 1][:, ::-1], up[:, ::-1], -BIG, ALU.add, ALU.max))
                            dve.sem_inc(top_ready, 1)
                        if c is not None and u == 1:
                            dve.wait_ge(top_turned, c + 1)
                            both = TOPS.rearrange("p (t h) -> p t h", h=HEADS)
                            ch.add(nc.vector.tensor_tensor(centre[:], alpha[:, h], both, ALU.subtract))
                            ch.add(nc.vector.tensor_copy(tops[:, h], both))
                            ch.settle()
                            dve.sem_inc(centred, 1)
                    if edge_rows is not None:
                        if scores:
                            dve.wait_ge(e_free, i * (4 * BODY) + b * 4 + 4 + 2)
                            dve.sem_inc(ring_free, 1)
                    if edge_rows is None and sums:
                        dve.wait_ge(msg_ready, (i * BODY + b - LAG + 1) * (4 * STEPS))
                        dve.sem_inc(ring_free, 1)
                    if edge_rows is None and scores:
                        gathered[r].wait(dve, i * 64 + 64)
                        dve.wait_ge(near_ready, i * BODY + b + 1)
                        ch.link(nc.vector.tensor_tensor(raw[:], far[:, r, :, D:SW], ps[:, PROJ[b % 2], 0:4 * HEADS].rearrange("p (t h) -> p t h", h=HEADS), ALU.add))
                        ch.link(nc.vector.scalar_tensor_tensor(alpha[:, b // 4, (b % 4) * 4:(b % 4) * 4 + 4, :], raw[:], 0.2, raw[:], ALU.mult, ALU.max))
                    if scores and b % 4 == 3:
                        ch.settle()
                        if edge_rows is not None:
                            dve.wait_ge(scored, i * (4 * BODY) + b * 4 + 4 + 3)
                        ch.link(nc.vector.tensor_scalar(node_by_head[:], node[:, b - 3:b + 1, :].rearrange("p q t -> p (q t)").unsqueeze(2).broadcast_to([P, CT, HEADS]), 1.0, None, ALU.mult))
                        dve.sem_inc(alpha_ready, 1)

                for b in range(AHEAD):
                    prepare(0, b)
                per = BODY * (3 if edge_rows is not None else 8) + 2 * (4 + 2 + 1)
                run(dve, quarter, lambda: ch.loop(BODIES - 2, per))


def starts_stage(core, base, count, by_dst, node_rows, table):
    W = node_rows.shape[1]
    with Stage(core, "starts") as st:
        nc = core.nc
        zero = st.sb("zero", [P, ETILES * W])
        own = st.sb("own", [P, TILES, W])
        f = st.sb("f", [P, 3, TILES])
        at = st.sb("at", [P, 3, TILES], I32)
        key, key_i = st.sb("key", [QT, 4, 1]), st.sb("key_i", [QT, 4], I32)
        opening = st.sb("opening", [QT, 4, W])
        loaded, chain, zeroed, cleared, indexed, stored = (st.sem(x) for x in ("loaded", "chain", "zeroed", "cleared", "indexed", "stored"))
        gathered, scattered = st.moved(0, 4), st.moved(1, TILES)
        flat = table.rearrange("p t w -> (p t) w")
        with st.block() as block:
            @block.sync
            def _(sp):
                sp.dma_start(own[:], node_rows.rearrange("(a p) w -> p a w", p=P)).then_inc(loaded, 16)
                sp.dma_start(key[:], by_dst.rearrange("(q p r) w -> p q r w", q=4, r=P)[:, :, 0, D:D + 1], allow_slow_non_contiguous=True).then_inc(loaded, 16)
                sp.wait_ge(zeroed, 1)
                sp.dma_start(table.rearrange("p t w -> p (t w)"), zero[:]).then_inc(cleared, 16)
                gathered.wait(sp, 4 * 16)
                scattered.wait(sp, TILES * 16)
                sp.dma_start(table[0].rearrange("(q p) w -> p q w", q=4), opening[:]).then_inc(stored, 16)
                sp.wait_ge(stored, 16)

            @block.vector
            def _(dve):
                ch = Chain(dve, chain)
                nc.vector.memset(zero[:], 0.0).then_inc(zeroed, 1)
                ch.link(nc.vector.tensor_copy(at[:, 0], base[:, 0]))
                ch.link(nc.vector.tensor_scalar(at[:, 1], at[:, 0], 7, None, ALU.logical_shift_right))
                ch.link(nc.vector.tensor_scalar(at[:, 0], at[:, 0], P - 1, None, ALU.bitwise_and))
                ch.link(nc.vector.tensor_copy(f[:, 0:2], at[:, 0:2]))
                ch.link(nc.vector.scalar_tensor_tensor(f[:, 0], f[:, 0], float(ETILES), f[:, 1], ALU.mult, ALU.add))
                ch.link(nc.vector.tensor_scalar(f[:, 1], count[:, 0], 0.0, None, ALU.is_equal))
                ch.link(nc.vector.scalar_tensor_tensor(f[:, 2], f[:, 1], float(EPAD), f[:, 0], ALU.mult, ALU.max))
                ch.link(nc.vector.tensor_copy(at[:, 2], f[:, 2]))
                dve.wait_ge(loaded, 32)
                ch.link(nc.vector.tensor_copy(key_i[:], key[:, :, 0]))
                dve.sem_inc(indexed, 1)

            @block.gpsimd
            def _(pool):
                pool.wait_ge(indexed, 1)
                pool.wait_ge(cleared, 16)
                for q in range(4):
                    gathered.count(nc.gpsimd.indirect_dma_start(out=opening[:, q, :], out_offset=None, in_=node_rows,
                                                 in_offset=bass.IndirectOffsetOnAxis(ap=key_i[:, q:q + 1], axis=0),
                                                 bounds_check=NPAD - 1, oob_is_err=False))
                for a in range(TILES):
                    scattered.count(nc.gpsimd.indirect_dma_start(out=flat, out_offset=bass.IndirectOffsetOnAxis(ap=at[:, 2, a:a + 1], axis=0),
                                                 in_=own[:, a, :], in_offset=None,
                                                 bounds_check=EPAD - 1, oob_is_err=False))


def filter_stage(core, name, edge_rows, table, wf1, bf1, wf2, bf2, partial):
    NG = wf1.shape[0]
    NG4 = 4 * NG
    with Stage(core, name) as st:
        nc, ps = core.nc, core.ps
        w1_raw, w1_sb, b1_sb, w2_sb = st.sb("w1_raw", [NG4, D]), st.sb("w1", [NG4, D], F32R), st.sb("b1", [P, KD]), st.sb("w2", [P, KD, D])
        b2_raw, b2_sb, ones2 = st.sb("b2_raw", [2, D]), st.sb("b2", [2, D], F32R), st.sb("ones2", [2, P], F32R)
        low_part = st.sb("low_part", [P, 2])
        edge = st.sb("edge", [P, 2, CT, NG + 2])
        high = st.sb("high", [P, CT, NG], F32R)
        parts = st.sb("parts", [P, 2, CT, 2, 2, NG])
        far = st.sb("far", [P, 2, CT, D])
        index = st.sb("index", [P, 2, CT], I32)
        rbf_t = st.sb("rbf_t", [NG4, 2, 4 * P], F32R)
        hid = st.sb("hid", [P, 2, KD, 4 * P])
        same = st.sb("same", [P, 4, P], F32R)
        msg = st.sb("msg", [P, 4, 2, D], F32R)
        out = st.sb("out", [P, 2, CT, D + 1])
        loaded = st.sem("loaded")
        edge_loaded = [st.sem("edge_loaded0"), st.sem("edge_loaded1")]
        gathered = [st.moved(q, CHUNKS // 2 * CT) for q in range(2)]
        stored = [st.sem("stored0"), st.sem("stored1")]
        names = ("chain", "weights_split", "indexed", "rbf_turned", "rbf_copied", "hid_ready", "hid_done", "keys_turned", "filtered", "same_made",
                 "multiplied", "high_made", "msg_ready", "summed", "copied", "chunk_free", "pool_passed")
        (chain, weights_split, indexed, rbf_turned, rbf_copied, hid_ready, hid_done, keys_turned, filtered, same_made,
         multiplied, high_made, msg_ready, summed, copied, chunk_free, pool_passed) = map(st.sem, names)
        RBF, HIDB, KEYS, FILT, SUMS = 0, 1, (2, 3), (4, 5), (6, 7)
        PAIRS = CHUNKS // 2

        def pairs(eng, body):
            with eng.Fori(0, PAIRS - 1) as i:
                body(i, True)
            body(PAIRS - 1, False)

        with st.block() as block:
            @block.sync
            def _(sp):
                for k in range(4):
                    sp.dma_start(w1_raw[k * NG:(k + 1) * NG, :], wf1).then_inc(loaded, 16)
                for to, of in ((b1_sb[:], bf1), (w2_sb[:], rows(wf2)), (b2_raw[:], bf2.partition_broadcast(2))):
                    sp.dma_start(to, of).then_inc(loaded, 16)
                with sp.Fori(0, CHUNKS // 2) as i:
                    for q in range(2):
                        c = i * 2 + q
                        sp.wait_ge(chunk_free, c + 1)
                        sp.dma_start(edge[:, q], edge_rows[bass.ds(c * CHUNK, CHUNK), :].rearrange("(t p) d -> p t d", p=P)).then_inc(edge_loaded[q], 16)

            @block.gpsimd
            def _(pool):
                with pool.Fori(0, CHUNKS // 2) as i:
                    for q in range(2):
                        c = i * 2 + q
                        pool.wait_ge(indexed, c + 1)
                        pool.wait_ge(chunk_free, c + 1)
                        pool.sem_inc(pool_passed, 1)
                        for t in range(CT):
                            gathered[q].count(nc.gpsimd.indirect_dma_start(out=far[:, q, t, :], out_offset=None, in_=table,
                                                         in_offset=bass.IndirectOffsetOnAxis(ap=index[:, q, t:t + 1], axis=0),
                                                         bounds_check=NPAD - 1, oob_is_err=False))

            @block.tensor
            def _(pe):
                ident = core.c("ident")

                def turn_rbf(q, b, m):
                    pe.wait_ge(rbf_copied, m + 1)
                    for u in range(4):
                        last = nc.tensor.transpose(ps[0:NG4, RBF, u * P:(u + 1) * P], parts[:, q, b * 4 + u].rearrange("p a b g -> p (a b g)"), ident)
                    last.then_inc(rbf_turned, 1)

                def hidden(b, m, k):
                    pe.wait_ge(rbf_copied, m + 2)
                    pe.wait_ge(hid_done, m * 2 + k + 1)
                    nc.tensor.matmul(ps[:, HIDB, :], w1_sb[:, k * P:(k + 1) * P], rbf_t[:, b % 2, :], start=True, stop=True).then_inc(hid_ready, 1)

                def turn_keys(q, b, m):
                    for u in range(4):
                        last = nc.tensor.transpose(ps[:, KEYS[b % 2], u * P:(u + 1) * P], edge[:, q, b * 4 + u, NG:NG + 1].broadcast_to([P, P]), ident)
                    last.then_inc(keys_turned, 1)

                def total(t, n):
                    pe.wait_ge(same_made, n + 1)
                    pe.wait_ge(msg_ready, n + 1)
                    pe.wait_ge(copied, n + 1)
                    nc.tensor.matmul(ps[:, SUMS[t % 2], 0:D], same[:, t % 4, :], msg[:, t % 4, 0, :], start=True, stop=False)
                    nc.tensor.matmul(ps[:, SUMS[t % 2], 0:D], same[:, t % 4, :], msg[:, t % 4, 1, :], start=False, stop=True).then_inc(summed, 1)

                pe.wait_ge(loaded, 112)
                pe.wait_ge(weights_split, 1)
                pe.wait_ge(indexed, 1)
                turn_rbf(0, 0, 0)
                for k in range(KD):
                    hidden(0, 0, k)
                turn_keys(0, 0, 0)

                def body(i, more):
                    for qb in range(8):
                        q, b, m = qb // 4, qb % 4, i * 8 + qb
                        q_, b_ = (qb + 1) // 4 % 2, (qb + 1) % 4
                        ahead = more or qb < 7
                        pe.wait_ge(hid_done, m * 2 + 3)
                        for u in range(4):
                            t = qb * 4 + u
                            n = m * 4 + u
                            pe.wait_ge(msg_ready, n - 1) if t >= 2 else None
                            nc.tensor.matmul(ps[:, FILT[u % 2], 0:D], ones2[:], b2_sb[:], start=True, stop=False)
                            for k in range(KD):
                                last = nc.tensor.matmul(ps[:, FILT[u % 2], 0:D], hid[:, b % 2, k, u * P:(u + 1) * P], w2_sb[:, k, :], start=False, stop=(k == KD - 1))
                            last.then_inc(filtered, 1)
                            if ahead and u == 0:
                                if b_ == 0:
                                    pe.wait_ge(indexed, i * 2 + q + 2)
                                turn_rbf(q_, b_, m + 1)
                            if ahead and u in (1, 2):
                                hidden(b_, m + 1, u - 1)
                            if t >= 2:
                                total(t - 2, n - 2)
                            if ahead and u == 3:
                                turn_keys(q_, b_, m + 1)
                    for t in (30, 31):
                        total(t, i * 32 + t)

                pairs(pe, body)

            @block.scalar
            def _(act):
                act.sem_inc(copied, 2)
                act.sem_inc(rbf_copied, 1)
                act.sem_inc(hid_done, 1)
                for s in range(2):
                    act.sem_inc(stored[s], 16)
                act.wait_ge(loaded, 112)

                def copy_rbf(b, m):
                    act.wait_ge(rbf_turned, m + 1)
                    nc.scalar.copy(rbf_t[:, b % 2, :], ps[0:NG4, RBF, :]).then_inc(rbf_copied, 1)

                def silu(b, m, k):
                    act.wait_ge(hid_ready, m * 2 + k + 1)
                    nc.scalar.activation(hid[:, b % 2, k, :], ps[:, HIDB, :], ACT.Silu, bias=b1_sb[:, k:k + 1]).then_inc(hid_done, 1)

                def high_of(t, n):
                    act.wait_ge(multiplied, n + 1)
                    nc.scalar.copy(msg[:, t % 4, 0, :], ps[:, FILT[t % 2], 0:D]).then_inc(high_made, 1)

                def take(t, n):
                    act.wait_ge(summed, n + 1)
                    nc.scalar.copy(out[:, t // CT, t % CT, 0:D], ps[:, SUMS[t % 2], 0:D]).then_inc(copied, 1)

                def store(i, q):
                    act.wait_ge(copied, (i * 2 + q + 1) * CT + 2)
                    act.dma_start(partial[bass.ds((i * 2 + q) * CHUNK, CHUNK), :].rearrange("(t p) d -> p t d", p=P), out[:, q]).then_inc(stored[q], 16)

                copy_rbf(0, 0)
                for k in range(KD):
                    silu(0, 0, k)

                def body(i, more):
                    for qb in range(8):
                        b, m = qb % 4, i * 8 + qb
                        ahead = more or qb < 7
                        for u in range(4):
                            t = qb * 4 + u
                            n = m * 4 + u
                            high_of(t, n)
                            if ahead and u == 0:
                                copy_rbf(b + 1, m + 1)
                            if t >= 2 and (t - 2) % CT == 0:
                                act.wait_ge(stored[(t - 2) // CT], i * 16 + 16)
                            if ahead and u in (1, 2):
                                silu(b + 1, m + 1, u - 1)
                            if t >= 2:
                                take(t - 2, n - 2)
                            if t == CT + 1:
                                store(i, 0)
                    for t in (30, 31):
                        take(t, i * 32 + t)
                    store(i, 1)

                pairs(act, body)
                for q in range(2):
                    act.wait_ge(stored[q], (CHUNKS // 2) * 16 + 16)

            @block.vector
            def _(dve):
                ch = Chain(dve, chain)
                dve.wait_ge(loaded, 112)
                dve.sem_inc(chunk_free, 2)
                ch.add(nc.vector.tensor_copy(ones2[:], core.c("ones")[0:2, :]))
                ch.link(nc.vector.tensor_scalar(low_part[:, 0:1], core.c("iota_p"), float(2 * NG), None, ALU.is_ge))
                ch.link(nc.vector.tensor_scalar(low_part[:, 1:2], core.c("iota_p"), 1.0, None, ALU.is_ge))
                for raw, to, low in ((w1_raw, w1_sb, low_part[0:NG4, 0:1]), (b2_raw, b2_sb, low_part[0:2, 1:2])):
                    ch.link(nc.vector.tensor_copy(to[:], raw[:]))
                    ch.link(nc.vector.tensor_scalar(raw[:], raw[:], low, None, ALU.mult))
                    ch.link(nc.vector.scalar_tensor_tensor(raw[:], to[:], low, raw[:], ALU.mult, ALU.subtract))
                    ch.link(nc.vector.scalar_tensor_tensor(raw[:], to[:], low, raw[:], ALU.mult, ALU.add))
                    ch.link(nc.vector.tensor_tensor(to[:], to[:], raw[:], ALU.subtract))
                dve.sem_inc(weights_split, 1)

                def prepare(q, i):
                    dve.wait_ge(edge_loaded[q], i * 16 + 16)
                    ch.add(nc.vector.tensor_copy(index[:, q], edge[:, q, :, NG + 1]))
                    ch.add(nc.vector.tensor_copy(high[:], edge[:, q, :, 0:NG]))
                    ch.settle()
                    both = lambda v: v.unsqueeze(2).broadcast_to([P, CT, 2, NG])
                    ch.add(nc.vector.tensor_copy(parts[:, q, :, :, 0, :], both(high[:])))
                    ch.add(nc.vector.tensor_tensor(parts[:, q, :, :, 1, :], both(edge[:, q, :, 0:NG]), both(high[:]), ALU.subtract))
                    ch.settle()
                    dve.sem_inc(indexed, 1)
                PER = 4

                prepare(0, 0)

                def same_of(q, t, n):
                    if t >= 4:
                        dve.wait_ge(summed, n - 3)
                    nc.vector.scalar_tensor_tensor(same[:, t % 4, :], ps[:, KEYS[(t // 4) % 2], (t % 4) * P:(t % 4 + 1) * P], edge[:, q, t % CT, NG:NG + 1],
                                                   core.c("le"), ALU.is_equal, ALU.mult).then_inc(same_made, 1)

                def body(i, more):
                    for q in range(2):
                        c = i * 2 + q
                        gathered[q].wait(dve, i * CT * 16 + CT * 16)
                        for t in range(q * CT, q * CT + CT):
                            n = i * 32 + t
                            if t % 4 == 0:
                                dve.wait_ge(keys_turned, i * 8 + t // 4 + 1)
                                same_of(q, t, n)
                            dve.wait_ge(filtered, n + 1)
                            nc.vector.tensor_tensor(ps[:, FILT[t % 2], 0:D], ps[:, FILT[t % 2], 0:D], far[:, q, t % CT, :], ALU.mult).then_inc(multiplied, 1)
                            if t % 4 < 3:
                                same_of(q, t + 1, n + 1)
                            dve.wait_ge(high_made, n + 1)
                            nc.vector.tensor_tensor(msg[:, t % 4, 1, :], ps[:, FILT[t % 2], 0:D], msg[:, t % 4, 0, :], ALU.subtract).then_inc(msg_ready, 1)
                            if t % CT == 1:
                                dve.wait_ge(stored[q], i * 16 + 16)
                                ch.add(nc.vector.tensor_copy(out[:, q, :, D], edge[:, q, :, NG]))
                            if t % CT == 3 and (more or q == 0):
                                prepare(1 - q, i + q)
                        dve.wait_ge(msg_ready, c * CT + CT)
                        ch.settle()
                        dve.sem_inc(chunk_free, 1)

                with ch.loop(PAIRS - 1, 2 + 2 * PER) as i:
                    body(i, True)
                body(PAIRS - 1, False)


def carry_stage(core, name, partial, carry, sums, tops, scale):
    W = sums + tops
    with Stage(core, name) as st:
        nc, ps = core.nc, core.ps
        part = st.sb("part", [QT, 4, W + 1])
        last_node = st.sb("last_node", [QT, 4])
        node_row = st.sb("node_row", [P, ETILES])
        reach = st.sb("reach", [QT, 4, 4, QT])
        out = st.sb("out", [QT, 4, W])
        loaded, chain, nodes_ready, turned, row_copied, reach_ready, summed, done, stored = (
            st.sem(x) for x in ("loaded", "chain", "nodes_ready", "turned", "row_copied", "reach_ready", "summed", "done", "stored"))
        if tops:
            fresh = st.sb("fresh", [HEADS, ETILES + 1])
            up, down = st.sb("up", [HEADS, ETILES]), st.sb("down", [HEADS, ETILES])
            factor = st.sb("factor", [QT, 4, HEADS])
            top_ready, top_turned, centred, expd = (st.sem(x) for x in ("top_ready", "top_turned", "centred", "expd"))
        ident = core.c("ident")
        with st.block() as block:
            @block.sync
            def _(sp):
                sp.dma_start(part[:], partial.rearrange("(q p r) w -> p q r w", q=4, r=P)[:, :, P - 1, :]).then_inc(loaded, 16)
                sp.wait_ge(done, 1)
                sp.dma_start(carry.rearrange("(q p) w -> p q w", q=4), out[:]).then_inc(stored, 16)
                sp.wait_ge(stored, 16)

            @block.tensor
            def _(pe):
                pe.wait_ge(nodes_ready, 1)
                for q in range(4):
                    last = nc.tensor.transpose(ps[:, 0, q * QT:(q + 1) * QT], last_node[:, q:q + 1].broadcast_to([QT, P]), ident[0:QT, 0:QT])
                if tops:
                    for q in range(4):
                        last = nc.tensor.transpose(ps[0:HEADS, 1, q * QT:(q + 1) * QT], part[:, q, sums:W], ident[0:QT, 0:QT])
                last.then_inc(turned, 1)
                if tops:
                    pe.wait_ge(top_ready, 1)
                    for q in range(4):
                        last = nc.tensor.transpose(ps[0:QT, 2, q * HEADS:(q + 1) * HEADS], down[:, q * QT:(q + 1) * QT], ident[0:HEADS, 0:HEADS])
                    last.then_inc(top_turned, 1)
                pe.wait_ge(reach_ready, 1)
                for qo in range(4):
                    for qi in range(qo + 1):
                        last = nc.tensor.matmul(ps[0:QT, 3 + qo, 0:sums], reach[:, qi, qo, :], part[:, qi, 0:sums], start=(qi == 0), stop=(qi == qo))
                last.then_inc(summed, 1)

            @block.scalar
            def _(act):
                if tops:
                    act.wait_ge(centred, 1)
                    nc.scalar.activation(factor[:], factor[:], ACT.Exp, scale=scale).then_inc(expd, 1)

            @block.vector
            def _(dve):
                ch = Chain(dve, chain)
                dve.wait_ge(loaded, 16)
                ch.link(nc.vector.tensor_copy(last_node[:], part[:, :, W]))
                dve.sem_inc(nodes_ready, 1)
                dve.wait_ge(turned, 1)
                ch.link(nc.vector.tensor_copy(node_row[:], ps[:, 0, 0:ETILES]))
                if tops:
                    ch.link(nc.vector.memset(fresh[:], 0.0))
                    ch.link(nc.vector.tensor_tensor(fresh[:, 1:ETILES], node_row[0:HEADS, 1:], node_row[0:HEADS, 0:ETILES - 1], ALU.not_equal))
                    ch.link(nc.vector.tensor_scalar(fresh[:, 1:ETILES], fresh[:, 1:ETILES], -BIG, None, ALU.mult))
                    ch.link(nc.vector.tensor_tensor_scan(up[:], fresh[:, 0:ETILES], ps[0:HEADS, 1, 0:ETILES], -BIG, ALU.add, ALU.max))
                    ch.link(nc.vector.tensor_tensor_scan(down[:, ::-1], fresh[:, 1:][:, ::-1], up[:, ::-1], -BIG, ALU.add, ALU.max))
                    dve.sem_inc(top_ready, 1)
                    dve.wait_ge(top_turned, 1)
                    both = ps[0:QT, 2, 0:4 * HEADS].rearrange("p (q h) -> p q h", q=4)
                    ch.link(nc.vector.tensor_tensor(factor[:], part[:, :, sums:W], both, ALU.subtract))
                    dve.sem_inc(centred, 1)
                    ch.link(nc.vector.tensor_copy(out[:, :, sums:W], both))
                    dve.wait_ge(expd, 1)
                    for q in range(4):
                        v = part[:, q, 0:D].rearrange("p (h c) -> p h c", h=HEADS)
                        ch.add(nc.vector.tensor_tensor(v, v, factor[:, q].unsqueeze(2).broadcast_to([QT, HEADS, HD]), ALU.mult))
                    ch.link(nc.vector.tensor_tensor(part[:, :, D:sums], part[:, :, D:sums], factor[:], ALU.mult))
                for qo in range(4):
                    for qi in range(qo + 1):
                        to, row, own = reach[:, qi, qo, :], node_row[0:QT, qo * QT:(qo + 1) * QT], last_node[:, qi:qi + 1]
                        if qi == qo:
                            ch.add(nc.vector.scalar_tensor_tensor(to, row, own, core.c("le")[0:QT, 0:QT], ALU.is_equal, ALU.mult))
                        else:
                            ch.add(nc.vector.tensor_scalar(to, row, own, None, ALU.is_equal))
                ch.settle()
                dve.sem_inc(reach_ready, 1)
                dve.wait_ge(summed, 1)
                ch.link(nc.vector.tensor_copy(out[:, :, 0:sums], ps[0:QT, 3:7, 0:sums]))
                dve.sem_inc(done, 1)


def node_stage(core, name, s, base, count, partial, carry, sums, tops, scale, agg=None, bias=None, self_rows=None):
    W = sums + tops
    with Stage(core, name) as st:
        nc, x = core.nc, core.x
        end, spans, tile = st.sb("end", [P, TILES]), st.sb("spans", [P, TILES]), st.sb("tile", [P, TILES])
        end_i, tile_i, carry_i = st.sb("end_i", [P, TILES], I32), st.sb("tile_i", [P, TILES], I32), st.sb("carry_i", [P, TILES], I32)
        own = st.sb("own", [P, TILES, W + 1])
        far = st.sb("far", [P, TILES, W])
        f = st.sb("f", [P, 6, TILES, HEADS])
        if self_rows is not None:
            own_value, own_score = st.sb("own_value", [P, TILES, SEG]), st.sb("own_score", [P, TILES, HEADS])
        PARTS = 3 if self_rows is not None else 2
        loaded, chain, indexed, centred, expd = (st.sem(x) for x in ("loaded", "chain", "indexed", "centred", "expd"))
        gathered = st.moved(0, 2 * TILES)
        if bias is not None:
            bias_sb = st.sb("bias", [P, D])
        with st.block() as block:
            @block.sync
            def _(sp):
                if bias is not None:
                    sp.dma_start(bias_sb[:], bcast(bias)).then_inc(loaded, 16)
                if self_rows is not None:
                    for to, of in zip((own_value, own_score), self_rows):
                        sp.dma_start(to[:], of.rearrange("(a p) d -> p a d", p=P)).then_inc(loaded, 16)

            @block.gpsimd
            def _(pool):
                pool.wait_ge(indexed, 1)
                for a in range(TILES):
                    for to, table, index in ((own, partial, end_i), (far, carry, carry_i)):
                        gathered.count(nc.gpsimd.indirect_dma_start(out=to[:, a, :], out_offset=None, in_=table,
                                                     in_offset=bass.IndirectOffsetOnAxis(ap=index[:, a:a + 1], axis=0),
                                                     bounds_check=table.shape[0] - 1, oob_is_err=False))

            @block.scalar
            def _(act):
                if tops:
                    act.wait_ge(centred, 1)
                    nc.scalar.activation(f[:, 1:1 + PARTS], f[:, 1:1 + PARTS], ACT.Exp, scale=scale).then_inc(expd, 1)

            @block.vector
            def _(dve):
                ch = Chain(dve, chain)
                b, n = base[:, s], count[:, s]
                bh = lambda v: v.unsqueeze(2).broadcast_to([P, TILES, HEADS])
                ch.link(nc.vector.scalar_tensor_tensor(end[:], b, -1.0, n, ALU.add, ALU.add))
                ch.link(nc.vector.tensor_scalar(end[:], end[:], 0.0, None, ALU.max))
                ch.link(nc.vector.tensor_copy(end_i[:], end[:]))
                ch.link(nc.vector.tensor_scalar(tile_i[:], end_i[:], 7, None, ALU.logical_shift_right))
                ch.link(nc.vector.tensor_copy(tile[:], tile_i[:]))
                ch.link(nc.vector.scalar_tensor_tensor(spans[:], tile[:], float(P), b, ALU.mult, ALU.is_gt))
                ch.link(nc.vector.tensor_scalar(tile[:], tile[:], 1.0, 0.0, ALU.subtract, ALU.max))
                ch.link(nc.vector.tensor_copy(carry_i[:], tile[:]))
                dve.sem_inc(indexed, 1)
                ch.link(nc.vector.tensor_scalar(end[:], n, 0.0, None, ALU.is_gt))
                gathered.wait(dve, 2 * TILES * 16)
                if bias is not None:
                    dve.wait_ge(loaded, 48 if self_rows is not None else 16)
                if tops:
                    mine, its = own[:, :, sums:W], far[:, :, sums:W]
                    ch.link(nc.vector.tensor_tensor(f[:, 0], its, bh(spans[:]), ALU.mult))
                    ch.link(nc.vector.tensor_scalar(tile[:], spans[:], 1.0, BIG, ALU.subtract, ALU.mult))
                    ch.link(nc.vector.tensor_tensor(f[:, 0], f[:, 0], bh(tile[:]), ALU.add))
                    if self_rows is not None:
                        ch.link(nc.vector.tensor_tensor(mine, mine, bh(end[:]), ALU.mult))
                        ch.link(nc.vector.tensor_scalar(tile[:], end[:], 1.0, BIG, ALU.subtract, ALU.mult))
                        ch.link(nc.vector.tensor_tensor(mine, mine, bh(tile[:]), ALU.add))
                        ch.link(nc.vector.tensor_tensor(f[:, 5], own_value[:, :, D:SEG], own_score[:], ALU.add))
                        ch.link(nc.vector.scalar_tensor_tensor(f[:, 3], f[:, 5], 0.2, f[:, 5], ALU.mult, ALU.max))
                    ch.link(nc.vector.tensor_tensor(f[:, 4], f[:, 0], mine, ALU.max))
                    if self_rows is not None:
                        ch.link(nc.vector.tensor_tensor(f[:, 4], f[:, 4], f[:, 3], ALU.max))
                        ch.link(nc.vector.tensor_tensor(f[:, 3], f[:, 3], f[:, 4], ALU.subtract))
                    ch.link(nc.vector.tensor_tensor(f[:, 1], mine, f[:, 4], ALU.subtract))
                    ch.link(nc.vector.tensor_tensor(f[:, 2], f[:, 0], f[:, 4], ALU.subtract))
                    dve.sem_inc(centred, 1)
                    dve.wait_ge(expd, 1)
                    ch.link(nc.vector.tensor_tensor(f[:, 4], own[:, :, D:sums], f[:, 1], ALU.mult))
                    ch.link(nc.vector.tensor_tensor(f[:, 5], far[:, :, D:sums], f[:, 2], ALU.mult))
                    ch.link(nc.vector.tensor_tensor(f[:, 4], f[:, 4], f[:, 5], ALU.add))
                    if self_rows is not None:
                        ch.link(nc.vector.tensor_tensor(f[:, 4], f[:, 4], f[:, 3], ALU.add))
                    ch.link(nc.vector.reciprocal(f[:, 4], f[:, 4]))
                    if self_rows is None:
                        ch.link(nc.vector.tensor_tensor(f[:, 4], f[:, 4], bh(end[:]), ALU.mult))
                    for k in range(1, 1 + PARTS):
                        ch.link(nc.vector.tensor_tensor(f[:, k], f[:, k], f[:, 4], ALU.mult))
                    parts = [(1, own), (2, far)] + ([(3, own_value)] if self_rows is not None else [])
                    with ch.loop(GROUPS, 2 * PARTS * GROUP) as g:
                        for k, rows_ in parts:
                            for j in range(GROUP):
                                v = rows_[:, bass.ds(g * GROUP + j, 1), 0:D].rearrange("p a (h c) -> p (a h) c", h=HEADS)
                                w = f[:, k, bass.ds(g * GROUP + j, 1), :].rearrange("p a h -> p (a h)").unsqueeze(2).broadcast_to([P, HEADS, HD])
                                ch.add(nc.vector.tensor_tensor(v, v, w, ALU.mult))
                        ch.settle()
                        for k, rows_ in parts[1:]:
                            for j in range(GROUP):
                                at = bass.ds(g * GROUP + j, 1)
                                ch.add(nc.vector.tensor_tensor(own[:, at, 0:D], own[:, at, 0:D], rows_[:, at, 0:D], ALU.add))
                            ch.settle()
                        for j in range(GROUP):
                            at = bass.ds(g * GROUP + j, 1)
                            if agg is None:
                                ch.add(nc.vector.tensor_tensor(x[:, at, :], x[:, at, :], own[:, at, 0:D], ALU.add))
                            else:
                                ch.add(nc.vector.tensor_tensor(agg[:, at, :], own[:, at, 0:D], bias_sb[:].unsqueeze(1), ALU.add))
                        ch.settle()
                else:
                    with ch.loop(TILES, 2) as a:
                        at = bass.ds(a, 1)
                        v, w = own[:, at, 0:D].rearrange("p a d -> p (a d)"), far[:, at, 0:D].rearrange("p a d -> p (a d)")
                        ch.link(nc.vector.tensor_scalar(v, v, end[:, at], None, ALU.mult))
                        ch.link(nc.vector.scalar_tensor_tensor(agg[:, at, :].rearrange("p a d -> p (a d)"), w, spans[:, at], v, ALU.mult, ALU.add))


def turn(core, pe, act_free, turned, src):
    for a in range(TILES):
        pe.wait_ge(act_free, a + 1)
        for k in range(KD):
            last = core.nc.tensor.transpose(core.ps[:, a % GROUP, k * P:(k + 1) * P], src[:, a, k * P:(k + 1) * P], core.c("ident"))
        last.then_inc(turned, 1)


def update_stage(core, agg, ht, wu1, bu1, wu2, bu2):
    with Stage(core, "up") as st:
        nc, ps = core.nc, core.ps
        w_sb, b_sb = st.sb("w", [P, 2, KD, D]), st.sb("b", [P, 2, KD])
        hid = st.sb("hid", [P, KD, HALF])
        loaded, turned, bank_free, ready, done = (st.sem(s) for s in ("loaded", "turned", "bank_free", "ready", "done"))
        BLOCKS = NPAD // HALF
        with st.block() as block:
            @block.sync
            def _(sp):
                for to, of in ((w_sb[:, 0], rows(wu1)), (w_sb[:, 1], rows(wu2)), (b_sb[:, 0], bu1), (b_sb[:, 1], bu2)):
                    sp.dma_start(to, of).then_inc(loaded, 16)

            @block.tensor
            def _(pe):
                turn(core, pe, bank_free, turned, agg)
                pe.wait_ge(loaded, 64)
                pe.wait_ge(bank_free, TILES + GROUP)
                with pe.Fori(0, BLOCKS) as g:
                    for layer in range(2):
                        for m in range(KD):
                            n = layer * KD + m
                            pe.wait_ge(done, g * 4 + (KD if layer else 0) + 1)
                            for k in range(KD):
                                src = ht[:, k, bass.ds(g * HALF, HALF)] if layer == 0 else hid[:, k, :]
                                last = nc.tensor.matmul(ps[:, n, 0:HALF], w_sb[:, layer, k, m * P:(m + 1) * P], src, start=(k == 0), stop=(k == KD - 1))
                            last.then_inc(ready, 1)

            @block.scalar
            def _(act):
                act.sem_inc(bank_free, GROUP)
                for a in range(TILES):
                    act.wait_ge(turned, a + 1)
                    nc.scalar.copy(ht[:, :, a * P:(a + 1) * P], ps[:, a % GROUP, 0:D].rearrange("p (k t) -> p k t", k=KD)).then_inc(bank_free, 1)
                act.sem_inc(done, 1)
                act.wait_ge(loaded, 64)
                with act.Fori(0, BLOCKS) as g:
                    for m in range(KD):
                        act.wait_ge(ready, g * 4 + m + 1)
                        nc.scalar.activation(hid[:, m, :], ps[:, m, 0:HALF], ACT.Silu, bias=b_sb[:, 0, m:m + 1]).then_inc(done, 1)
                    for m in range(KD):
                        act.wait_ge(ready, g * 4 + KD + KD)
                        nc.scalar.activation(ht[:, m, bass.ds(g * HALF, HALF)], ps[:, KD + m, 0:HALF], ACT.Identity, bias=b_sb[:, 1, m:m + 1]).then_inc(done, 1)


def batchnorm_stage(core, name, ht, agg, gamma, beta):
    SPLIT = [(k, min(512, N - k)) for k in range(0, N, 512)]
    with Stage(core, name) as st:
        nc, ps, x, xn = core.nc, core.ps, core.x, core.xn
        gb = st.sb("gb", [P, 2, KD])
        stats = st.sb("stats", [P, KD, len(SPLIT), 6])
        mv = st.sb("mv", [P, KD, 2])
        std = st.sb("std", [P, KD])
        lines = st.sb("lines", [P, 2, D])
        scratch = st.sb("scratch", [P, 2, D])
        loaded, chain, turned, bank_free, var_ready, std_ready, coef_ready, spread, values, added, copied = (
            st.sem(s) for s in ("loaded", "chain", "turned", "bank_free", "var_ready", "std_ready", "coef_ready", "spread", "values", "added", "copied"))
        with st.block() as block:
            @block.sync
            def _(sp):
                sp.dma_start(gb[:, 0], gamma).then_inc(loaded, 16)
                sp.dma_start(gb[:, 1], beta).then_inc(loaded, 16)

            @block.tensor
            def _(pe):
                if agg is not None:
                    turn(core, pe, bank_free, turned, agg)
                pe.wait_ge(coef_ready, 1)
                for i in range(2):
                    for k in range(KD):
                        last = nc.tensor.transpose(ps[:, 5 + i, k * P:(k + 1) * P], gb[:, i, k:k + 1].broadcast_to([P, P]), core.c("ident"))
                last.then_inc(spread, 1)
                if agg is None:
                    for a in range(TILES):
                        pe.wait_ge(added, a + 1)
                        for k in range(KD):
                            last = nc.tensor.transpose(ps[:, a % 4, k * P:(k + 1) * P], ht[:, k, a * P:(a + 1) * P], core.c("ident"))
                        last.then_inc(values, 1)

            @block.scalar
            def _(act):
                if agg is not None:
                    act.sem_inc(bank_free, GROUP)
                    for a in range(TILES):
                        act.wait_ge(turned, a + 1)
                        nc.scalar.copy(ht[:, :, a * P:(a + 1) * P], ps[:, a % GROUP, 0:D].rearrange("p (k t) -> p k t", k=KD)).then_inc(bank_free, 1)
                act.wait_ge(var_ready, 1)
                nc.scalar.activation(std[:], std[:], ACT.Sqrt).then_inc(std_ready, 1)

            @block.vector
            def _(dve):
                ch = Chain(dve, chain)
                dve.wait_ge(loaded, 32)
                if agg is None:
                    dve.sem_inc(added, 4)
                else:
                    dve.wait_ge(bank_free, TILES + GROUP)
                for k in range(KD):
                    for b, (at, w) in enumerate(SPLIT):
                        ch.add(nc.vector.bn_stats(stats[:, k, b, :], ht[:, k, at:at + w]))
                ch.settle()
                for k in range(KD):
                    ch.add(nc.vector.bn_aggr(mv[:, k, :], stats[:, k].rearrange("p b s -> p (b s)")))
                ch.settle()
                ch.link(nc.vector.tensor_scalar_add(std[:], mv[:, :, 1], 1e-5))
                dve.sem_inc(var_ready, 1)
                dve.wait_ge(std_ready, 1)
                ch.link(nc.vector.reciprocal(std[:], std[:]))
                ch.link(nc.vector.tensor_tensor(gb[:, 0], gb[:, 0], std[:], ALU.mult))
                ch.link(nc.vector.tensor_tensor(std[:], mv[:, :, 0], gb[:, 0], ALU.mult))
                ch.link(nc.vector.tensor_tensor(gb[:, 1], gb[:, 1], std[:], ALU.subtract))
                dve.sem_inc(coef_ready, 1)
                dve.wait_ge(spread, 1)
                ch.link(nc.vector.tensor_copy(lines[:], ps[:, 5:7, 0:D]))
                for a in range(TILES):
                    if agg is None:
                        dve.wait_ge(values, a + 1)
                        v = ps[:, a % 4, 0:D]
                    else:
                        v = agg[:, a, :]
                    ch.add(nc.vector.tensor_tensor(xn[:, a, :], xn[:, a, :], lines[:, 1, :], ALU.add))
                    ch.link(nc.vector.tensor_tensor(scratch[:, a % 2, :], v, lines[:, 0, :], ALU.mult))
                    if agg is None:
                        dve.sem_inc(added, 1)
                    ch.add(nc.vector.tensor_tensor(x[:, a, :], x[:, a, :], xn[:, a, :], ALU.add))
                    ch.settle()
                    ch.link(nc.vector.tensor_tensor(x[:, a, :], x[:, a, :], scratch[:, a % 2, :], ALU.add))


def store_rows_stage(core, name, rows_sb, table):
    with Stage(core, name) as st:
        stored = st.sem("stored")
        with st.block() as block:
            @block.sync
            def _(sp):
                sp.dma_start(table.rearrange("(a p) d -> p a d", p=P), rows_sb[:]).then_inc(stored, 16)
                sp.wait_ge(stored, 16)


def project3_stage(core, xt, weight, att_src, att_dst, src_table, dst_table):
    with Stage(core, "p3") as st:
        nc, ps = core.nc, core.ps
        w_sb, av = st.sb("w", [P, KD, D]), st.sb("av", [P, 2, D])
        out = st.sb("out", [P, TILES, SEG])
        near = st.sb("near", [P, TILES, HEADS])
        prod = st.sb("prod", [P, 2, D])
        loaded, chain, projected, bank_free, copied, stored = (st.sem(s) for s in ("loaded", "chain", "projected", "bank_free", "copied", "stored"))
        with st.block() as block:
            @block.sync
            def _(sp):
                for to, of in ((w_sb[:], rows(weight)), (av[:, 0], bcast(att_src)), (av[:, 1], bcast(att_dst))):
                    sp.dma_start(to, of).then_inc(loaded, 16)
                sp.wait_ge(bank_free, TILES + GROUP)
                sp.dma_start(src_table.rearrange("(a p) d -> p a d", p=P), out[:]).then_inc(stored, 16)
                sp.dma_start(dst_table.rearrange("(a p) d -> p a d", p=P), near[:]).then_inc(stored, 16)
                sp.wait_ge(stored, 32)

            @block.tensor
            def _(pe):
                pe.sem_inc(bank_free, GROUP)
                pe.wait_ge(loaded, 48)
                for a in range(TILES):
                    pe.wait_ge(bank_free, a + 1)
                    for k in range(KD):
                        last = nc.tensor.matmul(ps[:, a % GROUP, 0:D], xt[:, k, a * P:(a + 1) * P], w_sb[:, k, :], start=(k == 0), stop=(k == KD - 1))
                    last.then_inc(projected, 1)

            @block.scalar
            def _(act):
                for a in range(TILES):
                    act.wait_ge(projected, a + 1)
                    nc.scalar.copy(out[:, a, 0:D], ps[:, a % GROUP, 0:D]).then_inc(copied, 1)

            @block.vector
            def _(dve):
                ch = Chain(dve, chain)
                dve.wait_ge(loaded, 48)
                for a in range(TILES):
                    dve.wait_ge(copied, a + 1)
                    for s in range(2):
                        ch.add(nc.vector.tensor_tensor(prod[:, s, :], ps[:, a % GROUP, 0:D], av[:, s, :], ALU.mult))
                    ch.settle()
                    for s, to in ((0, out[:, a, D:SEG]), (1, near[:, a, :])):
                        ch.add(nc.vector.tensor_reduce(to, prod[:, s, :].rearrange("p (h c) -> p h c", h=HEADS), AX, ALU.add))
                    ch.settle()
                    dve.sem_inc(bank_free, 1)


def gnn_ffn_kernel(nc, a, out):
    dram = lambda name, shape: nc.dram_tensor(name, shape, F32, kind="Internal").ap()
    inv = float(HD) ** -0.5
    with ExitStack() as ctx:
        core = Core(nc, ctx)

        def sb(name, shape, to=ctx):
            return to.enter_context(nc.sbuf_tensor(name, shape, F32))

        base, count, ends = sb("base", [P, 2, TILES]), sb("count", [P, 2, TILES]), sb("ends", [P, 2, ETILES])
        by_dst, by_src = dram("by_dst", (EPAD, D + 2)), dram("by_src", (EPAD, a["edge_attr_20"].shape[1] + 2))
        partial, carry = dram("partial", (EPAD, ROW)), dram("carry", (ETILES, ROW - 1))
        partial_f, carry_f = dram("partial_f", (EPAD, D + 1)), dram("carry_f", (ETILES, D))
        load_stage(core, a["x"], a["consts"])

        with ExitStack() as own:
            split = sb("split", [P, 2, 3, ETILES], own)
            count_stage(core, (a["dst"], a["src"]), split, base, count)
            sort_stage(core, split, base, a["edge_attr_256"], a["edge_attr_20"], by_dst, by_src)

        with ExitStack() as own:
            xt = sb("xt0", [P, KD, NPAD], own)
            norm_stage(core, "n0", xt)
            l0_gnn_stage(core, xt, a["src"], a["dst"], a["L0_gnn_weight"], a["L0_gnn_attn_l"], a["L0_gnn_attn_r"],
                         dram("xt_table", (NPAD, D)), dram("al_table", (NPAD, 8)))
            norm_stage(core, "n1", xt)
            l0_ffn_stage(core, xt, *(a[f"L0_ffn_{k}"] for k in ("wr", "br", "w1", "b1", "w2", "b2")))
            norm_stage(core, "n2", xt)
            q_table, kv_table = dram("q_table", (NPAD, D)), dram("kv_table", (NPAD, 2 * D))
            project_stage(core, xt, [a[f"L1_gnn_W{k}"] for k in "qkvs"], [a[f"L1_gnn_b{k}"] for k in "qkvs"], q_table, kv_table)
        attend_stage(core, "a1", ends, kv_table, q_table, by_dst, partial, inv, a["L1_gnn_We"])
        carry_stage(core, "c1", partial, carry, SEG, HEADS, inv)
        node_stage(core, "m1", 0, base, count, partial, carry, SEG, HEADS, inv)
        with ExitStack() as own:
            xt = sb("xt1", [P, KD, NPAD], own)
            norm_stage(core, "n3", xt)
            l1_ffn_stage(core, xt, *(a[f"L1_ffn_{k}"] for k in ("router_w", "router_b", "W1", "b1", "W2", "b2")), a["expert_rows"])
            norm_stage(core, "n4", xt)
        x_table = dram("x_table", (NPAD, D))
        store_rows_stage(core, "rows", core.xn, x_table)
        filter_stage(core, "fl", by_src, x_table, *(a[f"L2_gnn_{k}"] for k in ("Wf1", "bf1", "Wf2", "bf2")), partial_f)
        carry_stage(core, "c2", partial_f, carry_f, D, 0, 1.0)
        with ExitStack() as own:
            agg = sb("agg2", [P, TILES, D], own)
            node_stage(core, "m2", 1, base, count, partial_f, carry_f, D, 0, 1.0, agg)
            ht = sb("ht2", [P, KD, NPAD], own)
            update_stage(core, agg, ht, *(a[f"L2_gnn_{k}"] for k in ("Wu1", "bu1", "Wu2", "bu2")))
            batchnorm_stage(core, "b2", ht, None, a["L2_gnn_gamma"], a["L2_gnn_beta"])
        with ExitStack() as own:
            xt = sb("xt2", [P, KD, NPAD], own)
            norm_stage(core, "n5", xt)
            l2_ffn_stage(core, xt, *(a[f"L2_ffn_{k}"] for k in ("Wr", "br", "W1", "bn1", "W2", "bn2", "Wo", "bo")))
            norm_stage(core, "n6", xt)
            src_table, dst_table = dram("src_table", (NPAD, SEG)), dram("dst_table", (NPAD, HEADS))
            project3_stage(core, xt, a["L3_gnn_W"], a["L3_gnn_att_src"], a["L3_gnn_att_dst"], src_table, dst_table)
        starts = dram("starts", (P, ETILES, HEADS))
        starts_stage(core, base, count, by_dst, dst_table, starts)
        attend_stage(core, "a3", ends, src_table, starts, None, partial, 1.0)
        carry_stage(core, "c3", partial, carry, SEG, HEADS, 1.0)
        with ExitStack() as own:
            agg = sb("agg3", [P, TILES, D], own)
            node_stage(core, "m3", 0, base, count, partial, carry, SEG, HEADS, 1.0, agg, a["L3_gnn_bias"], (src_table, dst_table))
            ht = sb("ht3", [P, KD, NPAD], own)
            batchnorm_stage(core, "b3", ht, agg, a["L3_gnn_gamma"], a["L3_gnn_beta"])
        with ExitStack() as own:
            xt = sb("xt3", [P, KD, NPAD], own)
            norm_stage(core, "n7", xt)
            l3_ffn_stage(core, xt, *(a[f"L3_ffn_{k}"] for k in ("sW1", "sb1", "sW2", "sb2", "sW3", "eW1", "eb1", "eW2", "eb2", "eW3", "b3", "gW", "gb")))
        with Stage(core, "out") as st:
            stored = st.sem("stored")
            with st.block() as block:
                @block.sync
                def _(sp):
                    full = (TILES - 1) * P
                    sp.dma_start(out[0:full, :].rearrange("(a p) d -> p a d", p=P), core.x[:, 0:TILES - 1, :]).then_inc(stored, 16)
                    sp.dma_start(out[full:N, :], core.x[0:N - full, TILES - 1, :]).then_inc(stored, 16)
                    sp.wait_ge(stored, 32)


def layout(inputs):
    a = {k: np.asarray(v) for k, v in inputs.items()}
    del a["L0_ffn_attention_mask"]
    pad = lambda v, fill: np.concatenate([v, np.full((EPAD - E,) + v.shape[1:], fill, v.dtype)])
    columns = lambda v: np.ascontiguousarray(v.reshape(-1, P).T)
    a["src"], a["dst"] = pad(a["src"], N), pad(a["dst"], N)
    a["edge_attr_20"], a["edge_attr_256"] = pad(a["edge_attr_20"], 0), pad(a["edge_attr_256"], 0)
    for k in ("L0_gnn_attn_l", "L0_gnn_attn_r", "L0_ffn_wr", "L3_gnn_att_src", "L3_gnn_att_dst"):
        a[k] = a[k].reshape(-1)
    for k in ("L1_ffn_b1", "L2_gnn_bf1", "L2_gnn_bu1", "L2_gnn_bu2", "L2_gnn_gamma", "L2_gnn_beta", "L3_gnn_gamma", "L3_gnn_beta",
              "L3_ffn_sb1", "L3_ffn_sb2"):
        a[k] = columns(a[k])
    a["L1_ffn_router_w"] = np.ascontiguousarray(a["L1_ffn_router_w"].T)
    experts, _, hidden = a["L1_ffn_W1"].shape
    a["L1_ffn_W1"] = np.ascontiguousarray(a["L1_ffn_W1"].transpose(1, 0, 2)).reshape(D, -1)
    a["L1_ffn_W2"] = a["L1_ffn_W2"].reshape(-1, D)
    a["expert_rows"] = np.repeat(np.eye(experts, dtype=np.float32), hidden, axis=1)
    for k in ("W1", "W2", "Wo"):
        a[f"L2_ffn_{k}"] = a[f"L2_ffn_{k}"].reshape(-1, D)
    for i in "12":
        a[f"L2_ffn_bn{i}"] = np.stack([columns(a.pop(f"L2_ffn_{k}{i}")) for k in ("b", "g", "be", "m", "v")], axis=1)
    a["L3_ffn_eb1"], a["L3_ffn_eb2"] = np.ascontiguousarray(a["L3_ffn_eb1"].T), np.ascontiguousarray(a["L3_ffn_eb2"].T)
    a["L3_ffn_b3"] = np.concatenate([a.pop("L3_ffn_eb3"), a.pop("L3_ffn_sb3")[None]])
    a["consts"] = constants()
    return a


def kernel(**inputs):
    import concourse.bacc as _bacc
    from concourse.bass_utils import run_bass_kernel_spmd as _run

    nc = _bacc.Bacc("TRN2", target_bir_lowering=False, num_devices=1)
    arrays = {f"in_{k}": np.ascontiguousarray(v) for k, v in layout(inputs).items()}
    args = {k[3:]: nc.dram_tensor(k, v.shape, mybir.dt.from_np(v.dtype), kind="ExternalInput").ap() for k, v in arrays.items()}
    out = nc.dram_tensor("out_dram", (N, D), F32, kind="ExternalOutput").ap()
    gnn_ffn_kernel(nc, args, out)
    return _run(nc, [arrays], core_ids=[0]).results[0]["out_dram"]
```
